# Optimizing a Trainium2 kernel written in Bass

```python
import numpy as np
import jax
import jax.numpy as jnp

def _softmax(x, axis=-1):
    return jax.nn.softmax(x, axis=axis)

def _gelu(x):
    return jax.nn.gelu(x, approximate=True)

def _silu(x):
    return jax.nn.silu(x)

def _sigmoid(x):
    return jax.nn.sigmoid(x)

def _layernorm(x, axis=-1, eps=1e-05):
    m = jnp.mean(x, axis=axis, keepdims=True)
    v = jnp.var(x, axis=axis, keepdims=True)
    return (x - m) / jnp.sqrt(v + eps)

def _scatter_add(tgt, idx, src, axis=0):
    return tgt.at[idx].add(src)

def _segment_sum(src, seg, n):
    return jax.ops.segment_sum(src, seg, n)
kernel_name = 'mk_seq_postln_d2_jaxref_r8_92897b'

def setup_inputs(seed: int=0):
    np.random.seed(seed)
    _w = jnp.asarray

    def _L0_attn_setup():
        import jax, jax.numpy as jnp
        import numpy as np
        EPS = 0.0001

        def mp_normalize(x, axis):
            red = int(np.prod([x.shape[a] for a in axis])) if isinstance(axis, (list, tuple)) else x.shape[axis]
            w = jnp.sqrt(jnp.sum(jnp.square(x.astype(jnp.float32)), axis=axis, keepdims=True))
            w = EPS + w / np.sqrt(red)
            return x / w.astype(x.dtype)

        def mp_linear(x, w, gain):
            fan_in = w.shape[1]
            wn = mp_normalize(w.astype(jnp.float32), axis=(1,)) * (gain / np.sqrt(fan_in))
            return jnp.einsum('bse,oe->bso', x, wn.astype(x.dtype))

        def attention(query, gain, w_q, w_k, w_v, w_o, num_heads=16, attn_balance=0.5):
            B, S, E = query.shape
            hd = E // num_heads
            res = query
            q = mp_linear(query, w_q, gain).reshape(B, S, num_heads, hd).transpose(0, 2, 1, 3)
            k = mp_linear(query, w_k, gain).reshape(B, S, num_heads, hd).transpose(0, 2, 1, 3)
            v = mp_linear(query, w_v, gain).reshape(B, S, num_heads, hd).transpose(0, 2, 1, 3)
            q = mp_normalize(q, axis=(3,))
            k = mp_normalize(k, axis=(3,))
            scores = jnp.einsum('bnsh,bnsk->bnhk', q, k / np.sqrt(S))
            attn = jax.nn.softmax(scores, axis=3)
            o = jnp.einsum('bnhk,bnsk->bnsh', attn, v)
            o = o.transpose(0, 2, 1, 3).reshape(B, S, E)
            out = mp_linear(o, w_o, gain)
            t = attn_balance
            return (res * (1.0 - t) + out * t) / np.sqrt((1 - t) ** 2 + t ** 2)
        key = jax.random.key(seed)
        ks = jax.random.split(key, 5)
        B, S, E = (4, 512, 128)
        return {'query': jax.random.normal(ks[0], (B, S, E), dtype=jnp.float32), 'gain': jnp.float32(1.0), 'w_q': jax.random.normal(ks[1], (E, E), dtype=jnp.float32), 'w_k': jax.random.normal(ks[2], (E, E), dtype=jnp.float32), 'w_v': jax.random.normal(ks[3], (E, E), dtype=jnp.float32), 'w_o': jax.random.normal(ks[4], (E, E), dtype=jnp.float32)}
    _L0_attn_in = _L0_attn_setup()

    def _L0_ffn_setup():
        import jax, jax.numpy as jnp
        import numpy as np
        DIM = 128

        def _reference_tuple_inner(x, W_r, W_k, W_v, mu_r, mu_k):
            B, T, C = x.shape
            x_prev = jnp.concatenate([jnp.zeros((B, 1, C), x.dtype), x[:, :-1, :]], axis=1)
            xr = mu_r * x + (1.0 - mu_r) * x_prev
            xk = mu_k * x + (1.0 - mu_k) * x_prev
            r = jax.nn.sigmoid(jnp.einsum('btc,dc->btd', xr, W_r))
            k = jnp.einsum('btc,dc->btd', xk, W_k)
            k_act = jnp.square(jax.nn.relu(k))
            out = r * jnp.einsum('btc,dc->btd', k_act, W_v)
            new_state = x[:, -1, :]
            return (out, new_state)
        key = jax.random.key(seed)
        ks = jax.random.split(key, 6)
        B, T, C = (8, 256, DIM)
        x = jax.random.normal(ks[0], (B, T, C), dtype=jnp.float32)
        s = 1.0 / np.sqrt(C)
        W_r = jax.random.uniform(ks[1], (C, C), jnp.float32, -s, s)
        W_k = jax.random.uniform(ks[2], (C, C), jnp.float32, -s, s)
        W_v = jax.random.uniform(ks[3], (C, C), jnp.float32, -s, s)
        mu_r = jax.random.uniform(ks[4], (C,), jnp.float32)
        mu_k = jax.random.uniform(ks[5], (C,), jnp.float32)
        return {'x': x, 'W_r': W_r, 'W_k': W_k, 'W_v': W_v, 'mu_r': mu_r, 'mu_k': mu_k}
    _L0_ffn_in = _L0_ffn_setup()

    def _L1_attn_setup():
        import jax, jax.numpy as jnp
        import numpy as np
        B_SZ, L, D, N, H = (2, 256, 128, 16, 128)

        def celu(x):
            return jnp.where(x > 0, x, jnp.expm1(x))

        def _reference_tuple_inner(x, W1, b1, W2, b2, W3, b3, Wl1, bl1, Wl2, bl2, Wf1, bf1, Wf2, bf2, state_init, A):
            b = x.shape[0]
            lifted = jnp.tanh(jax.nn.relu(x @ Wl1 + bl1) @ Wl2 + bl2)
            combined = jnp.concatenate([x, lifted], axis=-1)
            x_trans = jax.nn.relu(combined @ Wf1 + bf1) @ Wf2 + bf2
            h_prev = jnp.broadcast_to(state_init, (b,) + state_init.shape[1:])
            Bm = x_trans @ W2 + b2
            Cm = x_trans @ W3 + b3
            delta = jax.nn.softplus(x_trans @ W1 + b1)
            dB = delta[..., :, None] * Bm[..., None, :]
            dA = jnp.exp(-celu(delta[..., :, None] * A[None, None]))
            h_new = dA * h_prev[:, None] + x_trans[..., None] * dB
            output = jnp.einsum('bln,bldn->bld', Cm, h_new)
            last_h_state = h_new[:, -1]
            return (output, last_h_state)
        key = jax.random.key(seed)
        ks = jax.random.split(key, 16)
        s = lambda fan_in: 1.0 / np.sqrt(fan_in)
        inp = {'x': jax.random.normal(ks[0], (B_SZ, L, D), jnp.float32), 'W1': jax.random.normal(ks[1], (D, D), jnp.float32) * s(D), 'b1': jnp.zeros((D,), jnp.float32), 'W2': jax.random.normal(ks[2], (D, N), jnp.float32) * s(D), 'b2': jnp.zeros((N,), jnp.float32), 'W3': jax.random.normal(ks[3], (D, N), jnp.float32) * s(D), 'b3': jnp.zeros((N,), jnp.float32), 'Wl1': jax.random.normal(ks[4], (D, H), jnp.float32) * s(D), 'bl1': jnp.zeros((H,), jnp.float32), 'Wl2': jax.random.normal(ks[5], (H, D), jnp.float32) * s(H), 'bl2': jnp.zeros((D,), jnp.float32), 'Wf1': jax.random.normal(ks[6], (2 * D, H), jnp.float32) * s(2 * D), 'bf1': jnp.zeros((H,), jnp.float32), 'Wf2': jax.random.normal(ks[7], (H, D), jnp.float32) * s(H), 'bf2': jnp.zeros((D,), jnp.float32), 'state_init': jnp.zeros((1, D, N), jnp.float32), 'A': jax.random.normal(ks[8], (D, N), jnp.float32) * np.sqrt(2.0 / N)}
        return inp
    _L1_attn_in = _L1_attn_setup()

    def _L1_ffn_setup():
        import jax, jax.numpy as jnp
        import numpy as np
        D_IN, D_HID = (128, 512)

        def _ternary(key, shape):
            return jax.random.randint(key, shape, -1, 2).astype(jnp.float32)

        def _tlin(x, w, s):
            return jnp.einsum('bsi,oi->bso', x, w) * s
        key = jax.random.key(seed)
        ks = jax.random.split(key, 12)
        inv = lambda fan: 1.0 / np.sqrt(fan).astype(np.float32)
        return {'x': jax.random.normal(ks[0], (4, 256, D_IN), dtype=jnp.float32), 'w1_w': _ternary(ks[1], (D_HID, D_IN)), 'w1_s': jax.random.uniform(ks[2], (D_HID,), dtype=jnp.float32) * inv(D_IN), 'w2_w': _ternary(ks[3], (D_HID, D_IN)), 'w2_s': jax.random.uniform(ks[4], (D_HID,), dtype=jnp.float32) * inv(D_IN), 'h1_w': _ternary(ks[5], (D_HID, D_HID)), 'h1_s': jax.random.uniform(ks[6], (D_HID,), dtype=jnp.float32) * inv(D_HID), 'h2_w': _ternary(ks[7], (D_HID, D_HID)), 'h2_s': jax.random.uniform(ks[8], (D_HID,), dtype=jnp.float32) * inv(D_HID), 'w3_w': _ternary(ks[9], (D_IN, D_HID)), 'w3_s': jax.random.uniform(ks[10], (D_IN,), dtype=jnp.float32) * inv(D_HID)}
    _L1_ffn_in = _L1_ffn_setup()
    _d = {'L0_attn_query': _L0_attn_in['query'], 'L0_attn_gain': _L0_attn_in['gain'], 'L0_attn_w_q': _L0_attn_in['w_q'], 'L0_attn_w_k': _L0_attn_in['w_k'], 'L0_attn_w_v': _L0_attn_in['w_v'], 'L0_attn_w_o': _L0_attn_in['w_o'], 'L0_ffn_W_r': _L0_ffn_in['W_r'], 'L0_ffn_W_k': _L0_ffn_in['W_k'], 'L0_ffn_W_v': _L0_ffn_in['W_v'], 'L0_ffn_mu_r': _L0_ffn_in['mu_r'], 'L0_ffn_mu_k': _L0_ffn_in['mu_k'], 'L1_attn_W1': _L1_attn_in['W1'], 'L1_attn_b1': _L1_attn_in['b1'], 'L1_attn_W2': _L1_attn_in['W2'], 'L1_attn_b2': _L1_attn_in['b2'], 'L1_attn_W3': _L1_attn_in['W3'], 'L1_attn_b3': _L1_attn_in['b3'], 'L1_attn_Wl1': _L1_attn_in['Wl1'], 'L1_attn_bl1': _L1_attn_in['bl1'], 'L1_attn_Wl2': _L1_attn_in['Wl2'], 'L1_attn_bl2': _L1_attn_in['bl2'], 'L1_attn_Wf1': _L1_attn_in['Wf1'], 'L1_attn_bf1': _L1_attn_in['bf1'], 'L1_attn_Wf2': _L1_attn_in['Wf2'], 'L1_attn_bf2': _L1_attn_in['bf2'], 'L1_attn_state_init': _L1_attn_in['state_init'], 'L1_attn_A': _L1_attn_in['A'], 'L1_ffn_w1_w': _L1_ffn_in['w1_w'], 'L1_ffn_w1_s': _L1_ffn_in['w1_s'], 'L1_ffn_w2_w': _L1_ffn_in['w2_w'], 'L1_ffn_w2_s': _L1_ffn_in['w2_s'], 'L1_ffn_h1_w': _L1_ffn_in['h1_w'], 'L1_ffn_h1_s': _L1_ffn_in['h1_s'], 'L1_ffn_h2_w': _L1_ffn_in['h2_w'], 'L1_ffn_h2_s': _L1_ffn_in['h2_s'], 'L1_ffn_w3_w': _L1_ffn_in['w3_w'], 'L1_ffn_w3_s': _L1_ffn_in['w3_s']}
    _x0 = _d['L0_attn_query']
    _d['L0_attn_query'] = jax.random.normal(jax.random.fold_in(jax.random.key(seed), 1), (1, 2048, 128), dtype=_x0.dtype)
    del _x0
    return _d

def reference(L0_attn_query, L0_attn_gain, L0_attn_w_q, L0_attn_w_k, L0_attn_w_v, L0_attn_w_o, L0_ffn_W_r, L0_ffn_W_k, L0_ffn_W_v, L0_ffn_mu_r, L0_ffn_mu_k, L1_attn_W1, L1_attn_b1, L1_attn_W2, L1_attn_b2, L1_attn_W3, L1_attn_b3, L1_attn_Wl1, L1_attn_bl1, L1_attn_Wl2, L1_attn_bl2, L1_attn_Wf1, L1_attn_bf1, L1_attn_Wf2, L1_attn_bf2, L1_attn_state_init, L1_attn_A, L1_ffn_w1_w, L1_ffn_w1_s, L1_ffn_w2_w, L1_ffn_w2_s, L1_ffn_h1_w, L1_ffn_h1_s, L1_ffn_h2_w, L1_ffn_h2_s, L1_ffn_w3_w, L1_ffn_w3_s):

    def _L0_attn_ref(query, gain, w_q, w_k, w_v, w_o):
        import jax, jax.numpy as jnp
        import numpy as np
        EPS = 0.0001

        def mp_normalize(x, axis):
            red = int(np.prod([x.shape[a] for a in axis])) if isinstance(axis, (list, tuple)) else x.shape[axis]
            w = jnp.sqrt(jnp.sum(jnp.square(x.astype(jnp.float32)), axis=axis, keepdims=True))
            w = EPS + w / np.sqrt(red)
            return x / w.astype(x.dtype)

        def mp_linear(x, w, gain):
            fan_in = w.shape[1]
            wn = mp_normalize(w.astype(jnp.float32), axis=(1,)) * (gain / np.sqrt(fan_in))
            return jnp.einsum('bse,oe->bso', x, wn.astype(x.dtype))

        def attention(query, gain, w_q, w_k, w_v, w_o, num_heads=16, attn_balance=0.5):
            B, S, E = query.shape
            hd = E // num_heads
            res = query
            q = mp_linear(query, w_q, gain).reshape(B, S, num_heads, hd).transpose(0, 2, 1, 3)
            k = mp_linear(query, w_k, gain).reshape(B, S, num_heads, hd).transpose(0, 2, 1, 3)
            v = mp_linear(query, w_v, gain).reshape(B, S, num_heads, hd).transpose(0, 2, 1, 3)
            q = mp_normalize(q, axis=(3,))
            k = mp_normalize(k, axis=(3,))
            scores = jnp.einsum('bnsh,bnsk->bnhk', q, k / np.sqrt(S))
            attn = jax.nn.softmax(scores, axis=3)
            o = jnp.einsum('bnhk,bnsk->bnsh', attn, v)
            o = o.transpose(0, 2, 1, 3).reshape(B, S, E)
            out = mp_linear(o, w_o, gain)
            t = attn_balance
            return (res * (1.0 - t) + out * t) / np.sqrt((1 - t) ** 2 + t ** 2)
        return attention(query, gain, w_q, w_k, w_v, w_o)

    def _L0_ffn_ref(x, W_r, W_k, W_v, mu_r, mu_k):
        import jax, jax.numpy as jnp
        import numpy as np
        DIM = 128

        def _reference_tuple_inner(x, W_r, W_k, W_v, mu_r, mu_k):
            B, T, C = x.shape
            x_prev = jnp.concatenate([jnp.zeros((B, 1, C), x.dtype), x[:, :-1, :]], axis=1)
            xr = mu_r * x + (1.0 - mu_r) * x_prev
            xk = mu_k * x + (1.0 - mu_k) * x_prev
            r = jax.nn.sigmoid(jnp.einsum('btc,dc->btd', xr, W_r))
            k = jnp.einsum('btc,dc->btd', xk, W_k)
            k_act = jnp.square(jax.nn.relu(k))
            out = r * jnp.einsum('btc,dc->btd', k_act, W_v)
            new_state = x[:, -1, :]
            return (out, new_state)
        return _reference_tuple_inner(x, W_r, W_k, W_v, mu_r, mu_k)[0]

    def _L1_attn_ref(x, W1, b1, W2, b2, W3, b3, Wl1, bl1, Wl2, bl2, Wf1, bf1, Wf2, bf2, state_init, A):
        import jax, jax.numpy as jnp
        import numpy as np
        B_SZ, L, D, N, H = (2, 256, 128, 16, 128)

        def celu(x):
            return jnp.where(x > 0, x, jnp.expm1(x))

        def _reference_tuple_inner(x, W1, b1, W2, b2, W3, b3, Wl1, bl1, Wl2, bl2, Wf1, bf1, Wf2, bf2, state_init, A):
            b = x.shape[0]
            lifted = jnp.tanh(jax.nn.relu(x @ Wl1 + bl1) @ Wl2 + bl2)
            combined = jnp.concatenate([x, lifted], axis=-1)
            x_trans = jax.nn.relu(combined @ Wf1 + bf1) @ Wf2 + bf2
            h_prev = jnp.broadcast_to(state_init, (b,) + state_init.shape[1:])
            Bm = x_trans @ W2 + b2
            Cm = x_trans @ W3 + b3
            delta = jax.nn.softplus(x_trans @ W1 + b1)
            dB = delta[..., :, None] * Bm[..., None, :]
            dA = jnp.exp(-celu(delta[..., :, None] * A[None, None]))
            h_new = dA * h_prev[:, None] + x_trans[..., None] * dB
            output = jnp.einsum('bln,bldn->bld', Cm, h_new)
            last_h_state = h_new[:, -1]
            return (output, last_h_state)
        return _reference_tuple_inner(x, W1, b1, W2, b2, W3, b3, Wl1, bl1, Wl2, bl2, Wf1, bf1, Wf2, bf2, state_init, A)[0]

    def _L1_ffn_ref(x, w1_w, w1_s, w2_w, w2_s, h1_w, h1_s, h2_w, h2_s, w3_w, w3_s):
        import jax, jax.numpy as jnp
        import numpy as np
        D_IN, D_HID = (128, 512)

        def _ternary(key, shape):
            return jax.random.randint(key, shape, -1, 2).astype(jnp.float32)

        def _tlin(x, w, s):
            return jnp.einsum('bsi,oi->bso', x, w) * s
        h = jax.nn.silu(_tlin(x, w1_w, w1_s)) * _tlin(x, w2_w, w2_s)
        h = jax.nn.gelu(_tlin(h, h1_w, h1_s), approximate=False)
        h = jax.nn.gelu(_tlin(h, h2_w, h2_s), approximate=False)
        return _tlin(h, w3_w, w3_s)
    x = L0_attn_query
    x = _layernorm(x + _L0_attn_ref(x, L0_attn_gain, L0_attn_w_q, L0_attn_w_k, L0_attn_w_v, L0_attn_w_o), axis=-1)
    x = _layernorm(x + _L0_ffn_ref(x, L0_ffn_W_r, L0_ffn_W_k, L0_ffn_W_v, L0_ffn_mu_r, L0_ffn_mu_k), axis=-1)
    x = _layernorm(x + _L1_attn_ref(x, L1_attn_W1, L1_attn_b1, L1_attn_W2, L1_attn_b2, L1_attn_W3, L1_attn_b3, L1_attn_Wl1, L1_attn_bl1, L1_attn_Wl2, L1_attn_bl2, L1_attn_Wf1, L1_attn_bf1, L1_attn_Wf2, L1_attn_bf2, L1_attn_state_init, L1_attn_A), axis=-1)
    x = _layernorm(x + _L1_ffn_ref(x, L1_ffn_w1_w, L1_ffn_w1_s, L1_ffn_w2_w, L1_ffn_w2_s, L1_ffn_h1_w, L1_ffn_h1_s, L1_ffn_h2_w, L1_ffn_h2_s, L1_ffn_w3_w, L1_ffn_w3_s), axis=-1)
    return x

_drawn_inputs = setup_inputs


def setup_inputs(seed=0):
    import zlib

    import numpy as np

    out = dict(_drawn_inputs(seed))
    spreads = {'L1_attn_b1': (0.0, 0.1),
     'L1_attn_b2': (0.0, 0.1),
     'L1_attn_b3': (0.0, 0.1),
     'L1_attn_bl1': (0.0, 0.1),
     'L1_attn_bl2': (0.0, 0.1),
     'L1_attn_bf1': (0.0, 0.1),
     'L1_attn_bf2': (0.0, 0.1),
     'L1_attn_state_init': (0.0, 0.1)}
    factors = {'L0_ffn_mu_r': 5.19,
     'L1_ffn_w1_w': 8.0,
     'L1_ffn_w1_s': 8.0,
     'L1_ffn_w2_w': 8.0,
     'L1_ffn_w2_s': 8.0,
     'L1_ffn_h1_w': 8.0,
     'L1_ffn_h1_s': 8.0,
     'L1_ffn_h2_w': 8.0,
     'L1_ffn_h2_s': 8.0,
     'L1_ffn_w3_w': 8.0,
     'L1_ffn_w3_s': 8.0}
    for name, (base, spread) in spreads.items():
        noise = np.random.default_rng([zlib.crc32(name.encode()), seed]).standard_normal(out[name].shape)
        drawn = base * np.exp(spread * noise) if base else spread * noise
        out[name] = jnp.asarray(drawn.astype(out[name].dtype))
    for name, factor in factors.items():
        out[name] = (out[name] * factor).astype(out[name].dtype)
    return out
```

```python
from contextlib import ExitStack

import numpy as np
import concourse.bass as bass
from concourse import mybir

F32 = mybir.dt.float32
F32R = mybir.dt.float32r
ALU = mybir.AluOpType
ACT = mybir.ActivationFunctionType
AX = mybir.AxisListType

P = 128
CH = 512
HEADS = 16
HD = P // HEADS
NS = 16
NG = 4
GN = NS // NG
EPS_MP = 1e-4
EPS_LN = 1e-5
LN_EXP = "natural_log_exp_and_others"

MU_R, MU_K, BL1, BL2, BF1, BF2, B1, S3, S1, S2, SH1, SH2, B2, B3 = 0, 1, 2, 3, 4, 5, 6, 7, 8, 12, 16, 20, 24, 25
NVEC = 32


def build(nc, t, out):
    x_d = t["L0_attn_query"].rearrange("a (n p) c -> (a p) n c", p=P)
    out_d = out.rearrange("a (n p) c -> (a p) n c", p=P)
    T = x_d.shape[1] * P
    NCH = T // CH
    NT = T // P
    TPC = CH // P
    HID = t["L1_ffn_w1_w"].shape[0]
    KH = HID // P
    res_gain = 1.0 + 0.5 / np.sqrt(0.5)
    out_gain = 0.5 / np.sqrt(0.5)

    ctx = ExitStack()
    with ctx:
        def sb(name, shape, dt=F32):
            return ctx.enter_context(nc.sbuf_tensor(name, shape, dt))

        def sem(name):
            return ctx.enter_context(nc.semaphore(name))

        ps = ctx.enter_context(nc.psum_tensor("ps", [P, 8, CH], F32))

        ident = sb("ident", [P, P])
        ones = sb("ones", [P, P])
        ones_n = sb("ones_n", [32, P])
        res_ident = sb("res_ident", [P, P])
        mask = sb("mask", [P, P])
        vrow = sb("vrow", [NVEC, P])
        vec = sb("vec", [P, NVEC])
        mu1 = sb("mu1", [P, 2])
        gain = sb("gain", [P, 1])
        wa = sb("wa", [P, 4, P])
        wss = sb("wss", [P, 4])
        wnorm = sb("wnorm", [P, 4])

        wqk = sb("wqk", [P, 2, 2 * P], F32R)
        woT = sb("woT", [P, P])
        sm = sb("sm", [P, P])
        smax = sb("smax", [P, 1])
        ssum = sb("ssum", [P, 1])
        srec = sb("srec", [P, 1])
        prob = sb("prob", [P, P])
        u_sb = sb("u_sb", [P, P])
        mix = sb("mix", [P, P])
        mrow = sb("mrow", [P, 1])
        mixr = sb("mixr", [P, 2, P], F32R)
        w0raw = sb("w0raw", [P, 3, P])
        w0f = sb("w0f", [P, 5, P])
        w0 = sb("w0", [P, 5, 2, P], F32R)
        w1 = sb("w1", [P, 8, 2, P], F32R)
        h0raw = sb("h0raw", [P, 96])
        h0T = sb("h0T", [96, P])
        h0hi = sb("h0hi", [96, P], F32R)
        eps_ln = sb("eps_ln", [P, 1])
        h0sel = sb("h0sel", [96, NS, P], F32R)
        amat = sb("amat", [P, NS])
        amin = sb("amin", [P, NS])
        amax = sb("amax", [P, NS])
        nfill = 3 + 2 * KH
        wf = sb("wf", [P, nfill, 2, HID], F32R)
        ss = sb("ss", [P, NCH * 2, 2, 2, HEADS])
        qkrec = sb("qkrec", [P, NCH * 2, 2, HEADS])
        stats = sb("stats", [P, 2, TPC, 6])
        mdif = sb("mdif", [P, 2, TPC])
        mv = sb("mv", [P, 2, TPC, 2])
        rstd = sb("rstd", [P, 2, TPC])
        xr = sb("xr", [P, 2, T], F32R)
        x1r = sb("x1r", [P, 2, T + 2], F32R)
        tr = sb("tr", [P, 2, T], F32R)
        lr = sb("lr", [P, 2, T], F32R)
        bx1, bs1, bs2, bs3, bx2, bxt, bdl = [sb(n, [P, T]) for n in ("bx1", "bs1", "bs2", "bs3", "bx2", "bxt", "bdl")]

        x_tok = bx2[:, :].rearrange("p (n c) -> p n c", c=P)
        q_sb = bx1[:, :].rearrange("p (n c) -> p n c", c=P)
        k_sb = bxt[:, :].rearrange("p (n c) -> p n c", c=P)
        sq = bdl[:, :].rearrange("p (n c) -> p n c", c=CH)
        w1raw = bdl[:, T // 2:].rearrange("p (w c) -> p w c", c=P)
        hraw = [b[:, :].rearrange("p (r c) -> p r c", c=HID) for b in (bs1, bs2)]
        w12raw = bs3[:, :].rearrange("p (w r c) -> p w r c", w=4, c=P)
        slot = [xr[:, :, :].rearrange("p s (k n) -> p s k n", k=KH),
                x1r[:, :, 2:].rearrange("p s (k n) -> p s k n", k=KH),
                tr[:, :, :].rearrange("p s (k n) -> p s k n", k=KH)]
        vbuf = [b[:, :].rearrange("p (k n) -> p k n", k=GN) for b in (bs1, bs2, bs3, bx1)]

        ld_x = [sem(f"ld_x{c}") for c in range(NCH)]
        ld_wa, ld_vec, ld_w0, ld_w1, ld_f, ld_h1, ld_h2, stored = [
            sem(n) for n in ("ld_wa", "ld_vec", "ld_w0", "ld_w1", "ld_f", "ld_h1", "ld_h2", "stored")]
        pads, ident_ok, mask_ok, consts = [sem(n) for n in ("pads", "ident_ok", "mask_ok", "consts")]
        wnorm_ok, ws_ok, wT_mm, wqk_hi, wqk_lo, woT_ok = [
            sem(n) for n in ("wnorm_ok", "ws_ok", "wT_mm", "wqk_hi",
                             "wqk_lo", "woT_ok")]
        vecT_mm, vec_ok, mu1_ok, w0T_mm, w0f_ok, w0_hi, w0_lo, w1_hi, w1_lo = [
            sem(n) for n in ("vecT_mm", "vec_ok", "mu1_ok", "w0T_mm", "w0f_ok", "w0_hi", "w0_lo", "w1_hi", "w1_lo")]
        h0T_mm, h0f_ok, h0sel_ok, a_ok = [
            sem(n) for n in ("h0T_mm", "h0f_ok", "h0sel_ok", "a_ok")]
        fill_mm, fill_hi, fill_lo = [sem(n) for n in ("fill_mm", "fill_hi", "fill_lo")]
        xT_mm, x_hi, x_lo, qk_mm, sq_ok, k_ok, q_ok, ss_ok, nrm_ok, nrm_step, qn_ok = [
            sem(n) for n in ("xT_mm", "x_hi", "x_lo", "qk_mm", "sq_ok", "k_ok", "q_ok", "ss_ok", "nrm_ok", "nrm_step",
                             "qn_ok")]
        sc_mm, sm_ok, smax_ok, exp_ok, srec_ok, prob_ok, u_mm, u_ok, m_mm, mix_ok = [
            sem(n) for n in ("sc_mm", "sm_ok", "smax_ok", "exp_ok", "srec_ok", "prob_ok", "u_mm", "u_ok", "m_mm",
                             "mix_ok")]
        y1_mm, y1_sq, y1_var, y1_ln, y1_rs, x1_ok, x1_hi, x1_lo = [
            sem(n) for n in ("y1_mm", "y1_sq", "y1_var", "y1_ln", "y1_rs", "x1_ok", "x1_hi", "x1_lo")]
        rk_mm, th_ok, relu_ok, k2_ok, k2_hi, k2_lo, v_mm, p_ok, y2_ok, y2_mean, y2_c, y2_sq, y2_var, y2_ln, y2_rs = [
            sem(n) for n in ("rk_mm", "th_ok", "relu_ok", "k2_ok", "k2_hi", "k2_lo", "v_mm", "p_ok", "y2_ok",
                             "y2_mean", "y2_c", "y2_sq", "y2_var", "y2_ln", "y2_rs")]
        x2_ok, x2_hi, x2_lo, l1_mm, l1_ok, l1_hi, l1_lo, l2_mm, l2_ok, l2_hi, l2_lo = [
            sem(n) for n in ("x2_ok", "x2_hi", "x2_lo", "l1_mm", "l1_ok", "l1_hi", "l1_lo", "l2_mm", "l2_ok",
                             "l2_hi", "l2_lo")]
        f1_mm, f1_ok, f1_hi, f1_lo, xt_mm, xt_ok, xt_hi, xt_lo, d_mm, d_abs, d_exp, d_ln, d_max, d_ok = [
            sem(n) for n in ("f1_mm", "f1_ok", "f1_hi", "f1_lo", "xt_mm", "xt_ok", "xt_hi", "xt_lo", "d_mm", "d_abs",
                             "d_exp", "d_ln", "d_max", "d_ok")]
        c_mm, b_mm, c_hi, c_lo, c_f, bc_ok, bc_mm, g_ok, o2_ok, o2x_ok = [
            sem(n) for n in ("c_mm", "b_mm", "c_hi", "c_lo", "c_f", "bc_ok", "bc_mm", "g_ok", "o2_ok", "o2x_ok")]
        e_t, e_v, e_da, e_ch, e_p, e_sum = [sem(n) for n in ("e_t", "e_v", "e_da", "e_ch", "e_p", "e_sum")]
        y3_ok, y3_mean, y3_c, y3_sq, y3_var, y3_ln, y3_rs, x3_ok, x3_hi, x3_lo = [
            sem(n) for n in ("y3_ok", "y3_mean", "y3_c", "y3_sq", "y3_var", "y3_ln", "y3_rs", "x3_ok", "x3_hi",
                             "x3_lo")]
        m_mm_, m_act, m_full, m_hi, m_lo = [sem(n) for n in ("mlp_mm", "mlp_act", "mlp_full", "mlp_hi", "mlp_lo")]
        o_mm, o_y, o_T, o_st, o_stat, o_mv, o_sd, o_rs, o_ok = [
            sem(n) for n in ("o_mm", "o_y", "o_T", "o_st", "o_stat", "o_mv", "o_sd", "o_rs", "o_ok")]

        def cs(c):
            return slice(c * CH, (c + 1) * CH)

        def full(b):
            return b.bitcast(F32)

        def mm3(dst, w, xs, start=True, stop=True):
            nc.tensor.matmul(dst, w[0], xs[0], start=start, stop=False)
            nc.tensor.matmul(dst, w[0], xs[1], start=False, stop=False)
            return nc.tensor.matmul(dst, w[1], xs[0], start=False, stop=stop)

        def pair(w, *i):
            return w[(slice(None), *i, 0)], w[(slice(None), *i, 1)]

        def parts(b, c, shift=0):
            s = slice(c * CH + shift, (c + 1) * CH + shift)
            return b[:, 0, s], b[:, 1, s]

        block = ctx.enter_context(nc.Block())

        @block.sync
        def _(sp):
            n_wa = [("w_q", 0), ("w_k", 1), ("w_o", 2), ("w_v", 3)]
            for name, i in n_wa:
                sp.dma_start(wa[:, i, :], t["L0_attn_" + name]).then_inc(ld_wa, 16)
            sp.dma_start(gain[:, :], t["L0_attn_gain"].partition_broadcast(P)).then_inc(ld_wa, 16)
            for c in range(NCH):
                n = slice(c * TPC, (c + 1) * TPC)
                sp.dma_start(x_tok[:, n, :], x_d[:, n, :]).then_inc(ld_x[c], 16)
            for i, name in enumerate(("w1_w", "w2_w")):
                sp.dma_start(w12raw[:, i], t["L1_ffn_" + name].rearrange("(r p) c -> p r c", p=P)).then_inc(ld_f, 16)
            sp.dma_start(w12raw[:, 2], t["L1_ffn_w3_w"].rearrange("p (r c) -> p r c", c=P)).then_inc(ld_f, 16)
            sp.dma_start(hraw[0], t["L1_ffn_h1_w"].rearrange("(r p) c -> p r c", p=P)).then_inc(ld_h1, 16)
            sp.dma_start(hraw[1], t["L1_ffn_h2_w"].rearrange("(r p) c -> p r c", p=P)).then_inc(ld_h2, 16)
            with sp.Fori(0, NCH // 2) as i:
                for k in range(2):
                    sp.wait_ge(o_ok, (2 * i + k + 1) * TPC + 1)
                    sp.dma_start(out_d[:, bass.ds((2 * i + k) * TPC, TPC), :],
                                 bdl[:, bass.ts(2 * i + k, CH)].rearrange("p (n c) -> p n c", c=P)).then_inc(stored, 16)
            sp.wait_ge(stored, 16 * NCH)

        @block.gpsimd
        def _(pool):
            g = nc.gpsimd
            g.memset(vrow[:, :], 0.0).then_inc(pads, 1)
            g.memset(w1raw[:, 6:8, :], 0.0).then_inc(pads, 1)
            g.memset(h0raw[:, :], 0.0).then_inc(pads, 1)
            g.memset(ident[:, :], 0.0).then_inc(pads, 1)
            g.memset(mask[:, :], 0.0).then_inc(pads, 1)
            pool.wait_ge(pads, 5)
            g.affine_select(out=ident[:, :], in_=ident[:, :], compare_op=ALU.not_equal, fill=1.0, base=0,
                            pattern=[[-1, P]], channel_multiplier=1).then_inc(ident_ok, 1)
            rows = [("L0_ffn_mu_r", MU_R, 1), ("L0_ffn_mu_k", MU_K, 1), ("L1_attn_bl1", BL1, 1),
                    ("L1_attn_bl2", BL2, 1), ("L1_attn_bf1", BF1, 1), ("L1_attn_bf2", BF2, 1),
                    ("L1_attn_b1", B1, 1), ("L1_ffn_w3_s", S3, 1), ("L1_ffn_w1_s", S1, KH),
                    ("L1_ffn_w2_s", S2, KH), ("L1_ffn_h1_s", SH1, KH), ("L1_ffn_h2_s", SH2, KH)]
            for name, r, k in rows:
                g.dma_start(vrow[r:r + k, :], t[name].rearrange("(r c) -> r c", r=k)).then_inc(ld_vec, 16)
            g.dma_start(vrow[B2:B2 + 1, 0:NS], t["L1_attn_b2"].rearrange("(r c) -> r c", r=1)).then_inc(ld_vec, 16)
            for j in range(3):
                g.dma_start(vrow[B3:B3 + 1, 32 * j:32 * j + NS],
                            t["L1_attn_b3"].rearrange("(r c) -> r c", r=1)).then_inc(ld_vec, 16)
            for i, name in enumerate(("W_r", "W_k", "W_v")):
                g.dma_start(w0raw[:, i, :], t["L0_ffn_" + name]).then_inc(ld_w0, 16)
            m3 = mask[:, :].rearrange("p (h k) -> p h k", k=HD)
            g.affine_select(out=m3, in_=m3, compare_op=ALU.is_ge, fill=-1e30, base=0,
                            pattern=[[-HD, HEADS], [0, HD]], channel_multiplier=1).then_inc(mask_ok, 1)
            pool.wait_ge(mask_ok, 1)
            g.affine_select(out=m3, in_=m3, compare_op=ALU.is_ge, fill=-1e30, base=HD - 1,
                            pattern=[[HD, HEADS], [0, HD]], channel_multiplier=-1).then_inc(mask_ok, 1)
            for i, name in enumerate(("Wl1", "Wl2")):
                g.dma_start(w1raw[:, i, :], t["L1_attn_" + name]).then_inc(ld_w1, 16)
            g.dma_start(w1raw[:, 2:4, :], t["L1_attn_Wf1"].rearrange("(h p) c -> p h c", p=P)).then_inc(ld_w1, 16)
            g.dma_start(w1raw[:, 4, :], t["L1_attn_Wf2"]).then_inc(ld_w1, 16)
            g.dma_start(w1raw[:, 5, :], t["L1_attn_W1"]).then_inc(ld_w1, 16)
            for j in range(3):
                g.dma_start(w1raw[:, 6, 32 * j:32 * j + NS], t["L1_attn_W3"]).then_inc(ld_w1, 16)
                g.dma_start(h0raw[:, 32 * j:32 * j + NS],
                            t["L1_attn_state_init"].rearrange("a d n -> (a d) n")).then_inc(ld_w1, 16)
            g.dma_start(w1raw[:, 7, 0:NS], t["L1_attn_W2"]).then_inc(ld_w1, 16)
            g.dma_start(amat[:, :], t["L1_attn_A"]).then_inc(ld_w1, 16)
            pool.wait_ge(mask_ok, 2)
            pool.wait_ge(h0f_ok, 4)
            for j in range(3):
                r = slice(32 * j, 32 * j + 32)
                if j:
                    pool.wait_ge(h0sel_ok, j)
                src = h0T[r, :].rearrange("p (n c) -> p n c", n=1).broadcast_to([32, NS, P])
                g.affine_select(out=h0sel[r, :, :], in_=src, compare_op=ALU.is_equal, fill=0.0, base=0,
                                pattern=[[-1, NS], [0, P]], channel_multiplier=1).then_inc(h0sel_ok, 1)
            def lows(hi_sem, lo_sem, full_buf, r):
                for c in range(NCH):
                    pool.wait_ge(hi_sem, c + 1)
                    hi, lo = r(c)
                    g.tensor_tensor(lo, full_buf[:, cs(c)], full(hi), ALU.subtract).then_inc(lo_sem, 1)

            pool.wait_ge(h0sel_ok, 3)
            lows(x1_hi, x1_lo, bx1, lambda c: parts(x1r, c, 2))
            lows(k2_hi, k2_lo, bs3, lambda c: parts(tr, c))
            lows(x2_hi, x2_lo, bx2, lambda c: parts(xr, c))
            lows(l1_hi, l1_lo, bs1, lambda c: parts(tr, c))
            lows(l2_hi, l2_lo, bs3, lambda c: parts(lr, c))
            lows(f1_hi, f1_lo, bs1, lambda c: parts(tr, c))
            lows(xt_hi, xt_lo, bxt, lambda c: parts(x1r, c, 2))
            for c in range(NCH):
                pool.wait_ge(d_ln, c + 1)
                pool.wait_ge(d_max, c + 1)
                g.tensor_tensor(bdl[:, cs(c)], bs1[:, cs(c)], bs2[:, cs(c)], ALU.add).then_inc(d_ok, 1)
            for c in range(NCH):
                pool.wait_ge(d_ok, c + 1)
                pool.wait_ge(xt_lo, c + 1)
                g.tensor_tensor(bxt[:, cs(c)], bxt[:, cs(c)], bdl[:, cs(c)], ALU.mult).then_inc(g_ok, 1)
            for c in range(NCH):
                pool.wait_ge(o2_ok, c + 1)
                g.tensor_tensor(bxt[:, cs(c)], bxt[:, cs(c)], bx2[:, cs(c)], ALU.add).then_inc(o2x_ok, 1)
            lows(x3_hi, x3_lo, bx2, lambda c: parts(lr, c))
            with pool.Fori(0, NCH // 2) as i:
                for stage in range(3):
                    for k in range(2):
                        for o in range(KH):
                            n = (stage * 2 + k) * KH + o
                            pool.wait_ge(m_hi, 6 * KH * i + n + 1)
                            sl = slot[(2 * stage + k) % 3]
                            g.tensor_tensor(sl[:, 1, o, :], vbuf[k][:, o, :], full(sl[:, 0, o, :]),
                                            ALU.subtract).then_inc(m_lo, 1)

        @block.scalar
        def _(act):
            a = nc.scalar
            act.preload_act_table(ACT.Sqrt)
            act.wait_ge(ld_wa, 16 * 5)
            for i in range(4):
                a.activation(bxt[:, i * P:(i + 1) * P], wa[:, i, :], ACT.Square, accum_out=wss[:, i:i + 1]).then_inc(wnorm_ok, 1)
            act.wait_ge(wnorm_ok, 4)
            a.activation(wnorm[:, :], wss[:, :], ACT.Sqrt).then_inc(wnorm_ok, 1)
            act.wait_ge(wT_mm, 1)
            a.activation(wqk[:, 0, :], ps[:, 4, 0:2 * P], ACT.Copy).then_inc(wqk_hi, 1)
            a.activation(woT[:, :], ps[:, 4, 2 * P:3 * P], ACT.Copy).then_inc(woT_ok, 1)
            for c in range(NCH):
                act.wait_ge(xT_mm, c + 1)
                a.activation(xr[:, 0, cs(c)], ps[:, c, :], ACT.Copy).then_inc(x_hi, 1)
            for p in range(2 * NCH):
                act.wait_ge(qk_mm, p + 1)
                if p >= 2:
                    act.wait_ge(ss_ok, p - 1)
                a.activation(sq[:, p % 2, :], ps[:, p % 4, :], ACT.Square).then_inc(sq_ok, 1)
                qk = ps[:, p % 4, :].rearrange("p (t w c) -> p t w c", t=2, w=2)
                a.activation(k_sb[:, 2 * p:2 * p + 2, :], qk[:, :, 1, :], ACT.Copy).then_inc(k_ok, 1)
                if p % NCH == NCH - 1:
                    h = slice(p - NCH + 1, p + 1)
                    act.wait_ge(ss_ok, p + 1)
                    a.activation(ss[:, h], ss[:, h], ACT.Sqrt, scale=1.0 / HD).then_inc(nrm_ok, 1)
            act.preload_act_table_set(LN_EXP)

            def fills(lo, hi):
                for f in range(lo, hi):
                    act.wait_ge(fill_mm, f + 1)
                    a.activation(wf[:, f, 0, :], ps[:, f % 4, :], ACT.Copy).then_inc(fill_hi, 1)

            fills(0, 4)
            act.wait_ge(smax_ok, 1)
            a.activation(prob[:, :], sm[:, :], ACT.Exp, bias=smax[:, :], accum_out=ssum[:, :]).then_inc(exp_ok, 1)
            act.wait_ge(u_mm, 1)
            a.activation(u_sb[:, :], ps[:, 5, 0:P], ACT.Copy).then_inc(u_ok, 1)
            fills(4, nfill)

            def rstds(var_sem, ln_sem, rs_sem, buf, bank):
                for c in range(NCH):
                    act.wait_ge(var_sem, c + 1)
                    a.activation(buf[:, cs(c)], ps[:, bank + c, :], ACT.Ln, bias=eps_ln[:, :]).then_inc(ln_sem, 1)
                    act.wait_ge(ln_sem, c + 1)
                    a.activation(buf[:, cs(c)], buf[:, cs(c)], ACT.Exp, scale=-0.5).then_inc(rs_sem, 1)

            for c in range(NCH):
                act.wait_ge(y1_mm, c + 1)
                a.activation(bs1[:, cs(c)], ps[:, 4 + c, :], ACT.Square).then_inc(y1_sq, 1)
            rstds(y1_var, y1_ln, y1_rs, bs2, 0)
            for c in range(NCH):
                act.wait_ge(rk_mm, c + 1)
                act.wait_ge(y1_var, c + 1)
                a.activation(bs1[:, cs(c)], ps[:, c, :], ACT.Tanh, scale=0.5).then_inc(th_ok, 1)
                a.activation(bs2[:, cs(c)], ps[:, 4 + c, :], ACT.Relu).then_inc(relu_ok, 1)
                act.wait_ge(relu_ok, c + 1)
                a.activation(bs3[:, cs(c)], bs2[:, cs(c)], ACT.Square).then_inc(k2_ok, 1)
            act.preload_act_table_set(LN_EXP)
            for c in range(NCH):
                act.wait_ge(y2_c, c + 1)
                a.activation(bs1[:, cs(c)], bs3[:, cs(c)], ACT.Square).then_inc(y2_sq, 1)
            rstds(y2_var, y2_ln, y2_rs, bs2, 0)
            for c in range(NCH):
                act.wait_ge(l1_mm, c + 1)
                a.activation(bs1[:, cs(c)], ps[:, 4 + c, :], ACT.Relu, bias=vec[:, BL1:BL1 + 1]).then_inc(l1_ok, 1)
            for c in range(NCH):
                act.wait_ge(l2_mm, c + 1)
                a.activation(bs3[:, cs(c)], ps[:, c, :], ACT.Tanh, bias=vec[:, BL2:BL2 + 1]).then_inc(l2_ok, 1)
            for c in range(NCH):
                act.wait_ge(f1_mm, c + 1)
                a.activation(bs1[:, cs(c)], ps[:, 4 + c, :], ACT.Relu, bias=vec[:, BF1:BF1 + 1]).then_inc(f1_ok, 1)
            act.preload_act_table_set(LN_EXP)
            for c in range(NCH):
                act.wait_ge(xt_mm, c + 1)
                a.activation(bxt[:, cs(c)], ps[:, c, :], ACT.Identity, bias=vec[:, BF2:BF2 + 1]).then_inc(xt_ok, 1)
            for c in range(NCH):
                act.wait_ge(d_mm, c + 1)
                a.activation(bs1[:, cs(c)], ps[:, 4 + c, :], ACT.Abs, bias=vec[:, B1:B1 + 1]).then_inc(d_abs, 1)
                act.wait_ge(d_abs, c + 1)
                a.activation(bs1[:, cs(c)], bs1[:, cs(c)], ACT.Exp, scale=-1.0).then_inc(d_exp, 1)
                act.wait_ge(d_exp, c + 1)
                a.activation(bs1[:, cs(c)], bs1[:, cs(c)], ACT.Ln, bias=1.0).then_inc(d_ln, 1)
            for c in range(NCH):
                act.wait_ge(c_mm, c + 1)
                a.activation(tr[0:96, 0, cs(c)], ps[0:96, c, :], ACT.Identity, bias=vec[0:96, B3:B3 + 1]).then_inc(c_hi, 1)

            def state_t(i, g):
                for j in range(GN):
                    n = g * GN + j
                    a.activation(vbuf[g][:, j, :], bdl[:, bass.ts(i, CH)], ACT.Exp,
                                 scale=amin[:, n:n + 1]).then_inc(e_t, 1)

            def state_da(i, g, ahead=True):
                if ahead and not (isinstance(i, int) and NG * i + g < 2):
                    act.wait_ge(e_sum, NG * i + g - 1)
                act.wait_ge(e_v, (NG * i + g + 1) * GN)
                a.activation(vbuf[g][:, :, :], vbuf[g][:, :, :], ACT.Exp, scale=-1.0, bias=1.0).then_inc(e_da, 1)

            act.wait_ge(a_ok, 2)
            act.wait_ge(o2x_ok, NCH)
            state_t(0, 0)
            for g in range(NG - 1):
                state_t(0, g + 1)
                state_da(0, g)
            with act.Fori(1, NCH) as i:
                state_t(i, 0)
                state_da(i - 1, NG - 1)
                for g in range(NG - 1):
                    state_t(i, g + 1)
                    state_da(i, g)
            state_da(NCH - 1, NG - 1, ahead=False)

            for c in range(NCH):
                act.wait_ge(y3_c, c + 1)
                act.wait_ge(e_p, NG * NCH)
                a.activation(bdl[:, cs(c)], bxt[:, cs(c)], ACT.Square).then_inc(y3_sq, 1)
            rstds(y3_var, y3_ln, y3_rs, bs1, 4)

            act.wait_ge(x3_ok, NCH)
            with act.Fori(0, NCH // 2) as i:
                for k in range(2):
                    for o in range(KH):
                        act.wait_ge(m_mm_, 6 * KH * i + k * KH + o + 1)
                        a.activation(vbuf[k][:, o, :], ps[:, 2 * o, :], ACT.Silu,
                                     scale=vec[:, S1 + o:S1 + o + 1]).then_inc(m_act, 1)
                for stage, s in ((1, SH1), (2, SH2)):
                    for k in range(2):
                        for o in range(KH):
                            n = (stage * 2 + k) * KH + o
                            act.wait_ge(m_mm_, 6 * KH * i + n + 1)
                            act.wait_ge(m_lo, 6 * KH * i + n + 1 - 2 * KH)
                            a.activation(vbuf[k][:, o, :], ps[:, 4 * k + o, :], ACT.Gelu,
                                         scale=vec[:, s + o:s + o + 1]).then_inc(m_act, 1)
                for k in range(2):
                    act.wait_ge(o_mv, 2 * i + k + 1)
                    a.activation(rstd[:, k, :], mv[:, k, :, 1], ACT.Sqrt, scale=1.0 / P, bias=eps_ln[:, :]).then_inc(o_sd, 1)

        @block.vector
        def _(dve):
            v = nc.vector
            v.memset(ones[:, :], 1.0 / P).then_inc(o_ok, 1)
            dve.wait_ge(o_ok, 1)
            v.memset(ones_n[:, :], 1.0).then_inc(consts, 1)
            v.memset(full(x1r[:, :, 0:2]), 0.0).then_inc(consts, 1)
            v.memset(eps_ln[:, :], EPS_LN).then_inc(consts, 1)
            dve.wait_ge(ident_ok, 1)
            v.tensor_scalar(res_ident[:, :], ident[:, :], float(res_gain), None, ALU.mult).then_inc(consts, 1)
            dve.wait_ge(wnorm_ok, 5)
            v.tensor_scalar(wnorm[:, :], wnorm[:, :], float(np.sqrt(P) * EPS_MP), None, ALU.add).then_inc(wnorm_ok, 1)
            dve.wait_ge(wnorm_ok, 6)
            v.reciprocal(wnorm[:, :], wnorm[:, :]).then_inc(wnorm_ok, 1)
            dve.wait_ge(wnorm_ok, 7)
            v.tensor_scalar(wnorm[:, :], wnorm[:, :], gain[:, :], None, ALU.mult).then_inc(wnorm_ok, 1)
            dve.wait_ge(wnorm_ok, 8)
            for i in range(4):
                v.tensor_scalar(wa[:, i, :], wa[:, i, :], wnorm[:, i:i + 1], None, ALU.mult).then_inc(ws_ok, 1)
            dve.wait_ge(wqk_hi, 1)
            dve.wait_ge(woT_ok, 1)
            v.tensor_tensor(wqk[:, 1, :], ps[:, 4, 0:2 * P], full(wqk[:, 0, :]), ALU.subtract).then_inc(wqk_lo, 1)
            for c in range(NCH):
                dve.wait_ge(x_hi, c + 1)
                v.tensor_tensor(xr[:, 1, cs(c)], ps[:, c, :], full(xr[:, 0, cs(c)]), ALU.subtract).then_inc(x_lo, 1)
            for p in range(2 * NCH):
                dve.wait_ge(k_ok, p + 1)
                qk = ps[:, p % 4, :].rearrange("p (t w c) -> p t w c", t=2, w=2)
                v.tensor_copy(q_sb[:, 2 * p:2 * p + 2, :], qk[:, :, 0, :]).then_inc(q_ok, 1)
                dve.wait_ge(sq_ok, p + 1)
                v.tensor_reduce(ss[:, p].rearrange("p a b h -> p (a b h)"),
                                sq[:, p % 2, :].rearrange("p (g e) -> p g e", e=HD), AX.X, ALU.add).then_inc(ss_ok, 1)
                if p % NCH == NCH - 1:
                    h = p // NCH
                    s = slice(h * NCH, (h + 1) * NCH)
                    dve.wait_ge(nrm_ok, h + 1)
                    v.tensor_scalar(ss[:, s], ss[:, s], EPS_MP, None, ALU.add).then_inc(nrm_step, 1)
                    dve.wait_ge(nrm_step, 3 * h + 1)
                    v.tensor_tensor(qkrec[:, s], ss[:, s, :, 0, :], ss[:, s, :, 1, :], ALU.mult).then_inc(nrm_step, 1)
                    dve.wait_ge(nrm_step, 3 * h + 2)
                    v.reciprocal(qkrec[:, s], qkrec[:, s]).then_inc(nrm_step, 1)
                    dve.wait_ge(nrm_step, 3 * h + 3)
                    qh = q_sb[:, h * NT // 2:(h + 1) * NT // 2, :].rearrange("p n (h e) -> p (n h) e", e=HD)
                    r = qkrec[:, s].rearrange("p a b (h e) -> p (a b h) e", e=1).broadcast_to([P, NT // 2 * HEADS, HD])
                    dve.wait_ge(q_ok, NCH * (h + 1))
                    v.tensor_tensor(qh, qh, r, ALU.mult).then_inc(qn_ok, 1)
            dve.wait_ge(vecT_mm, 1)
            dve.wait_ge(h0T_mm, 1)
            v.tensor_copy(vec[:, :], ps[:, 5, 0:NVEC]).then_inc(vec_ok, 1)
            dve.wait_ge(vec_ok, 1)
            v.tensor_scalar(mu1[:, :], vec[:, MU_R:MU_R + 2], -1.0, 1.0, ALU.mult, ALU.add).then_inc(mu1_ok, 1)
            v.tensor_copy(h0T[:, :], ps[0:96, 5, P:2 * P]).then_inc(h0f_ok, 1)
            dve.wait_ge(h0f_ok, 1)
            v.tensor_copy(h0hi[:, :], h0T[:, :]).then_inc(h0f_ok, 1)
            dve.wait_ge(h0f_ok, 2)
            v.tensor_copy(h0T[0:64, :], full(h0hi[0:64, :])).then_inc(h0f_ok, 1)
            v.tensor_tensor(h0T[64:96, :], h0T[64:96, :], full(h0hi[64:96, :]), ALU.subtract).then_inc(h0f_ok, 1)
            dve.wait_ge(h0f_ok, 4)
            dve.wait_ge(sc_mm, 1)
            dve.wait_ge(mask_ok, 2)
            v.scalar_tensor_tensor(sm[:, :], ps[:, 4, 0:P], float(1.0 / np.sqrt(T)), mask[:, :], ALU.mult,
                                   ALU.add).then_inc(sm_ok, 1)
            dve.wait_ge(sm_ok, 1)
            v.tensor_reduce(smax[:, :], sm[:, :], AX.X, ALU.max, negate=True).then_inc(smax_ok, 1)
            dve.wait_ge(exp_ok, 1)
            v.reciprocal(srec[:, :], ssum[:, :]).then_inc(srec_ok, 1)
            dve.wait_ge(srec_ok, 1)
            v.tensor_scalar(prob[:, :], prob[:, :], srec[:, :], None, ALU.mult).then_inc(prob_ok, 1)
            dve.wait_ge(w0T_mm, 1)
            dve.wait_ge(mu1_ok, 1)
            for i, (j, s) in enumerate(((0, vec[:, MU_R:MU_R + 1]), (0, mu1[:, 0:1]), (1, vec[:, MU_K:MU_K + 1]),
                                        (1, mu1[:, 1:2]))):
                v.tensor_scalar(w0f[:, i, :], ps[:, 6, j * P:(j + 1) * P], s, None, ALU.mult).then_inc(w0f_ok, 1)
            v.tensor_copy(w0f[:, 4, :], ps[:, 6, 2 * P:3 * P]).then_inc(w0f_ok, 1)
            dve.wait_ge(m_mm, 1)
            v.scalar_tensor_tensor(mix[:, :], ps[:, 7, 0:P], float(out_gain), res_ident[:, :], ALU.mult,
                                   ALU.add).then_inc(mix_ok, 1)
            dve.wait_ge(mix_ok, 1)
            v.tensor_reduce(mrow[:, :], mix[:, :], AX.X, ALU.add).then_inc(mix_ok, 1)
            dve.wait_ge(mix_ok, 2)
            v.tensor_scalar(mrow[:, :], mrow[:, :], 1.0 / P, None, ALU.mult).then_inc(mix_ok, 1)
            dve.wait_ge(mix_ok, 3)
            v.tensor_scalar(mix[:, :], mix[:, :], mrow[:, :], None, ALU.subtract).then_inc(mix_ok, 1)
            dve.wait_ge(mix_ok, 4)
            v.tensor_copy(mixr[:, 0, :], mix[:, :]).then_inc(mix_ok, 1)
            dve.wait_ge(mix_ok, 5)
            v.tensor_tensor(mixr[:, 1, :], mix[:, :], full(mixr[:, 0, :]), ALU.subtract).then_inc(mix_ok, 1)
            dve.wait_ge(w0f_ok, 5)
            v.tensor_copy(w0[:, :, 0, :], w0f[:, :, :]).then_inc(w0_hi, 1)
            dve.wait_ge(w0_hi, 1)
            v.tensor_tensor(w0[:, :, 1, :], w0f[:, :, :], full(w0[:, :, 0, :]), ALU.subtract).then_inc(w0_lo, 1)
            dve.wait_ge(ld_w1, 16 * 13)
            v.tensor_copy(w1[:, :, 0, :], w1raw[:, :, :]).then_inc(w1_hi, 1)
            dve.wait_ge(w1_hi, 1)
            v.tensor_tensor(w1[:, :, 1, :], w1raw[:, :, :], full(w1[:, :, 0, :]), ALU.subtract).then_inc(w1_lo, 1)
            v.tensor_scalar(amin[:, :], amat[:, :], 0.0, None, ALU.min).then_inc(a_ok, 1)
            v.tensor_scalar(amax[:, :], amat[:, :], 0.0, None, ALU.max).then_inc(a_ok, 1)
            for f in range(nfill):
                dve.wait_ge(fill_hi, f + 1)
                v.tensor_tensor(wf[:, f, 1, :], ps[:, f % 4, :], full(wf[:, f, 0, :]), ALU.subtract).then_inc(fill_lo, 1)

            def high(full_sem, hi_sem, full_buf, dst, c):
                dve.wait_ge(full_sem, c + 1)
                v.tensor_copy(dst(c)[0], full_buf[:, cs(c)]).then_inc(hi_sem, 1)

            for c in range(NCH):
                dve.wait_ge(y1_rs, c + 1)
                v.tensor_tensor(bx1[:, cs(c)], ps[:, 4 + c, :], bs2[:, cs(c)], ALU.mult).then_inc(x1_ok, 1)
                high(x1_ok, x1_hi, bx1, lambda c: parts(x1r, c, 2), c)
            for c in range(NCH):
                high(k2_ok, k2_hi, bs3, lambda c: parts(tr, c), c)
            for c in range(NCH):
                dve.wait_ge(v_mm, c + 1)
                dve.wait_ge(th_ok, c + 1)
                v.scalar_tensor_tensor(bs1[:, cs(c)], bs1[:, cs(c)], 1.0, ps[:, c, :], ALU.add,
                                       ALU.mult).then_inc(p_ok, 1)
                dve.wait_ge(p_ok, c + 1)
                v.scalar_tensor_tensor(bs3[:, cs(c)], bs1[:, cs(c)], 0.5, bx1[:, cs(c)], ALU.mult,
                                       ALU.add).then_inc(y2_ok, 1)
            for c in range(NCH):
                dve.wait_ge(y2_mean, c + 1)
                v.tensor_tensor(bs3[:, cs(c)], bs3[:, cs(c)], ps[:, 4 + c, :], ALU.subtract).then_inc(y2_c, 1)
            for c in range(NCH):
                dve.wait_ge(y2_rs, c + 1)
                v.tensor_tensor(bx2[:, cs(c)], bs3[:, cs(c)], bs2[:, cs(c)], ALU.mult).then_inc(x2_ok, 1)
                high(x2_ok, x2_hi, bx2, lambda c: parts(xr, c), c)
            for c in range(NCH):
                high(l1_ok, l1_hi, bs1, lambda c: parts(tr, c), c)
            for c in range(NCH):
                high(l2_ok, l2_hi, bs3, lambda c: parts(lr, c), c)
            for c in range(NCH):
                high(f1_ok, f1_hi, bs1, lambda c: parts(tr, c), c)
            for c in range(NCH):
                high(xt_ok, xt_hi, bxt, lambda c: parts(x1r, c, 2), c)
            for c in range(NCH):
                dve.wait_ge(d_abs, c + 1)
                v.tensor_scalar(bs2[:, cs(c)], ps[:, 4 + c, :], vec[:, B1:B1 + 1], 0.0, ALU.add,
                                ALU.max).then_inc(d_max, 1)
            for c in range(NCH):
                dve.wait_ge(c_hi, c + 1)
                dve.wait_ge(d_ok, c + 1)
                v.tensor_scalar(bs2[0:32, cs(c)], ps[0:32, c, :], vec[0:32, B3:B3 + 1], None, ALU.add).then_inc(c_f, 1)
                v.scalar_tensor_tensor(tr[32:64, 0, cs(c)], ps[32:64, c, :], vec[32:64, B3:B3 + 1],
                                       full(tr[32:64, 0, cs(c)]), ALU.add, ALU.subtract).then_inc(c_lo, 1)
                dve.wait_ge(b_mm, c + 1)
                dve.wait_ge(c_f, c + 1)
                v.scalar_tensor_tensor(bs2[0:32, cs(c)], ps[0:32, 4 + c, :], vec[0:32, B2:B2 + 1], bs2[0:32, cs(c)],
                                       ALU.add, ALU.mult).then_inc(bc_ok, 1)
            for c in range(NCH):
                dve.wait_ge(g_ok, c + 1)
                dve.wait_ge(bc_mm, c + 1)
                v.tensor_tensor(bxt[:, cs(c)], bxt[:, cs(c)], ps[:, c, :], ALU.mult).then_inc(o2_ok, 1)

            def state_v(i, g):
                for j in range(GN):
                    n = g * GN + j
                    dve.wait_ge(e_t, (NG * i + g) * GN + j + 1)
                    v.scalar_tensor_tensor(vbuf[g][:, j, :], bdl[:, bass.ts(i, CH)], amax[:, n:n + 1],
                                           vbuf[g][:, j, :], ALU.mult, ALU.add).then_inc(e_v, 1)

            def state_p(i, g):
                dve.wait_ge(e_da, NG * i + g + 1)
                dve.wait_ge(e_ch, NG * i + g + 1)
                v.tensor_tensor(vbuf[g][:, :, :], vbuf[g][:, :, :], ps[:, 0:GN, :], ALU.mult).then_inc(e_p, 1)

            state_v(0, 0)
            for g in range(NG - 1):
                state_v(0, g + 1)
                state_p(0, g)
            with dve.Fori(1, NCH) as i:
                state_v(i, 0)
                state_p(i - 1, NG - 1)
                for g in range(NG - 1):
                    state_v(i, g + 1)
                    state_p(i, g)
            state_p(NCH - 1, NG - 1)

            for c in range(NCH):
                dve.wait_ge(e_sum, NG * (c + 1))
                dve.wait_ge(o2x_ok, c + 1)
                v.tensor_tensor(bxt[:, cs(c)], bxt[:, cs(c)], ps[:, 4 + c, :], ALU.add).then_inc(y3_ok, 1)
            for c in range(NCH):
                dve.wait_ge(y3_mean, c + 1)
                v.tensor_tensor(bxt[:, cs(c)], bxt[:, cs(c)], ps[:, c, :], ALU.subtract).then_inc(y3_c, 1)
            for c in range(NCH):
                dve.wait_ge(y3_rs, c + 1)
                v.tensor_tensor(bx2[:, cs(c)], bxt[:, cs(c)], bs1[:, cs(c)], ALU.mult).then_inc(x3_ok, 1)
                high(x3_ok, x3_hi, bx2, lambda c: parts(lr, c), c)

            with dve.Fori(0, NCH // 2) as i:
                for stage in range(3):
                    for k in range(2):
                        for o in range(KH):
                            n = (stage * 2 + k) * KH + o
                            dve.wait_ge(m_act, 6 * KH * i + n + 1)
                            if stage == 0:
                                v.scalar_tensor_tensor(vbuf[k][:, o, :], ps[:, 2 * o + 1, :],
                                                       vec[:, S2 + o:S2 + o + 1], vbuf[k][:, o, :], ALU.mult,
                                                       ALU.mult).then_inc(m_full, 1)
                                dve.wait_ge(m_full, 2 * KH * i + n + 1)
                            v.tensor_copy(slot[(2 * stage + k) % 3][:, 0, o, :], vbuf[k][:, o, :]).then_inc(m_hi, 1)
                yb = [bs3[:, k * CH:(k + 1) * CH] for k in range(2)]
                for k in range(2):
                    dve.wait_ge(o_mm, 2 * i + k + 1)
                    v.scalar_tensor_tensor(yb[k], ps[:, 4 * k, :], vec[:, S3:S3 + 1],
                                           bx2[:, bass.ts(2 * i + k, CH)], ALU.mult, ALU.add).then_inc(o_y, 1)
                for k in range(2):
                    dve.wait_ge(o_T, 2 * i + k + 1)
                    yt = ps[:, 4 * k + 1, :].rearrange("p (n c) -> p n c", c=P)
                    for n in range(TPC):
                        v.bn_stats(stats[:, k, n, :], yt[:, n, :]).then_inc(o_st, 1)
                    dve.wait_ge(o_st, (2 * i + k + 1) * TPC)
                    me, mo, m2e, m2o = [stats[:, k, :, j] for j in (1, 4, 2, 5)]
                    v.tensor_tensor(mv[:, k, :, 0], me, mo, ALU.add).then_inc(o_stat, 1)
                    v.tensor_tensor(mdif[:, k, :], me, mo, ALU.subtract).then_inc(o_stat, 1)
                    v.tensor_tensor(mv[:, k, :, 1], m2e, m2o, ALU.add).then_inc(o_stat, 1)
                    dve.wait_ge(o_stat, (2 * i + k) * 5 + 2)
                    v.tensor_tensor(mdif[:, k, :], mdif[:, k, :], mdif[:, k, :], ALU.mult).then_inc(o_stat, 1)
                    dve.wait_ge(o_stat, (2 * i + k) * 5 + 1)
                    v.tensor_scalar(mv[:, k, :, 0], mv[:, k, :, 0], 0.5, None, ALU.mult).then_inc(o_stat, 1)
                    dve.wait_ge(o_stat, (2 * i + k) * 5 + 4)
                    v.scalar_tensor_tensor(mv[:, k, :, 1], mdif[:, k, :], P / 4.0, mv[:, k, :, 1], ALU.mult,
                                           ALU.add).then_inc(o_mv, 1)
                for k in range(2):
                    dve.wait_ge(o_sd, 2 * i + k + 1)
                    v.reciprocal(rstd[:, k, :], rstd[:, k, :]).then_inc(o_rs, 1)
                    dve.wait_ge(o_rs, 2 * i + k + 1)
                    dve.wait_ge(o_stat, (2 * i + k) * 5 + 5)
                    yt = ps[:, 4 * k + 1, :].rearrange("p (n c) -> p n c", c=P)
                    for n in range(TPC):
                        v.tensor_scalar(bdl[:, bass.ds((2 * i + k) * CH + n * P, P)], yt[:, n, :],
                                        mv[:, k, n, 0:1], rstd[:, k, n:n + 1], ALU.subtract,
                                        ALU.mult).then_inc(o_ok, 1)

        @block.tensor
        def _(pe):
            m = nc.tensor
            pe.wait_ge(ident_ok, 1)
            pe.wait_ge(ws_ok, 3)
            for i in range(3):
                last = m.transpose(ps[:, 4, i * P:(i + 1) * P], wa[:, i, :], ident[:, :])
            last.then_inc(wT_mm, 1)
            for c in range(NCH):
                pe.wait_ge(ld_x[c], 16)
                for n in range(TPC):
                    last = m.transpose(ps[:, c, n * P:(n + 1) * P], x_tok[:, c * TPC + n, :], ident[:, :])
                last.then_inc(xT_mm, 1)
            pe.wait_ge(wqk_lo, 1)
            for p in range(2 * NCH):
                pe.wait_ge(x_lo, min(p + 1, NCH))
                if p >= 4:
                    pe.wait_ge(sq_ok, p - 3)
                    pe.wait_ge(k_ok, p - 3)
                    pe.wait_ge(q_ok, p - 3)
                for h in range(2):
                    tok = slice((2 * p + h) * P, (2 * p + h + 1) * P)
                    dst = ps[:, p % 4, h * 2 * P:(h + 1) * 2 * P]
                    last = mm3(dst, (xr[:, 0, tok], xr[:, 1, tok]), (wqk[:, 0, :], wqk[:, 1, :]))
                last.then_inc(qk_mm, 1)
            pe.wait_ge(ld_vec, 16 * 16)
            m.transpose(ps[:, 5, 0:NVEC], vrow[:, :], ident[0:NVEC, 0:NVEC]).then_inc(vecT_mm, 1)
            pe.wait_ge(ld_w1, 16 * 13)
            m.transpose(ps[0:96, 5, P:2 * P], h0raw[:, :], ident[:, :]).then_inc(h0T_mm, 1)
            pe.wait_ge(ld_w0, 16 * 3)
            for i in range(3):
                last = m.transpose(ps[:, 6, i * P:(i + 1) * P], w0raw[:, i, :], ident[:, :])
            last.then_inc(w0T_mm, 1)

            def fills(lo, hi):
                for f in range(lo, hi):
                    if f < 4:
                        pe.wait_ge(sq_ok, NCH + f + 1)
                        pe.wait_ge(k_ok, NCH + f + 1)
                        pe.wait_ge(q_ok, NCH + f + 1)
                    else:
                        pe.wait_ge(fill_lo, f - 3)
                    if f == 0:
                        pe.wait_ge(ld_f, 16 * 3)
                    if f == 3:
                        pe.wait_ge(ld_h1, 16)
                    if f == 3 + KH:
                        pe.wait_ge(ld_h2, 16)
                    for r in range(KH):
                        if f < 3:
                            src = w12raw[:, f, r, :]
                        else:
                            h, k = divmod(f - 3, KH)
                            src = hraw[h][:, r, k * P:(k + 1) * P]
                        last = m.transpose(ps[:, f % 4, r * P:(r + 1) * P], src, ident[:, :])
                    last.then_inc(fill_mm, 1)

            fills(0, 4)
            for n in range(NT):
                if n % (NT // 2) == 0:
                    pe.wait_ge(qn_ok, 2 * n // NT + 1)
                pe.wait_ge(k_ok, 2 * NCH)
                last = m.matmul(ps[:, 4, 0:P], q_sb[:, n, :], k_sb[:, n, :], start=(n == 0), stop=(n == NT - 1))
            last.then_inc(sc_mm, 1)
            pe.wait_ge(prob_ok, 1)
            pe.wait_ge(woT_ok, 1)
            pe.wait_ge(h0f_ok, 1)
            m.matmul(ps[:, 5, 0:P], prob[:, :], woT[:, :], start=True, stop=True).then_inc(u_mm, 1)
            pe.wait_ge(u_ok, 1)
            pe.wait_ge(ws_ok, 4)
            m.matmul(ps[:, 7, 0:P], wa[:, 3, :], u_sb[:, :], start=True, stop=True).then_inc(m_mm, 1)
            fills(4, nfill)

            def means(src_sem, dst_sem, buf, bank):
                for c in range(NCH):
                    pe.wait_ge(src_sem, c + 1)
                    m.matmul(ps[:, bank + c, :], ones[:, :], buf[:, cs(c)], start=True, stop=True).then_inc(dst_sem, 1)

            pe.wait_ge(mix_ok, 6)
            for c in range(NCH):
                m3 = mm3(ps[:, 4 + c, :], (mixr[:, 0, :], mixr[:, 1, :]), parts(xr, c))
                m3.then_inc(y1_mm, 1)
            pe.wait_ge(fill_lo, nfill)
            pe.wait_ge(consts, 4)
            pe.wait_ge(o_ok, 1)
            means(y1_sq, y1_var, bs1, 0)
            pe.wait_ge(w0_lo, 1)
            for c in range(NCH):
                pe.wait_ge(x1_lo, c + 1)
                for bank, w in ((c, 0), (4 + c, 2)):
                    mm3(ps[:, bank, :], pair(w0, w), parts(x1r, c, 2), stop=False)
                    last = mm3(ps[:, bank, :], pair(w0, w + 1), parts(x1r, c, 1), start=False)
                last.then_inc(rk_mm, 1)
            for c in range(NCH):
                pe.wait_ge(k2_lo, c + 1)
                mm3(ps[:, c, :], pair(w0, 4), parts(tr, c)).then_inc(v_mm, 1)
            means(y2_ok, y2_mean, bs3, 4)
            means(y2_sq, y2_var, bs1, 0)
            pe.wait_ge(w1_lo, 1)
            for c in range(NCH):
                pe.wait_ge(x2_lo, c + 1)
                mm3(ps[:, 4 + c, :], pair(w1, 0), parts(xr, c)).then_inc(l1_mm, 1)
            for c in range(NCH):
                pe.wait_ge(l1_lo, c + 1)
                mm3(ps[:, c, :], pair(w1, 1), parts(tr, c)).then_inc(l2_mm, 1)
            for c in range(NCH):
                mm3(ps[:, 4 + c, :], pair(w1, 2), parts(xr, c), stop=False)
                pe.wait_ge(l2_lo, c + 1)
                mm3(ps[:, 4 + c, :], pair(w1, 3), parts(lr, c), start=False).then_inc(f1_mm, 1)
            for c in range(NCH):
                pe.wait_ge(f1_lo, c + 1)
                mm3(ps[:, c, :], pair(w1, 4), parts(tr, c)).then_inc(xt_mm, 1)
            for c in range(NCH):
                pe.wait_ge(xt_lo, c + 1)
                mm3(ps[:, 4 + c, :], pair(w1, 5), parts(x1r, c, 2)).then_inc(d_mm, 1)
            for c in range(NCH):
                mm3(ps[:, c, :], pair(w1, 6), parts(x1r, c, 2)).then_inc(c_mm, 1)
            for c in range(NCH):
                pe.wait_ge(d_abs, c + 1)
                pe.wait_ge(d_max, c + 1)
                mm3(ps[:, 4 + c, :], pair(w1, 7), parts(x1r, c, 2)).then_inc(b_mm, 1)
            for c in range(NCH):
                pe.wait_ge(bc_ok, c + 1)
                pe.wait_ge(c_lo, c + 1)
                m.matmul(ps[:, c, :], ones_n[:, :], bs2[0:32, cs(c)], start=True, stop=True).then_inc(bc_mm, 1)

            def state_ch(i, g):
                for j in range(GN):
                    last = m.matmul(ps[:, j, :], h0sel[:, g * GN + j, :], tr[0:96, 0, bass.ts(i, CH)],
                                    start=True, stop=True)
                last.then_inc(e_ch, 1)

            def state_sum(i, g):
                for j in range(GN):
                    last = m.matmul(ps[:, i + 4, :], ident[:, :], vbuf[g][:, j, :], start=(g == 0 and j == 0),
                                    stop=(g == NG - 1 and j == GN - 1))
                last.then_inc(e_sum, 1)

            pe.wait_ge(h0sel_ok, 3)
            pe.wait_ge(o2_ok, NCH)
            state_ch(0, 0)
            for g in range(NG - 1):
                pe.wait_ge(e_p, g + 1)
                state_ch(0, g + 1)
                state_sum(0, g)
            with pe.Fori(1, NCH) as i:
                pe.wait_ge(e_p, NG * i)
                state_ch(i, 0)
                state_sum(i - 1, NG - 1)
                for g in range(NG - 1):
                    pe.wait_ge(e_p, NG * i + g + 1)
                    state_ch(i, g + 1)
                    state_sum(i, g)
            pe.wait_ge(e_p, NG * NCH)
            state_sum(NCH - 1, NG - 1)
            means(y3_ok, y3_mean, bxt, 0)
            means(y3_sq, y3_var, bdl, 4)

            pe.wait_ge(y3_rs, NCH)
            with pe.Fori(0, NCH // 2) as i:
                for k in range(2):
                    pe.wait_ge(x3_lo, 2 * i + k + 1)
                    s = bass.ts(2 * i + k, CH)
                    for o in range(KH):
                        if k == 0:
                            pe.wait_ge(o_ok, 2 * i * TPC + 1)
                        else:
                            pe.wait_ge(m_full, 2 * KH * i + o + 1)
                        wo = slice(o * P, (o + 1) * P)
                        mm3(ps[:, 2 * o, :], (wf[:, 0, 0, wo], wf[:, 0, 1, wo]), (lr[:, 0, s], lr[:, 1, s]))
                        mm3(ps[:, 2 * o + 1, :], (wf[:, 1, 0, wo], wf[:, 1, 1, wo]),
                            (lr[:, 0, s], lr[:, 1, s])).then_inc(m_mm_, 1)
                for stage in (1, 2):
                    for k in range(2):
                        src = slot[(2 * stage - 2 + k) % 3]
                        last_stage = 6 * KH * i + (2 * stage - 2 + k) * KH
                        pe.wait_ge(m_act, 6 * KH * i + (2 * stage - 1 + k) * KH)
                        if stage == 1:
                            pe.wait_ge(m_full, 2 * KH * i + 2 * KH)
                        for o in range(KH):
                            wo = slice(o * P, (o + 1) * P)
                            for kk in range(KH):
                                if o == 0:
                                    pe.wait_ge(m_lo, last_stage + kk + 1)
                                f = 3 + (stage - 1) * KH + kk
                                last = mm3(ps[:, 4 * k + o, :], (wf[:, f, 0, wo], wf[:, f, 1, wo]),
                                           (src[:, 0, kk, :], src[:, 1, kk, :]), start=(kk == 0), stop=(kk == KH - 1))
                            last.then_inc(m_mm_, 1)
                for k in range(2):
                    src = slot[(4 + k) % 3]
                    pe.wait_ge(m_act, 6 * KH * i + (5 + k) * KH)
                    for kk in range(KH):
                        pe.wait_ge(m_lo, 6 * KH * i + (4 + k) * KH + kk + 1)
                        wo = slice(kk * P, (kk + 1) * P)
                        last = mm3(ps[:, 4 * k, :], (wf[:, 2, 0, wo], wf[:, 2, 1, wo]),
                                   (src[:, 0, kk, :], src[:, 1, kk, :]), start=(kk == 0), stop=(kk == KH - 1))
                    last.then_inc(o_mm, 1)
                for k in range(2):
                    pe.wait_ge(o_y, 2 * i + k + 1)
                    for n in range(TPC):
                        last = m.transpose(ps[:, 4 * k + 1, n * P:(n + 1) * P],
                                           bs3[:, k * CH + n * P:k * CH + (n + 1) * P], ident[:, :])
                    last.then_inc(o_T, 1)


_INS = [
    "L0_attn_query", "L0_attn_gain", "L0_attn_w_q", "L0_attn_w_k", "L0_attn_w_v", "L0_attn_w_o", "L0_ffn_W_r",
    "L0_ffn_W_k", "L0_ffn_W_v", "L0_ffn_mu_r", "L0_ffn_mu_k", "L1_attn_W1", "L1_attn_b1", "L1_attn_W2", "L1_attn_b2",
    "L1_attn_W3", "L1_attn_b3", "L1_attn_Wl1", "L1_attn_bl1", "L1_attn_Wl2", "L1_attn_bl2", "L1_attn_Wf1",
    "L1_attn_bf1", "L1_attn_Wf2", "L1_attn_bf2", "L1_attn_state_init", "L1_attn_A", "L1_ffn_w1_w", "L1_ffn_w1_s",
    "L1_ffn_w2_w", "L1_ffn_w2_s", "L1_ffn_h1_w", "L1_ffn_h1_s", "L1_ffn_h2_w", "L1_ffn_h2_s", "L1_ffn_w3_w",
    "L1_ffn_w3_s",
]


def kernel(**inputs):
    import numpy as _np
    import concourse.bacc as _bacc
    from concourse import mybir as _mybir
    from concourse.bass_utils import run_bass_kernel_spmd as _run

    nc = _bacc.Bacc("TRN2", target_bir_lowering=False, num_devices=1)
    arrays, tensors = {}, {}
    for name in _INS:
        a = _np.ascontiguousarray(inputs[name])
        arrays[f"in_{name}_dram"] = a
        tensors[name] = nc.dram_tensor(f"in_{name}_dram", a.shape, _mybir.dt.from_np(a.dtype),
                                       kind="ExternalInput").ap()
    shape = inputs["L0_attn_query"].shape
    out = nc.dram_tensor("out_0_dram", tuple(shape), _mybir.dt.float32, kind="ExternalOutput").ap()
    build(nc, tensors, out)
    r = _run(nc, [arrays], core_ids=[0])
    return r.results[0]["out_0_dram"]
```

```python
from contextlib import ExitStack

import numpy as np
import concourse.bass as bass
from concourse import mybir

F32 = mybir.dt.float32
F32R = mybir.dt.float32r
ALU = mybir.AluOpType
ACT = mybir.ActivationFunctionType
AX = mybir.AxisListType

P = 128
CH = 512
HEADS = 16
HD = P // HEADS
NS = 16
GN = 2
NG = NS // GN
EPS_MP = 1e-4
EPS_LN = 1e-5
LN_EXP = "natural_log_exp_and_others"

MU_R, MU_K, BL1, BL2, BF1, BF2, B1, S3, S1, S2, SH1, SH2, B23 = 0, 1, 2, 3, 4, 5, 6, 7, 8, 12, 16, 20, 24
A_COL = 25
GAIN_COL = A_COL + NS
NSMALL = GAIN_COL + 1


def build(nc, t, out):
    x_d = t["x"]
    out_d = out.rearrange("a (n p) c -> (a p) n c", p=P)
    T = x_d.shape[1]
    NCH = T // CH
    NT = T // P
    TPC = CH // P
    HID = t["w_mlp"].shape[2]
    KH = HID // P
    res_gain = 1.0 + 0.5 / np.sqrt(0.5)
    out_gain = 0.5 / np.sqrt(0.5)

    ctx = ExitStack()
    with ctx:
        def sb(name, shape, dt=F32):
            return ctx.enter_context(nc.sbuf_tensor(name, shape, dt))

        def sem(name):
            return ctx.enter_context(nc.semaphore(name))

        ps = ctx.enter_context(nc.psum_tensor("ps", [P, 8, CH], F32))

        ident = sb("ident", [P, P])
        ones = sb("ones", [P, P])
        centre = sb("centre", [P, P])
        centre_r = sb("centre_r", [P, P], F32R)
        ones_n = sb("ones_n", [32, P])
        res_ident = sb("res_ident", [P, P])
        mask = sb("mask", [P, P])
        vec = sb("vec", [P, NSMALL])
        amat, gain = vec[:, A_COL:A_COL + NS], vec[:, GAIN_COL:GAIN_COL + 1]
        mu1 = sb("mu1", [P, 2])
        wa = sb("wa", [P, 4, P])
        wss = sb("wss", [P, 4])
        wnorm = sb("wnorm", [P, 4])

        wqk = sb("wqk", [P, 2, 2 * P], F32R)
        woT = sb("woT", [P, P])
        sm = sb("sm", [P, P])
        smax = sb("smax", [P, 1])
        ssum = sb("ssum", [P, 1])
        srec = sb("srec", [P, 1])
        prob = sb("prob", [P, P])
        u_sb = sb("u_sb", [P, P])
        mix = sb("mix", [P, P])
        mrow = sb("mrow", [P, 1])
        mixr = sb("mixr", [P, 2, P], F32R)
        w0raw = sb("w0raw", [P, 3, P])
        w0f = sb("w0f", [P, 5, P])
        w0 = sb("w0", [P, 5, 2, P], F32R)
        w1 = sb("w1", [P, 7, 2, P], F32R)
        h0T = sb("h0T", [96, P])
        h0hi = sb("h0hi", [96, P], F32R)
        eps_ln = sb("eps_ln", [P, 1])
        h0sel = sb("h0sel", [96, NS, P], F32R)
        amin = sb("amin", [P, NS])
        amax = sb("amax", [P, NS])
        nfill = 3 + 2 * KH
        NLOW = (nfill + 3) // 4
        wf = sb("wf", [P, nfill, 2, HID], F32R)
        ss = sb("ss", [P, NCH * 2, 2, 2, HEADS])
        qkrec = sb("qkrec", [P, NCH * 2, 2, HEADS])
        stats = sb("stats", [P, 2, TPC, 6])
        mdif = sb("mdif", [P, 2, TPC])
        mv = sb("mv", [P, 2, TPC, 2])
        rstd = sb("rstd", [P, 2, TPC])
        xr = sb("xr", [P, 2, T], F32R)
        x1r = sb("x1r", [P, 2, T + 2], F32R)
        tr = sb("tr", [P, 2, T], F32R)
        lr = sb("lr", [P, 2, T], F32R)
        bx1, bs1, bs2, bs3, bx2, bxt, bdl = [sb(n, [P, T]) for n in ("bx1", "bs1", "bs2", "bs3", "bx2", "bxt", "bdl")]

        q_sb = bx1[:, :].rearrange("p (n c) -> p n c", c=P)
        k_sb = bxt[:, :].rearrange("p (n c) -> p n c", c=P)
        sq = bdl[:, :].rearrange("p (n c) -> p n c", c=CH)
        w1raw = bdl[:, T // 2:T // 2 + 7 * P].rearrange("p (w c) -> p w c", c=P)
        FILL = T // HID
        staged = [b[:, :].rearrange("p (f c) -> p f c", c=HID) for b in (bs1, bs2, bs3)]
        slot = [xr[:, :, :].rearrange("p s (k n) -> p s k n", k=KH),
                x1r[:, :, 2:].rearrange("p s (k n) -> p s k n", k=KH),
                tr[:, :, :].rearrange("p s (k n) -> p s k n", k=KH)]
        vbuf = [b[:, :].rearrange("p (k n) -> p k n", k=GN) for b in (bx1, bx2, bs1, bs2, bs3)]
        NB = len(vbuf)
        zmax = bxt[:, 0:2 * CH]
        hbuf = [b[:, :].rearrange("p (k n) -> p k n", k=KH) for b in (bs1, bs2)]
        low_max = sb("low_max", [P, NLOW])
        low_any = sb("low_any", [P, 1])

        ld_x = [sem(f"ld_x{c}") for c in range(NCH)]
        ld_f = [sem(f"ld_f{j}") for j in range(NLOW)]
        ld_wa, ld_vec, ld_w0, ld_w1, ld_h0, stored = [
            sem(n) for n in ("ld_wa", "ld_vec", "ld_w0", "ld_w1", "ld_h0", "stored")]
        pads, ident_ok, mask_ok, consts = [sem(n) for n in ("pads", "ident_ok", "mask_ok", "consts")]
        wnorm_ok, ws_ok, wT_mm, wqk_hi, wqk_lo, woT_ok = [
            sem(n) for n in ("wnorm_ok", "ws_ok", "wT_mm", "wqk_hi",
                             "wqk_lo", "woT_ok")]
        mu1_ok, w0f_ok, w0_hi, w0_lo, w1_hi, w1_lo = [
            sem(n) for n in ("mu1_ok", "w0f_ok", "w0_hi", "w0_lo", "w1_hi", "w1_lo")]
        h0f_ok, h0sel_ok, a_ok = [
            sem(n) for n in ("h0f_ok", "h0sel_ok", "a_ok")]
        fill_hi0, fill_hi, fill_lo = [sem(n) for n in ("fill_hi0", "fill_hi", "fill_lo")]
        x_hi, x_lo_v, x_lo_p, qk_mm, sq_ok, k_ok, ss_ok, nrm_ok, nrm_step, qn_ok = [
            sem(n) for n in ("x_hi", "x_lo_dve", "x_lo_pool", "qk_mm", "sq_ok", "k_ok", "ss_ok", "nrm_ok", "nrm_step",
                             "qn_ok")]
        sc_mm, sm_ok, smax_ok, exp_ok, srec_ok, prob_ok, u_mm, u_ok, m_mm, mix_ok = [
            sem(n) for n in ("sc_mm", "sm_ok", "smax_ok", "exp_ok", "srec_ok", "prob_ok", "u_mm", "u_ok", "m_mm",
                             "mix_ok")]
        y1_mm, y1_sq, y1_var, y1_ln, y1_rs, x1_ok, x1_hi = [
            sem(n) for n in ("y1_mm", "y1_sq", "y1_var", "y1_ln", "y1_rs", "x1_ok", "x1_hi")]
        rk_mm, th_ok, relu_ok, k2_ok, k2_hi, v_mm, p_ok, y2_ok, y2_mm, y2_sq, y2_var, y2_ln, y2_rs = [
            sem(n) for n in ("rk_mm", "th_ok", "relu_ok", "k2_ok", "k2_hi", "v_mm", "p_ok", "y2_ok", "y2_mm", "y2_sq",
                             "y2_var", "y2_ln", "y2_rs")]
        x2_ok, x2_hi, l1_mm, l1_ok, l1_hi, l2_mm, l2_ok, l2_hi = [
            sem(n) for n in ("x2_ok", "x2_hi", "l1_mm", "l1_ok", "l1_hi", "l2_mm", "l2_ok", "l2_hi")]
        f1_mm, f1_ok, f1_hi, xt_mm, xt_ok, xt_hi, d_mm, d_abs, d_exp, d_ln, d_max, d_ok = [
            sem(n) for n in ("f1_mm", "f1_ok", "f1_hi", "xt_mm", "xt_ok", "xt_hi", "d_mm", "d_abs", "d_exp", "d_ln",
                             "d_max", "d_ok")]
        c_mm, c_hi, c_lo, b_ok, bc_ok, bc_mm, g_ok, o2_ok = [
            sem(n) for n in ("c_mm", "c_hi", "c_lo", "b_ok", "bc_ok", "bc_mm", "g_ok", "o2_ok")]
        e_first, e_t, e_v, e_zp, e_vp, e_da, e_ch, e_p, e_add, e_sum = [
            sem(n) for n in ("e_first", "e_t", "e_v_dve", "e_z_pool", "e_v_pool", "e_da", "e_ch", "e_p", "e_add", "e_sum")]
        y3_sq, y3_var, y3_ln, y3_rs, x3_ok, x3_hi = [
            sem(n) for n in ("y3_sq", "y3_var", "y3_ln", "y3_rs", "x3_ok", "x3_hi")]
        low_ok, low_mm, low_flag = [sem(n) for n in ("low_ok", "low_mm", "low_flag")]
        x1_lo, k2_lo, x2_lo, l1_lo, l2_lo, f1_lo, xt_lo, x3_lo = [
            (sem(n + "_dve"), sem(n + "_pool"))
            for n in ("x1_lo", "k2_lo", "x2_lo", "l1_lo", "l2_lo", "f1_lo", "xt_lo", "x3_lo")]
        m_mm_, m_act, m_full, m_hi, m_lo_p, m_lo_v = [
            sem(n) for n in ("mlp_mm", "mlp_act", "mlp_full", "mlp_hi", "mlp_lo_pool", "mlp_lo_dve")]
        o_mm, o_y, o_T, o_st, o_stat, o_mv, o_sd, o_rs, o_ok = [
            sem(n) for n in ("o_mm", "o_y", "o_T", "o_st", "o_stat", "o_mv", "o_sd", "o_rs", "o_ok")]

        def cs(c):
            return slice(c * CH, (c + 1) * CH)

        def full(b):
            return b.bitcast(F32)

        def mm3(dst, w, xs, start=True, stop=True):
            nc.tensor.matmul(dst, w[0], xs[0], start=start, stop=False)
            nc.tensor.matmul(dst, w[0], xs[1], start=False, stop=False)
            return nc.tensor.matmul(dst, w[1], xs[0], start=False, stop=stop)

        def pair(w, *i):
            return w[(slice(None), *i, 0)], w[(slice(None), *i, 1)]

        def parts(b, c, shift=0):
            s = slice(c * CH + shift, (c + 1) * CH + shift)
            return b[:, 0, s], b[:, 1, s]

        def wait_split(eng, lo_sems, c):
            eng.wait_ge(lo_sems[c % 2], c // 2 + 1)

        def v_on_pool(e, j):
            return e % 2 == 1 and j == 1

        def group_states(e):
            return [(e % NG) * GN + j for j in range(GN)]

        def pair_tokens(e):
            i = e // NG
            return slice(2 * i * CH, 2 * (i + 1) * CH)

        NE = NG * NCH // 2

        PAIR = 6 * KH
        RING = 6

        def mtile(i, stage, k, o):
            return PAIR * i + (2 * stage + k) * KH + o

        def mbank(i, stage, k, o):
            if stage == 0:
                return (PAIR + 2 * KH) * i + 2 * (k * KH + o)
            return (PAIR + 2 * KH) * i + 4 * KH + (2 * (stage - 1) + k) * KH + o

        def low_on_dve(n):
            return n % 4 == 3 if n % PAIR < 2 * KH else n % 2 == 1

        def wait_low(eng, n):
            on_dve = sum(low_on_dve(j) for j in range(n + 1))
            eng.wait_ge(m_lo_p, n + 1 - on_dve)
            if on_dve:
                eng.wait_ge(m_lo_v, on_dve)

        def wait_bank(pe, b):
            if b >= RING:
                i, r = divmod(b - RING, PAIR + 2 * KH)
                if r >= 4 * KH:
                    pe.wait_ge(m_act, PAIR * i + r - 2 * KH + 1)
                elif r % 2:
                    pe.wait_ge(m_full, 2 * KH * i + r // 2 + 1)
                else:
                    pe.wait_ge(m_act, PAIR * i + r // 2 + 1)

        block = ctx.enter_context(nc.Block())

        @block.sync
        def _(sp):
            sp.dma_start(wa[:, :, :], t["w_attn"]).then_inc(ld_wa, 16)
            sp.dma_start(vec[:, :], t["small"]).then_inc(ld_vec, 16)
            for c in range(NCH):
                sp.dma_start(bx2[:, cs(c)], x_d[:, cs(c)]).then_inc(ld_x[c], 16)
            for j in range(NLOW):
                n = min(FILL, nfill - j * FILL)
                if j == 0:
                    sp.dma_start(h0T[:, :], t["state"]).then_inc(ld_h0, 16)
                if j == 1:
                    sp.dma_start(w0raw[:, :, :], t["w_ffn"]).then_inc(ld_w0, 16)
                    sp.dma_start(w1raw, t["w_ssm"]).then_inc(ld_w1, 16)
                sp.dma_start(staged[j][:, 0:n, :], t["w_mlp"][:, j * FILL:j * FILL + n, :]).then_inc(ld_f[j], 16)
            with sp.Fori(0, NCH) as c:
                sp.wait_ge(o_ok, c * TPC + TPC + 1)
                sp.dma_start(out_d[:, bass.ts(c, TPC), :],
                             bdl[:, bass.ts(c, CH)].rearrange("p (n c) -> p n c", c=P)).then_inc(stored, 16)
            sp.wait_ge(stored, 16 * NCH)

        @block.gpsimd
        def _(pool):
            g = nc.gpsimd
            g.memset(ident[:, :], 0.0).then_inc(pads, 1)
            g.memset(mask[:, :], 0.0).then_inc(pads, 1)
            pool.wait_ge(pads, 2)
            g.affine_select(out=ident[:, :], in_=ident[:, :], compare_op=ALU.not_equal, fill=1.0, base=0,
                            pattern=[[-1, P]], channel_multiplier=1).then_inc(ident_ok, 1)
            m3 = mask[:, :].rearrange("p (h k) -> p h k", k=HD)
            g.affine_select(out=m3, in_=m3, compare_op=ALU.is_ge, fill=-1e30, base=0,
                            pattern=[[-HD, HEADS], [0, HD]], channel_multiplier=1).then_inc(mask_ok, 1)
            pool.wait_ge(mask_ok, 1)
            g.affine_select(out=m3, in_=m3, compare_op=ALU.is_ge, fill=-1e30, base=HD - 1,
                            pattern=[[HD, HEADS], [0, HD]], channel_multiplier=-1).then_inc(mask_ok, 1)
            for c in range(1, NCH, 2):
                pool.wait_ge(x_hi, c + 1)
                g.tensor_tensor(xr[:, 1, cs(c)], bx2[:, cs(c)], full(xr[:, 0, cs(c)]),
                                ALU.subtract).then_inc(x_lo_p, 1)
            pool.wait_ge(ld_f[0], 16)
            g.tensor_copy(wf[:, 0:FILL, 0, :], staged[0]).then_inc(fill_hi0, 1)
            pool.wait_ge(fill_hi0, 1)
            g.tensor_tensor(wf[:, 0:FILL, 1, :], staged[0], full(wf[:, 0:FILL, 0, :]), ALU.subtract).then_inc(fill_lo, 1)
            pool.wait_ge(mask_ok, 2)
            pool.wait_ge(h0f_ok, 3)
            for j in range(3):
                r = slice(32 * j, 32 * j + 32)
                if j:
                    pool.wait_ge(h0sel_ok, j)
                src = h0T[r, :].rearrange("p (n c) -> p n c", n=1).broadcast_to([32, NS, P])
                g.affine_select(out=h0sel[r, :, :], in_=src, compare_op=ALU.is_equal, fill=0.0, base=0,
                                pattern=[[-1, NS], [0, P]], channel_multiplier=1).then_inc(h0sel_ok, 1)
            pool.wait_ge(h0sel_ok, 3)
            for j in range(1, NLOW):
                n = min(FILL, nfill - j * FILL)
                pool.wait_ge(fill_hi, j)
                g.tensor_tensor(wf[:, j * FILL:j * FILL + n, 1, :], staged[j][:, 0:n, :],
                                full(wf[:, j * FILL:j * FILL + n, 0, :]), ALU.subtract).then_inc(fill_lo, 1)
            def lows(hi_sem, lo_sems, full_buf, r):
                for c in range(1, NCH, 2):
                    pool.wait_ge(hi_sem, c + 1)
                    hi, lo = r(c)
                    g.tensor_tensor(lo, full_buf[:, cs(c)], full(hi), ALU.subtract).then_inc(lo_sems[1], 1)

            lows(x1_hi, x1_lo, bx1, lambda c: parts(x1r, c, 2))
            lows(k2_hi, k2_lo, bs3, lambda c: parts(tr, c))
            lows(x2_hi, x2_lo, bx2, lambda c: parts(xr, c))
            lows(l1_hi, l1_lo, bs1, lambda c: parts(tr, c))
            lows(l2_hi, l2_lo, bs3, lambda c: parts(lr, c))
            lows(f1_hi, f1_lo, bs1, lambda c: parts(tr, c))
            lows(xt_hi, xt_lo, bxt, lambda c: parts(x1r, c, 2))
            for c in range(NCH):
                pool.wait_ge(d_ln, c + 1)
                pool.wait_ge(d_max, c + 1)
                g.tensor_tensor(bdl[:, cs(c)], bs1[:, cs(c)], bs2[:, cs(c)], ALU.add).then_inc(d_ok, 1)
            for c in range(NCH):
                pool.wait_ge(d_ok, c + 1)
                wait_split(pool, xt_lo, c)
                g.tensor_tensor(bxt[:, cs(c)], bxt[:, cs(c)], bdl[:, cs(c)], ALU.mult).then_inc(g_ok, 1)
            pool.wait_ge(a_ok, 2)
            pool.wait_ge(e_first, NCH)
            products = 0
            for e in range(NE):
                for j, n in enumerate(group_states(e)):
                    if v_on_pool(e, j):
                        if products:
                            pool.wait_ge(e_vp, products)
                        products += 1
                        g.tensor_scalar(zmax, bdl[:, pair_tokens(e)], amax[:, n:n + 1], None,
                                        ALU.mult).then_inc(e_zp, 1)
                        pool.wait_ge(e_zp, products)
                        pool.wait_ge(e_t, GN * e + j + 1)
                        g.tensor_tensor(vbuf[e % NB][:, j, :], vbuf[e % NB][:, j, :], zmax, ALU.add).then_inc(e_vp, 1)
                if e % 2:
                    pool.wait_ge(e_p, e)
                    b = vbuf[(e - 1) % NB]
                    g.tensor_tensor(b[:, 0, :], b[:, 0, :], b[:, 1, :], ALU.add).then_inc(e_add, 1)
            lows(x3_hi, x3_lo, bx2, lambda c: parts(lr, c))
            for i in range(NCH // 2):
                for stage in range(3):
                    for k in range(2):
                        for o in range(KH):
                            n = mtile(i, stage, k, o)
                            if low_on_dve(n):
                                continue
                            pool.wait_ge(m_hi, n + 1)
                            sl = slot[(2 * stage + k) % 3]
                            g.tensor_tensor(sl[:, 1, o, :], hbuf[k][:, o, :], full(sl[:, 0, o, :]),
                                            ALU.subtract).then_inc(m_lo_p, 1)

        @block.scalar
        def _(act):
            a = nc.scalar
            act.preload_act_table(ACT.Sqrt)
            act.wait_ge(ld_wa, 16)
            for i in range(4):
                a.activation(bxt[:, i * P:(i + 1) * P], wa[:, i, :], ACT.Square, accum_out=wss[:, i:i + 1]).then_inc(wnorm_ok, 1)
            act.wait_ge(wnorm_ok, 4)
            a.activation(wnorm[:, :], wss[:, :], ACT.Sqrt).then_inc(wnorm_ok, 1)
            act.wait_ge(wT_mm, 1)
            a.activation(wqk[:, 0, :], ps[:, 7, 0:2 * P], ACT.Copy).then_inc(wqk_hi, 1)
            a.activation(woT[:, :], ps[:, 7, 2 * P:3 * P], ACT.Copy).then_inc(woT_ok, 1)
            for p in range(2 * NCH):
                act.wait_ge(qk_mm, p + 1)
                if p >= 2:
                    act.wait_ge(ss_ok, p - 1)
                a.activation(sq[:, p % 2, :], ps[:, p, :], ACT.Square).then_inc(sq_ok, 1)
                qk = ps[:, p, :].rearrange("p (t w c) -> p t w c", t=2, w=2)
                a.activation(k_sb[:, 2 * p:2 * p + 2, :], qk[:, :, 1, :], ACT.Copy).then_inc(k_ok, 1)
                if p in (NCH, 2 * NCH - 1):
                    h = int(p > NCH)
                    act.wait_ge(ss_ok, NCH * (h + 1))
                    a.activation(ss[:, NCH * h:NCH * (h + 1)], ss[:, NCH * h:NCH * (h + 1)], ACT.Sqrt,
                                 scale=1.0 / HD).then_inc(nrm_ok, 1)
            act.preload_act_table_set(LN_EXP)
            for j in range(1, NLOW):
                n = min(FILL, nfill - j * FILL)
                act.wait_ge(ld_f[j], 16)
                a.activation(wf[:, j * FILL:j * FILL + n, 0, :], staged[j][:, 0:n, :], ACT.Copy).then_inc(fill_hi, 1)
            act.wait_ge(smax_ok, 1)
            a.activation(prob[:, :], sm[:, :], ACT.Exp, bias=smax[:, :], accum_out=ssum[:, :]).then_inc(exp_ok, 1)
            act.wait_ge(u_mm, 1)
            a.activation(u_sb[:, :], ps[:, 1, 0:P], ACT.Copy).then_inc(u_ok, 1)

            def rstds(var_sem, ln_sem, rs_sem, buf, bank):
                for c in range(NCH):
                    act.wait_ge(var_sem, c + 1)
                    a.activation(buf[:, cs(c)], ps[:, bank + c, :], ACT.Ln, bias=eps_ln[:, :]).then_inc(ln_sem, 1)
                    act.wait_ge(ln_sem, c + 1)
                    a.activation(buf[:, cs(c)], buf[:, cs(c)], ACT.Exp, scale=-0.5).then_inc(rs_sem, 1)

            for c in range(NCH):
                act.wait_ge(y1_mm, c + 1)
                act.wait_ge(fill_lo, 1)
                a.activation(bs1[:, cs(c)], ps[:, 4 + c, :], ACT.Square).then_inc(y1_sq, 1)
            act.wait_ge(fill_lo, NLOW)
            rstds(y1_var, y1_ln, y1_rs, bs2, 0)
            for c in range(NCH):
                act.wait_ge(rk_mm, c + 1)
                act.wait_ge(y1_var, c + 1)
                a.activation(bs1[:, cs(c)], ps[:, c, :], ACT.Tanh, scale=0.5).then_inc(th_ok, 1)
                a.activation(bs2[:, cs(c)], ps[:, 4 + c, :], ACT.Relu).then_inc(relu_ok, 1)
                act.wait_ge(relu_ok, c + 1)
                a.activation(bs3[:, cs(c)], bs2[:, cs(c)], ACT.Square).then_inc(k2_ok, 1)
            act.preload_act_table_set(LN_EXP)
            for c in range(NCH):
                act.wait_ge(y2_mm, c + 1)
                a.activation(bs1[:, cs(c)], ps[:, 4 + c, :], ACT.Square).then_inc(y2_sq, 1)
            rstds(y2_var, y2_ln, y2_rs, bs2, 0)
            for c in range(NCH):
                act.wait_ge(l1_mm, c + 1)
                a.activation(bs1[:, cs(c)], ps[:, 4 + c, :], ACT.Relu, bias=vec[:, BL1:BL1 + 1]).then_inc(l1_ok, 1)
            for c in range(NCH):
                act.wait_ge(l2_mm, c + 1)
                a.activation(bs3[:, cs(c)], ps[:, c, :], ACT.Tanh, bias=vec[:, BL2:BL2 + 1]).then_inc(l2_ok, 1)
            for c in range(NCH):
                act.wait_ge(f1_mm, c + 1)
                a.activation(bs1[:, cs(c)], ps[:, 4 + c, :], ACT.Relu, bias=vec[:, BF1:BF1 + 1]).then_inc(f1_ok, 1)
            act.preload_act_table_set(LN_EXP)
            for c in range(NCH):
                act.wait_ge(xt_mm, c + 1)
                a.activation(bxt[:, cs(c)], ps[:, c, :], ACT.Identity, bias=vec[:, BF2:BF2 + 1]).then_inc(xt_ok, 1)
            for c in range(NCH):
                act.wait_ge(d_mm, c + 1)
                a.activation(bs1[:, cs(c)], ps[:, 4 + c, :], ACT.Abs, bias=vec[:, B1:B1 + 1]).then_inc(d_abs, 1)
                act.wait_ge(d_abs, c + 1)
                a.activation(bs1[:, cs(c)], bs1[:, cs(c)], ACT.Exp, scale=-1.0).then_inc(d_exp, 1)
                act.wait_ge(d_exp, c + 1)
                a.activation(bs1[:, cs(c)], bs1[:, cs(c)], ACT.Ln, bias=1.0).then_inc(d_ln, 1)
            for c in range(NCH):
                act.wait_ge(c_mm, c + 1)
                a.activation(tr[0:96, 0, cs(c)], ps[0:96, c, :], ACT.Identity, bias=vec[0:96, B23:B23 + 1]).then_inc(c_hi, 1)
                a.activation(bs3[0:32, cs(c)], ps[96:128, c, :], ACT.Identity, bias=vec[96:128, B23:B23 + 1]).then_inc(b_ok, 1)

            def state_t(e):
                if e == 0:
                    act.wait_ge(d_ok, 2)
                if e == 2:
                    act.wait_ge(d_ok, NCH)
                if e == 4:
                    act.wait_ge(bc_mm, NCH)
                if e >= NB:
                    act.wait_ge(e_sum, e - NB + 1)
                for j, n in enumerate(group_states(e)):
                    a.activation(vbuf[e % NB][:, j, :], bdl[:, pair_tokens(e)], ACT.Exp,
                                 scale=amin[:, n:n + 1]).then_inc(e_t, 1)

            def state_da(e):
                on_pool = sum(v_on_pool(h, j) for h in range(e + 1) for j in range(GN))
                act.wait_ge(e_v, (e + 1) * GN - on_pool)
                if on_pool:
                    act.wait_ge(e_vp, on_pool)
                a.activation(vbuf[e % NB][:, :, :], vbuf[e % NB][:, :, :], ACT.Exp, scale=-1.0, bias=1.0).then_inc(e_da, 1)

            act.wait_ge(a_ok, 2)
            state_t(0)
            for e in range(NE):
                if e + 1 < NE:
                    state_t(e + 1)
                state_da(e)

            for c in range(NCH):
                act.wait_ge(e_sum, NG * (c // 2 + 1))
                act.wait_ge(e_p, NE)
                a.activation(bdl[:, cs(c)], ps[:, 4 + c, :], ACT.Square).then_inc(y3_sq, 1)
            rstds(y3_var, y3_ln, y3_rs, bs3, 0)

            def norm_sd(i, k):
                act.wait_ge(o_mv, 2 * i + k + 1)
                a.activation(rstd[:, k, :], mv[:, k, :, 1], ACT.Sqrt, scale=1.0 / P, bias=eps_ln[:, :]).then_inc(o_sd, 1)

            for i in range(NCH // 2):
                for stage, s in ((0, S1), (1, SH1), (2, SH2)):
                    for k in range(2):
                        for o in range(KH):
                            n = mtile(i, stage, k, o)
                            act.wait_ge(m_mm_, n + 1)
                            if n >= 2 * KH:
                                wait_low(act, n - 2 * KH)
                            a.activation(hbuf[k][:, o, :], ps[:, mbank(i, stage, k, o) % RING, :],
                                         ACT.Gelu if stage else ACT.Silu,
                                         scale=vec[:, s + o:s + o + 1]).then_inc(m_act, 1)
                    if i > 0 and stage == 0:
                        norm_sd(i - 1, 0)
                        norm_sd(i - 1, 1)
            act.preload_act_table(ACT.Sqrt)
            norm_sd(NCH // 2 - 1, 0)
            norm_sd(NCH // 2 - 1, 1)

        @block.vector
        def _(dve):
            v = nc.vector
            v.memset(ones[:, :], 1.0 / P).then_inc(o_ok, 1)
            dve.wait_ge(o_ok, 1)
            v.memset(ones_n[:, :], 1.0).then_inc(consts, 1)
            v.memset(full(x1r[:, :, 0:2]), 0.0).then_inc(consts, 1)
            v.memset(eps_ln[:, :], EPS_LN).then_inc(consts, 1)
            dve.wait_ge(ident_ok, 1)
            v.tensor_scalar(res_ident[:, :], ident[:, :], float(res_gain), None, ALU.mult).then_inc(consts, 1)
            v.tensor_scalar(centre[:, :], ident[:, :], 1.0 / P, None, ALU.subtract).then_inc(consts, 1)
            dve.wait_ge(consts, 5)
            v.tensor_copy(centre_r[:, :], centre[:, :]).then_inc(consts, 1)
            def x_high(c):
                dve.wait_ge(ld_x[c], 16)
                v.tensor_copy(xr[:, 0, cs(c)], bx2[:, cs(c)]).then_inc(x_hi, 1)

            def x_low(c):
                dve.wait_ge(x_hi, c + 1)
                v.tensor_tensor(xr[:, 1, cs(c)], bx2[:, cs(c)], full(xr[:, 0, cs(c)]), ALU.subtract).then_inc(x_lo_v, 1)

            x_high(0)
            dve.wait_ge(wnorm_ok, 5)
            v.tensor_scalar(wnorm[:, :], wnorm[:, :], float(np.sqrt(P) * EPS_MP), None, ALU.add).then_inc(wnorm_ok, 1)
            dve.wait_ge(wnorm_ok, 6)
            v.reciprocal(wnorm[:, :], wnorm[:, :]).then_inc(wnorm_ok, 1)
            dve.wait_ge(wnorm_ok, 7)
            dve.wait_ge(ld_vec, 16)
            v.tensor_scalar(wnorm[:, :], wnorm[:, :], gain, None, ALU.mult).then_inc(wnorm_ok, 1)
            dve.wait_ge(wnorm_ok, 8)
            for i in range(4):
                v.tensor_scalar(wa[:, i, :], wa[:, i, :], wnorm[:, i:i + 1], None, ALU.mult).then_inc(ws_ok, 1)
            x_high(1)
            x_low(0)
            dve.wait_ge(wqk_hi, 1)
            dve.wait_ge(woT_ok, 1)
            v.tensor_tensor(wqk[:, 1, :], ps[:, 7, 0:2 * P], full(wqk[:, 0, :]), ALU.subtract).then_inc(wqk_lo, 1)
            x_high(2)
            x_high(3)
            x_low(2)
            dve.wait_ge(ld_h0, 16)
            v.tensor_copy(h0hi[:, :], h0T[:, :]).then_inc(h0f_ok, 1)
            dve.wait_ge(h0f_ok, 1)
            v.tensor_copy(h0T[0:64, :], full(h0hi[0:64, :])).then_inc(h0f_ok, 1)
            v.tensor_tensor(h0T[64:96, :], h0T[64:96, :], full(h0hi[64:96, :]), ALU.subtract).then_inc(h0f_ok, 1)
            for p in range(2 * NCH):
                dve.wait_ge(sq_ok, p + 1)
                v.tensor_reduce(ss[:, p].rearrange("p a b h -> p (a b h)"),
                                sq[:, p % 2, :].rearrange("p (g e) -> p g e", e=HD), AX.X, ALU.add).then_inc(ss_ok, 1)
                if p in (NCH, 2 * NCH - 1):
                    h = int(p > NCH)
                    s = slice(h * NCH, (h + 1) * NCH)
                    dve.wait_ge(nrm_ok, h + 1)
                    v.tensor_scalar(ss[:, s], ss[:, s], EPS_MP, None, ALU.add).then_inc(nrm_step, 1)
                    dve.wait_ge(nrm_step, 3 * h + 1)
                    v.tensor_tensor(qkrec[:, s], ss[:, s, :, 0, :], ss[:, s, :, 1, :], ALU.mult).then_inc(nrm_step, 1)
                    dve.wait_ge(nrm_step, 3 * h + 2)
                    v.reciprocal(qkrec[:, s], qkrec[:, s]).then_inc(nrm_step, 1)
                    dve.wait_ge(nrm_step, 3 * h + 3)
                    dve.wait_ge(k_ok, NCH * (h + 1))
                    qh = ps[:, s, :].rearrange("p b (t w c) -> p (b t) w c", t=2, w=2)[:, :, 0, :]
                    r = qkrec[:, s].rearrange("p a b (h e) -> p (a b) h e", e=1).broadcast_to([P, NT // 2, HEADS, HD])
                    v.tensor_tensor(q_sb[:, h * NT // 2:(h + 1) * NT // 2, :].rearrange("p n (h e) -> p n h e", e=HD),
                                    qh.rearrange("p n (h e) -> p n h e", e=HD), r, ALU.mult).then_inc(qn_ok, 1)
            dve.wait_ge(ld_vec, 16)
            v.tensor_scalar(mu1[:, :], vec[:, MU_R:MU_R + 2], -1.0, 1.0, ALU.mult, ALU.add).then_inc(mu1_ok, 1)
            dve.wait_ge(mu1_ok, 1)
            dve.wait_ge(ld_w0, 16)
            for i, (j, sc) in enumerate(((0, vec[:, MU_R:MU_R + 1]), (0, mu1[:, 0:1]), (1, vec[:, MU_K:MU_K + 1]),
                                         (1, mu1[:, 1:2]))):
                v.tensor_scalar(w0f[:, i, :], w0raw[:, j, :], sc, None, ALU.mult).then_inc(w0f_ok, 1)
            v.tensor_copy(w0f[:, 4, :], w0raw[:, 2, :]).then_inc(w0f_ok, 1)
            dve.wait_ge(sc_mm, 1)
            dve.wait_ge(mask_ok, 2)
            v.scalar_tensor_tensor(sm[:, :], ps[:, 0, 0:P], float(1.0 / np.sqrt(T)), mask[:, :], ALU.mult,
                                   ALU.add).then_inc(sm_ok, 1)
            dve.wait_ge(sm_ok, 1)
            v.tensor_reduce(smax[:, :], sm[:, :], AX.X, ALU.max, negate=True).then_inc(smax_ok, 1)
            dve.wait_ge(exp_ok, 1)
            v.reciprocal(srec[:, :], ssum[:, :]).then_inc(srec_ok, 1)
            dve.wait_ge(srec_ok, 1)
            v.tensor_scalar(prob[:, :], prob[:, :], srec[:, :], None, ALU.mult).then_inc(prob_ok, 1)
            dve.wait_ge(m_mm, 1)
            v.scalar_tensor_tensor(mix[:, :], ps[:, 2, 0:P], float(out_gain), res_ident[:, :], ALU.mult,
                                   ALU.add).then_inc(mix_ok, 1)
            dve.wait_ge(mix_ok, 1)
            v.tensor_reduce(mrow[:, :], mix[:, :], AX.X, ALU.add).then_inc(mix_ok, 1)
            dve.wait_ge(mix_ok, 2)
            v.tensor_scalar(mrow[:, :], mrow[:, :], 1.0 / P, None, ALU.mult).then_inc(mix_ok, 1)
            dve.wait_ge(mix_ok, 3)
            v.tensor_scalar(mix[:, :], mix[:, :], mrow[:, :], None, ALU.subtract).then_inc(mix_ok, 1)
            dve.wait_ge(mix_ok, 4)
            v.tensor_copy(mixr[:, 0, :], mix[:, :]).then_inc(mix_ok, 1)
            dve.wait_ge(mix_ok, 5)
            v.tensor_tensor(mixr[:, 1, :], mix[:, :], full(mixr[:, 0, :]), ALU.subtract).then_inc(mix_ok, 1)
            dve.wait_ge(w0f_ok, 5)
            v.tensor_copy(w0[:, :, 0, :], w0f[:, :, :]).then_inc(w0_hi, 1)
            dve.wait_ge(w0_hi, 1)
            v.tensor_tensor(w0[:, :, 1, :], w0f[:, :, :], full(w0[:, :, 0, :]), ALU.subtract).then_inc(w0_lo, 1)
            dve.wait_ge(ld_w1, 16)
            v.tensor_copy(w1[:, :, 0, :], w1raw[:, :, :]).then_inc(w1_hi, 1)
            dve.wait_ge(w1_hi, 1)
            v.tensor_tensor(w1[:, :, 1, :], w1raw[:, :, :], full(w1[:, :, 0, :]), ALU.subtract).then_inc(w1_lo, 1)
            v.tensor_scalar(amin[:, :], amat[:, :], 0.0, None, ALU.min).then_inc(a_ok, 1)
            v.tensor_scalar(amax[:, :], amat[:, :], 0.0, None, ALU.max).then_inc(a_ok, 1)
            def split(full_sem, hi_sem, lo_sems, full_buf, dst, c):
                hi, lo = dst(c)
                dve.wait_ge(full_sem, c + 1)
                v.tensor_copy(hi, full_buf[:, cs(c)]).then_inc(hi_sem, 1)
                if c % 2 == 0:
                    dve.wait_ge(hi_sem, c + 1)
                    v.tensor_tensor(lo, full_buf[:, cs(c)], full(hi), ALU.subtract).then_inc(lo_sems[0], 1)

            for c in range(NCH):
                dve.wait_ge(y1_rs, c + 1)
                v.tensor_tensor(bx1[:, cs(c)], ps[:, 4 + c, :], bs2[:, cs(c)], ALU.mult).then_inc(x1_ok, 1)
                split(x1_ok, x1_hi, x1_lo, bx1, lambda c: parts(x1r, c, 2), c)
            def lows_max(j):
                n = min(FILL, nfill - j * FILL)
                dve.wait_ge(fill_lo, NLOW)
                v.tensor_reduce(low_max[:, j:j + 1], full(wf[:, j * FILL:j * FILL + n, 1, :]), AX.XY, ALU.max,
                                apply_absolute_value=True).then_inc(low_ok, 1)

            lows_max(0)
            for c in range(NCH):
                split(k2_ok, k2_hi, k2_lo, bs3, lambda c: parts(tr, c), c)
            for c in range(NCH):
                dve.wait_ge(v_mm, c + 1)
                dve.wait_ge(th_ok, c + 1)
                v.scalar_tensor_tensor(bs1[:, cs(c)], bs1[:, cs(c)], 1.0, ps[:, c, :], ALU.add,
                                       ALU.mult).then_inc(p_ok, 1)
                dve.wait_ge(p_ok, c + 1)
                wait_split(dve, k2_lo, c)
                v.scalar_tensor_tensor(bs3[:, cs(c)], bs1[:, cs(c)], 0.5, bx1[:, cs(c)], ALU.mult,
                                       ALU.add).then_inc(y2_ok, 1)
            for j in range(1, NLOW):
                lows_max(j)
            for c in range(NCH):
                dve.wait_ge(y2_rs, c + 1)
                v.tensor_tensor(bx2[:, cs(c)], ps[:, 4 + c, :], bs2[:, cs(c)], ALU.mult).then_inc(x2_ok, 1)
                split(x2_ok, x2_hi, x2_lo, bx2, lambda c: parts(xr, c), c)
            for c in range(NCH):
                split(l1_ok, l1_hi, l1_lo, bs1, lambda c: parts(tr, c), c)
            for c in range(NCH):
                split(l2_ok, l2_hi, l2_lo, bs3, lambda c: parts(lr, c), c)
            for c in range(NCH):
                split(f1_ok, f1_hi, f1_lo, bs1, lambda c: parts(tr, c), c)
            for c in range(NCH):
                split(xt_ok, xt_hi, xt_lo, bxt, lambda c: parts(x1r, c, 2), c)
            dve.wait_ge(low_mm, 1)
            v.tensor_reduce(low_any[:, :], ps[:, 7, 0:NLOW], AX.X, ALU.add).then_inc(low_flag, 1)
            for c in range(NCH):
                dve.wait_ge(d_abs, c + 1)
                v.tensor_scalar(bs2[:, cs(c)], ps[:, 4 + c, :], vec[:, B1:B1 + 1], 0.0, ALU.add,
                                ALU.max).then_inc(d_max, 1)
            for c in range(NCH):
                dve.wait_ge(c_hi, c + 1)
                dve.wait_ge(b_ok, c + 1)
                v.scalar_tensor_tensor(tr[32:64, 0, cs(c)], ps[32:64, c, :], vec[32:64, B23:B23 + 1],
                                       full(tr[32:64, 0, cs(c)]), ALU.add, ALU.subtract).then_inc(c_lo, 1)
                v.scalar_tensor_tensor(bs3[0:32, cs(c)], ps[0:32, c, :], vec[0:32, B23:B23 + 1], bs3[0:32, cs(c)],
                                       ALU.add, ALU.mult).then_inc(bc_ok, 1)
            for c in range(NCH):
                dve.wait_ge(g_ok, c + 1)
                dve.wait_ge(bc_mm, c + 1)
                v.tensor_tensor(bxt[:, cs(c)], bxt[:, cs(c)], ps[:, 4 + c, :], ALU.mult).then_inc(o2_ok, 1)

            def state_v(e):
                for j, n in enumerate(group_states(e)):
                    if not v_on_pool(e, j):
                        dve.wait_ge(e_t, GN * e + j + 1)
                        v.scalar_tensor_tensor(vbuf[e % NB][:, j, :], bdl[:, pair_tokens(e)], amax[:, n:n + 1],
                                               vbuf[e % NB][:, j, :], ALU.mult, ALU.add).then_inc(e_v, 1)

            def state_p(e):
                dve.wait_ge(e_da, e + 1)
                dve.wait_ge(e_ch, e + 1)
                v.tensor_tensor(vbuf[e % NB].rearrange("p j (k n) -> p (j k) n", n=CH),
                                vbuf[e % NB].rearrange("p j (k n) -> p (j k) n", n=CH), ps[:, 0:4, :],
                                ALU.mult).then_inc(e_p, 1)

            state_v(0)
            for e in range(NE):
                if e + 1 < NE:
                    state_v(e + 1)
                state_p(e)

            for c in range(NCH):
                dve.wait_ge(y3_rs, c + 1)
                v.tensor_tensor(bx2[:, cs(c)], ps[:, 4 + c, :], bs3[:, cs(c)], ALU.mult).then_inc(x3_ok, 1)
                split(x3_ok, x3_hi, x3_lo, bx2, lambda c: parts(lr, c), c)

            def mlp_tiles(i, stage, k):
                for o in range(KH):
                    n = mtile(i, stage, k, o)
                    sl = slot[(2 * stage + k) % 3]
                    dve.wait_ge(m_act, n + 1)
                    if stage == 0:
                        v.scalar_tensor_tensor(hbuf[k][:, o, :], ps[:, (mbank(i, stage, k, o) + 1) % RING, :],
                                               vec[:, S2 + o:S2 + o + 1], hbuf[k][:, o, :], ALU.mult,
                                               ALU.mult).then_inc(m_full, 1)
                        dve.wait_ge(m_full, 2 * KH * i + k * KH + o + 1)
                    v.tensor_copy(sl[:, 0, o, :], hbuf[k][:, o, :]).then_inc(m_hi, 1)
                    if low_on_dve(n):
                        dve.wait_ge(m_hi, n + 1)
                        v.tensor_tensor(sl[:, 1, o, :], hbuf[k][:, o, :], full(sl[:, 0, o, :]),
                                        ALU.subtract).then_inc(m_lo_v, 1)

            def residual(i, k):
                dve.wait_ge(o_mm, 2 * i + k + 1)
                v.scalar_tensor_tensor(bs3[:, k * CH:(k + 1) * CH], ps[:, RING + k, :], vec[:, S3:S3 + 1],
                                       bx2[:, cs(2 * i + k)], ALU.mult, ALU.add).then_inc(o_y, 1)

            def norm_stats(i, k):
                dve.wait_ge(o_T, 2 * i + k + 1)
                yt = ps[:, RING + k, :].rearrange("p (n c) -> p n c", c=P)
                for n in range(TPC):
                    v.bn_stats(stats[:, k, n, :], yt[:, n, :]).then_inc(o_st, 1)
                dve.wait_ge(o_st, (2 * i + k + 1) * TPC)
                me, mo, m2e, m2o = [stats[:, k, :, j] for j in (1, 4, 2, 5)]
                v.tensor_tensor(mv[:, k, :, 0], me, mo, ALU.add).then_inc(o_stat, 1)
                v.tensor_tensor(mdif[:, k, :], me, mo, ALU.subtract).then_inc(o_stat, 1)
                v.tensor_tensor(mv[:, k, :, 1], m2e, m2o, ALU.add).then_inc(o_stat, 1)
                dve.wait_ge(o_stat, (2 * i + k) * 5 + 2)
                v.tensor_tensor(mdif[:, k, :], mdif[:, k, :], mdif[:, k, :], ALU.mult).then_inc(o_stat, 1)
                dve.wait_ge(o_stat, (2 * i + k) * 5 + 1)
                v.tensor_scalar(mv[:, k, :, 0], mv[:, k, :, 0], 0.5, None, ALU.mult).then_inc(o_stat, 1)
                dve.wait_ge(o_stat, (2 * i + k) * 5 + 4)
                v.scalar_tensor_tensor(mv[:, k, :, 1], mdif[:, k, :], P / 4.0, mv[:, k, :, 1], ALU.mult,
                                       ALU.add).then_inc(o_mv, 1)

            def normalise(i, k):
                dve.wait_ge(o_sd, 2 * i + k + 1)
                v.reciprocal(rstd[:, k, :], rstd[:, k, :]).then_inc(o_rs, 1)
                dve.wait_ge(o_rs, 2 * i + k + 1)
                dve.wait_ge(o_stat, (2 * i + k) * 5 + 5)
                yt = ps[:, RING + k, :].rearrange("p (n c) -> p n c", c=P)
                for n in range(TPC):
                    v.tensor_scalar(bdl[:, bass.ds((2 * i + k) * CH + n * P, P)], yt[:, n, :],
                                    mv[:, k, n, 0:1], rstd[:, k, n:n + 1], ALU.subtract,
                                    ALU.mult).then_inc(o_ok, 1)

            for i in range(NCH // 2):
                for stage in range(3):
                    for k in range(2):
                        mlp_tiles(i, stage, k)
                        if i > 0 and stage == 0:
                            residual(i - 1, k)
                    if i > 0 and stage == 0:
                        for k in range(2):
                            norm_stats(i - 1, k)
                        for k in range(2):
                            normalise(i - 1, k)
            last = NCH // 2 - 1
            residual(last, 0)
            norm_stats(last, 0)
            normalise(last, 0)
            residual(last, 1)
            norm_stats(last, 1)
            normalise(last, 1)

        @block.tensor
        def _(pe):
            m = nc.tensor
            pe.wait_ge(ident_ok, 1)
            pe.wait_ge(ws_ok, 3)
            for i in range(3):
                last = m.transpose(ps[:, 7, i * P:(i + 1) * P], wa[:, i, :], ident[:, :])
            last.then_inc(wT_mm, 1)
            pe.wait_ge(wqk_lo, 1)
            for p in range(2 * NCH):
                c = p // 2
                if c % 2:
                    pe.wait_ge(x_lo_p, c // 2 + 1)
                else:
                    pe.wait_ge(x_lo_v, c // 2 + 1)
                if p == 2 * NCH - 1:
                    pe.wait_ge(woT_ok, 1)
                for h in range(2):
                    tok = slice((2 * p + h) * P, (2 * p + h + 1) * P)
                    last = mm3(ps[:, p, h * 2 * P:(h + 1) * 2 * P], (xr[:, 0, tok], xr[:, 1, tok]),
                               (wqk[:, 0, :], wqk[:, 1, :]))
                last.then_inc(qk_mm, 1)
            for n in range(NT):
                if n % (NT // 2) == 0:
                    pe.wait_ge(qn_ok, 2 * n // NT + 1)
                pe.wait_ge(k_ok, n // 2 + 1)
                last = m.matmul(ps[:, 0, 0:P], q_sb[:, n, :], k_sb[:, n, :], start=(n == 0), stop=(n == NT - 1))
            last.then_inc(sc_mm, 1)
            pe.wait_ge(prob_ok, 1)
            pe.wait_ge(woT_ok, 1)
            m.matmul(ps[:, 1, 0:P], prob[:, :], woT[:, :], start=True, stop=True).then_inc(u_mm, 1)
            pe.wait_ge(u_ok, 1)
            pe.wait_ge(ws_ok, 4)
            m.matmul(ps[:, 2, 0:P], wa[:, 3, :], u_sb[:, :], start=True, stop=True).then_inc(m_mm, 1)

            def over_channels(src_sem, dst_sem, w, buf, bank):
                for c in range(NCH):
                    pe.wait_ge(src_sem, c + 1)
                    m.matmul(ps[:, bank + c, :], w[:, :], buf[:, cs(c)], start=True, stop=True).then_inc(dst_sem, 1)

            pe.wait_ge(mix_ok, 6)
            for c in range(NCH):
                m3 = mm3(ps[:, 4 + c, :], (mixr[:, 0, :], mixr[:, 1, :]), parts(xr, c))
                m3.then_inc(y1_mm, 1)
            pe.wait_ge(consts, 6)
            pe.wait_ge(o_ok, 1)
            over_channels(y1_sq, y1_var, ones, bs1, 0)
            pe.wait_ge(w0_lo, 1)
            for c in range(NCH):
                wait_split(pe, x1_lo, c)
                for bank, w in ((c, 0), (4 + c, 2)):
                    mm3(ps[:, bank, :], pair(w0, w), parts(x1r, c, 2), stop=False)
                    last = mm3(ps[:, bank, :], pair(w0, w + 1), parts(x1r, c, 1), start=False)
                last.then_inc(rk_mm, 1)
            for c in range(NCH):
                wait_split(pe, k2_lo, c)
                mm3(ps[:, c, :], pair(w0, 4), parts(tr, c)).then_inc(v_mm, 1)
            over_channels(y2_ok, y2_mm, centre, bs3, 4)
            over_channels(y2_sq, y2_var, ones, bs1, 0)
            pe.wait_ge(w1_lo, 1)
            for c in range(NCH):
                wait_split(pe, x2_lo, c)
                mm3(ps[:, 4 + c, :], pair(w1, 0), parts(xr, c)).then_inc(l1_mm, 1)
            for c in range(NCH):
                wait_split(pe, l1_lo, c)
                mm3(ps[:, c, :], pair(w1, 1), parts(tr, c)).then_inc(l2_mm, 1)
            for c in range(NCH):
                mm3(ps[:, 4 + c, :], pair(w1, 2), parts(xr, c), stop=False)
                wait_split(pe, l2_lo, c)
                mm3(ps[:, 4 + c, :], pair(w1, 3), parts(lr, c), start=False).then_inc(f1_mm, 1)
            for c in range(NCH):
                wait_split(pe, f1_lo, c)
                mm3(ps[:, c, :], pair(w1, 4), parts(tr, c)).then_inc(xt_mm, 1)
            pe.wait_ge(low_ok, NLOW)
            pe.wait_ge(f1_ok, NCH)
            m.matmul(ps[:, 7, 0:NLOW], ones[:, :], low_max[:, :], start=True, stop=True).then_inc(low_mm, 1)
            for c in range(NCH):
                wait_split(pe, xt_lo, c)
                if c == 3:
                    pe.wait_ge(low_flag, 1)
                mm3(ps[:, 4 + c, :], pair(w1, 5), parts(x1r, c, 2)).then_inc(d_mm, 1)
            for c in range(NCH):
                mm3(ps[:, c, :], pair(w1, 6), parts(x1r, c, 2)).then_inc(c_mm, 1)
            for c in range(NCH):
                pe.wait_ge(bc_ok, c + 1)
                pe.wait_ge(d_abs, c + 1)
                pe.wait_ge(d_max, c + 1)
                m.matmul(ps[:, 4 + c, :], ones_n[:, :], bs3[0:32, cs(c)], start=True, stop=True).then_inc(bc_mm, 1)

            def state_ch(e):
                for j, n in enumerate(group_states(e)):
                    for k in range(2):
                        last = m.matmul(ps[:, 2 * j + k, :], h0sel[:, n, :], tr[0:96, 0, cs(2 * (e // NG) + k)],
                                        start=True, stop=True)
                last.then_inc(e_ch, 1)

            def state_first(c):
                pe.wait_ge(o2_ok, c + 1)
                for h in range(2):
                    m.matmul(ps[:, 4 + c, :], centre_r[:, :], xr[:, h, cs(c)], start=(h == 0), stop=False)
                m.matmul(ps[:, 4 + c, :], centre[:, :], bxt[:, cs(c)], start=False, stop=False).then_inc(e_first, 1)

            def state_sum(e):
                if e % 2 == 0:
                    pe.wait_ge(e_add, e // 2 + 1)
                for j in range(1 if e % 2 == 0 else GN):
                    for k in range(2):
                        last = m.matmul(ps[:, 4 + 2 * (e // NG) + k, :], centre[:, :],
                                        vbuf[e % NB][:, j, k * CH:(k + 1) * CH], start=False,
                                        stop=(e % NG == NG - 1 and j == GN - 1))
                last.then_inc(e_sum, 1)

            pe.wait_ge(h0sel_ok, 3)
            pe.wait_ge(c_lo, NCH)
            pe.wait_ge(bc_ok, NCH)
            state_ch(0)
            for c in range(NCH):
                state_first(c)
            for e in range(NE):
                pe.wait_ge(e_p, e + 1)
                if e + 1 < NE:
                    state_ch(e + 1)
                if e:
                    state_sum(e - 1)
            state_sum(NE - 1)
            over_channels(y3_sq, y3_var, ones, bdl, 0)

            def product(low_weights, dst, f, wo, x, start=True, stop=True):
                m.matmul(dst, wf[:, f, 0, wo], x[0], start=start, stop=False)
                last = m.matmul(dst, wf[:, f, 0, wo], x[1], start=False, stop=stop and not low_weights)
                if low_weights:
                    last = m.matmul(dst, wf[:, f, 1, wo], x[0], start=False, stop=stop)
                return last

            def gated(low_weights, i, k):
                wait_split(pe, x3_lo, 2 * i + k)
                for o in range(KH):
                    wo = slice(o * P, (o + 1) * P)
                    for f in range(2):
                        b = mbank(i, 0, k, o) + f
                        wait_bank(pe, b)
                        if b < 4:
                            pe.wait_ge(y3_ln, b + 1)
                        elif b < RING:
                            pe.wait_ge(x3_ok, b - 3)
                        last = product(low_weights, ps[:, b % RING, :], f, wo, parts(lr, 2 * i + k))
                    last.then_inc(m_mm_, 1)

            def hidden(low_weights, i, stage, k, tiles):
                src = slot[(2 * stage - 2 + k) % 3]
                for o in tiles:
                    b = mbank(i, stage, k, o)
                    wait_bank(pe, b)
                    for kk in range(KH):
                        if o == 0:
                            wait_low(pe, mtile(i, stage - 1, k, kk))
                        last = product(low_weights, ps[:, b % RING, :], 3 + (stage - 1) * KH + kk,
                                       slice(o * P, (o + 1) * P), (src[:, 0, kk, :], src[:, 1, kk, :]),
                                       start=(kk == 0), stop=(kk == KH - 1))
                    last.then_inc(m_mm_, 1)

            def output(low_weights, i, k):
                src = slot[(4 + k) % 3]
                if i > 0:
                    pe.wait_ge(o_ok, (2 * i - 1 + k) * TPC + 1)
                for kk in range(KH):
                    wait_low(pe, mtile(i, 2, k, kk))
                    last = product(low_weights, ps[:, RING + k, :], 2, slice(kk * P, (kk + 1) * P),
                                   (src[:, 0, kk, :], src[:, 1, kk, :]), start=(kk == 0), stop=(kk == KH - 1))
                last.then_inc(o_mm, 1)

            def token_major(i, k):
                pe.wait_ge(o_y, 2 * i + k + 1)
                for n in range(TPC):
                    last = m.transpose(ps[:, RING + k, n * P:(n + 1) * P],
                                       bs3[:, k * CH + n * P:k * CH + (n + 1) * P], ident[:, :])
                last.then_inc(o_T, 1)

            def mlp(low_weights):
                for i in range(NCH // 2):
                    for k in range(2):
                        gated(low_weights, i, k)
                        if i > 0:
                            output(low_weights, i - 1, k)
                    if i > 0:
                        hidden(low_weights, i, 1, 0, range(2))
                        token_major(i - 1, 0)
                        token_major(i - 1, 1)
                        hidden(low_weights, i, 1, 0, range(2, KH))
                    else:
                        hidden(low_weights, i, 1, 0, range(KH))
                    hidden(low_weights, i, 1, 1, range(KH))
                    for k in range(2):
                        hidden(low_weights, i, 2, k, range(KH))
                for k in range(2):
                    output(low_weights, NCH // 2 - 1, k)
                    token_major(NCH // 2 - 1, k)

            pe.wait_ge(low_flag, 1)
            has_low = pe.value_load(low_any[0:1, 0:1].bitcast(mybir.dt.int32))
            with pe.If(has_low):
                mlp(True)
            with pe.Else():
                mlp(False)


def layout(d):
    import numpy as _np

    def columns(name):
        a = d[name]
        return a.reshape(-1, P).T

    small = _np.zeros((P, NSMALL), _np.float32)
    for name, col in (("L0_ffn_mu_r", MU_R), ("L0_ffn_mu_k", MU_K), ("L1_attn_bl1", BL1), ("L1_attn_bl2", BL2),
                      ("L1_attn_bf1", BF1), ("L1_attn_bf2", BF2), ("L1_attn_b1", B1), ("L1_ffn_w3_s", S3),
                      ("L1_ffn_w1_s", S1), ("L1_ffn_w2_s", S2), ("L1_ffn_h1_s", SH1), ("L1_ffn_h2_s", SH2)):
        c = columns(name)
        small[:, col:col + c.shape[1]] = c
    for r in (0, 32, 64):
        small[r:r + NS, B23] = d["L1_attn_b3"]
    small[96:96 + NS, B23] = d["L1_attn_b2"]
    small[:, A_COL:A_COL + NS] = d["L1_attn_A"]
    small[:, GAIN_COL] = d["L0_attn_gain"]
    w_ssm = _np.zeros((P, 7, P), _np.float32)
    for i, w in enumerate((d["L1_attn_Wl1"], d["L1_attn_Wl2"], d["L1_attn_Wf1"][:P], d["L1_attn_Wf1"][P:],
                           d["L1_attn_Wf2"], d["L1_attn_W1"])):
        w_ssm[:, i] = w
    for r in (0, 32, 64):
        w_ssm[:, 6, r:r + NS] = d["L1_attn_W3"]
    w_ssm[:, 6, 96:96 + NS] = d["L1_attn_W2"]
    state = _np.zeros((96, P), _np.float32)
    for r in (0, 32, 64):
        state[r:r + NS] = d["L1_attn_state_init"][0].T
    hid = d["L1_ffn_w1_w"].shape[0]

    def blocks(w):
        return w.T.reshape(-1, P, w.shape[0]).transpose(1, 0, 2)

    w_mlp = _np.concatenate([blocks(d["L1_ffn_w1_w"]), blocks(d["L1_ffn_w2_w"]),
                             blocks(d["L1_ffn_w3_w"]).reshape(P, 1, hid), blocks(d["L1_ffn_h1_w"]),
                             blocks(d["L1_ffn_h2_w"])], axis=1)
    return {
        "x": d["L0_attn_query"].reshape(-1, P).T,
        "w_attn": _np.stack([d["L0_attn_" + n] for n in ("w_q", "w_k", "w_o", "w_v")], axis=1),
        "small": small,
        "w_ffn": _np.stack([d["L0_ffn_" + n].T for n in ("W_r", "W_k", "W_v")], axis=1),
        "w_ssm": w_ssm,
        "state": state,
        "w_mlp": w_mlp,
    }


def kernel(**inputs):
    import numpy as _np
    import concourse.bacc as _bacc
    from concourse import mybir as _mybir
    from concourse.bass_utils import run_bass_kernel_spmd as _run

    nc = _bacc.Bacc("TRN2", target_bir_lowering=False, num_devices=1)
    arrays, tensors = {}, {}
    for name, a in layout({k: _np.asarray(a) for k, a in inputs.items()}).items():
        a = _np.ascontiguousarray(a)
        arrays[f"in_{name}_dram"] = a
        tensors[name] = nc.dram_tensor(f"in_{name}_dram", a.shape, _mybir.dt.from_np(a.dtype),
                                       kind="ExternalInput").ap()
    shape = inputs["L0_attn_query"].shape
    out = nc.dram_tensor("out_0_dram", tuple(shape), _mybir.dt.float32, kind="ExternalOutput").ap()
    build(nc, tensors, out)
    r = _run(nc, [arrays], core_ids=[0])
    return r.results[0]["out_0_dram"]
```

```python
from contextlib import ExitStack

import numpy as np
import concourse.bass as bass
from concourse import mybir

F32 = mybir.dt.float32
F32R = mybir.dt.float32r
ALU = mybir.AluOpType
ACT = mybir.ActivationFunctionType
AX = mybir.AxisListType

P = 128
CH = 512
HEADS = 16
HD = P // HEADS
NS = 16
GN = 2
NG = NS // GN
EPS_MP = 1e-4
EPS_LN = 1e-5
LN_EXP = "natural_log_exp_and_others"

LV = 288
MU_R, MU_K, BL1, BL2, BF1, BF2, B1, S3, S1, S2, SH1, SH2, B23 = 0, 1, 2, 3, 4, 5, 6, 7, 8, 12, 16, 20, 24
A_COL = 25
GAIN_COL = A_COL + NS
NSMALL = GAIN_COL + 1


def build(nc, t, out):
    x_d = t["x"]
    out_d = out.rearrange("a (n p) c -> (a p) n c", p=P)
    T = x_d.shape[1]
    NCH = T // CH
    NT = T // P
    TPC = CH // P
    HID = t["w_mlp"].shape[2]
    KH = HID // P
    res_gain = 1.0 + 0.5 / np.sqrt(0.5)
    out_gain = 0.5 / np.sqrt(0.5)

    ctx = ExitStack()
    with ctx:
        def sb(name, shape, dt=F32):
            return ctx.enter_context(nc.sbuf_tensor(name, shape, dt))

        def sem(name):
            return ctx.enter_context(nc.semaphore(name))

        ps = ctx.enter_context(nc.psum_tensor("ps", [P, 8, CH], F32))

        ident = sb("ident", [P, P])
        ones = sb("ones", [P, P])
        centre = sb("centre", [P, P])
        centre_r = sb("centre_r", [P, P], F32R)
        ones_n = sb("ones_n", [32, P])
        res_centre = sb("res_centre", [P, P])
        mask = sb("mask", [P, P])
        vec = sb("vec", [P, NSMALL])
        amat, gain = vec[:, A_COL:A_COL + NS], vec[:, GAIN_COL:GAIN_COL + 1]
        mu1 = sb("mu1", [P, 2])
        wa = sb("wa", [P, 4, P])
        wss = sb("wss", [P, 4])
        wnorm = sb("wnorm", [P, 4])

        wqk = sb("wqk", [P, 2, 2 * P], F32R)
        woT = sb("woT", [P, P])
        sm = sb("sm", [P, P])
        smax = sb("smax", [P, 1])
        ssum = sb("ssum", [P, 1])
        srec = sb("srec", [P, 1])
        prob = sb("prob", [P, P])
        u_sb = sb("u_sb", [P, P])
        mix = sb("mix", [P, P])
        mrow = sb("mrow", [P, 1])
        mixr = sb("mixr", [P, 2, P], F32R)
        w0raw = sb("w0raw", [P, 3, P])
        w0f = sb("w0f", [P, 5, P])
        w0 = sb("w0", [P, 5, 2, P], F32R)
        w1 = sb("w1", [P, 7, 2, P], F32R)
        h0T = sb("h0T", [96, P])
        h0hi = sb("h0hi", [96, P], F32R)
        eps_ln = sb("eps_ln", [P, 1])
        h0sel = sb("h0sel", [96, NS, P], F32R)
        amin = sb("amin", [P, NS])
        amax = sb("amax", [P, NS])
        nfill = 3 + 2 * KH
        NLOW = (nfill + 3) // 4
        wf = sb("wf", [P, nfill, 2, HID], F32R)
        ss = sb("ss", [P, NCH * 2, 2, 2, HEADS])
        qkrec = sb("qkrec", [P, NCH * 2, 2, HEADS])
        stats = sb("stats", [P, 2, TPC, 6])
        mdif = sb("mdif", [P, 2, TPC])
        mv = sb("mv", [P, 2, TPC, 2])
        rstd = sb("rstd", [P, 2, TPC])
        xr = sb("xr", [P, 2, T], F32R)
        x1r = sb("x1r", [P, 2, T + 2], F32R)
        tr = sb("tr", [P, 2, T], F32R)
        lr = sb("lr", [P, 2, T], F32R)
        bx1, bs1, bs2, bs3, bx2, bxt, bdl = [sb(n, [P, T]) for n in ("bx1", "bs1", "bs2", "bs3", "bx2", "bxt", "bdl")]

        q_sb = bx1[:, :].rearrange("p (n c) -> p n c", c=P)
        k_sb = bxt[:, :].rearrange("p (n c) -> p n c", c=P)
        sq = bdl[:, :].rearrange("p (n c) -> p n c", c=CH)
        w1raw = bdl[:, T // 2:T // 2 + 7 * P].rearrange("p (w c) -> p w c", c=P)
        FILL = T // HID
        staged = [b[:, :].rearrange("p (f c) -> p f c", c=HID) for b in (bs1, bs2, bs3)]
        slot = [xr[:, :, :].rearrange("p s (k n) -> p s k n", k=KH),
                x1r[:, :, 2:].rearrange("p s (k n) -> p s k n", k=KH),
                tr[:, :, :].rearrange("p s (k n) -> p s k n", k=KH)]
        vbuf = [b[:, :].rearrange("p (k n) -> p k n", k=GN) for b in (bx1, bx2, bs1, bs2, bs3)]
        NB = len(vbuf)
        y3sq = [b[:, c * CH:(c + 1) * CH] for b in (bxt, bdl) for c in (2, 3)]
        zmax = bxt[:, 0:2 * CH]
        hbuf = [b[:, :].rearrange("p (k n) -> p k n", k=KH) for b in (bs1, bs2)]
        low_max = sb("low_max", [P, NLOW])
        low_any = sb("low_any", [P, 1])

        ld_x = [sem(f"ld_x{c}") for c in range(NCH)]
        ld_f = [sem(f"ld_f{j}") for j in range(NLOW)]
        ld_wa, ld_vec, ld_w0, ld_w1, ld_h0, stored = [
            sem(n) for n in ("ld_wa", "ld_vec", "ld_w0", "ld_w1", "ld_h0", "stored")]
        pads, ident_ok, mask_ok, consts = [sem(n) for n in ("pads", "ident_ok", "mask_ok", "consts")]
        wnorm_ok, wo_step, ws_ok, wT_mm, wqk_hi, wqk_lo, woT_ok = [
            sem(n) for n in ("wnorm_ok", "wo_step", "ws_ok", "wT_mm", "wqk_hi",
                             "wqk_lo", "woT_ok")]
        mu1_ok, w0f_ok, w0_hi, w0_lo, w1_hi, w1_lo = [
            sem(n) for n in ("mu1_ok", "w0f_ok", "w0_hi", "w0_lo", "w1_hi", "w1_lo")]
        h0f_ok, h0sel_ok, a_ok = [
            sem(n) for n in ("h0f_ok", "h0sel_ok", "a_ok")]
        fill_hi0, fill_hi, fill_lo = [sem(n) for n in ("fill_hi0", "fill_hi", "fill_lo")]
        x_hi, x_lo_v, x_lo_p, qk_mm, sq_ok, k_ok, ss_ok, nrm_ok, nrm_step, qn_ok = [
            sem(n) for n in ("x_hi", "x_lo_dve", "x_lo_pool", "qk_mm", "sq_ok", "k_ok", "ss_ok", "nrm_ok", "nrm_step",
                             "qn_ok")]
        sc_mm, sm_ok, smax_ok, exp_ok, srec_ok, prob_ok, u_mm, u_ok, m_mm, mix_ok = [
            sem(n) for n in ("sc_mm", "sm_ok", "smax_ok", "exp_ok", "srec_ok", "prob_ok", "u_mm", "u_ok", "m_mm",
                             "mix_ok")]
        y1_mm, y1_sq, y1_var, y1_ln, y1_rs, x1_ok, x1_hi = [
            sem(n) for n in ("y1_mm", "y1_sq", "y1_var", "y1_ln", "y1_rs", "x1_ok", "x1_hi")]
        rk_mm, th_ok, relu_ok, k2_ok, k2_hi, v_mm, p_ok, y2_ok, y2_mm, y2_sq, y2_var, y2_ln, y2_rs = [
            sem(n) for n in ("rk_mm", "th_ok", "relu_ok", "k2_ok", "k2_hi", "v_mm", "p_ok", "y2_ok", "y2_mm", "y2_sq",
                             "y2_var", "y2_ln", "y2_rs")]
        x2_ok, x2_hi, l1_mm, l1_ok, l1_hi, l2_mm, l2_ok, l2_hi = [
            sem(n) for n in ("x2_ok", "x2_hi", "l1_mm", "l1_ok", "l1_hi", "l2_mm", "l2_ok", "l2_hi")]
        f1_mm, f1_ok, f1_hi, xt_mm, xt_ok, xt_hi, d_mm, d_abs, d_exp, d_ln, d_max, d_ok = [
            sem(n) for n in ("f1_mm", "f1_ok", "f1_hi", "xt_mm", "xt_ok", "xt_hi", "d_mm", "d_abs", "d_exp", "d_ln",
                             "d_max", "d_ok")]
        c_mm, c_hi, c_lo, b_ok, bc_ok, bc_mm, g_ok, o2_ok = [
            sem(n) for n in ("c_mm", "c_hi", "c_lo", "b_ok", "bc_ok", "bc_mm", "g_ok", "o2_ok")]
        e_first, e_t, e_v, e_zp, e_vp, e_da, e_ch, e_p, e_add, e_add_last, e_sum = [
            sem(n) for n in ("e_first", "e_t", "e_v_dve", "e_z_pool", "e_v_pool", "e_da", "e_ch", "e_p", "e_add",
                             "e_add_last", "e_sum")]
        y3_sq, y3_var, y3_ln, y3_rs, x3_ok, x3_hi = [
            sem(n) for n in ("y3_sq", "y3_var", "y3_ln", "y3_rs", "x3_ok", "x3_hi")]
        low_ok, low_ok_v, low_mm, low_flag = [sem(n) for n in ("low_ok_act", "low_ok_dve", "low_mm", "low_flag")]
        x1_lo, k2_lo, x2_lo, l1_lo, l2_lo, f1_lo, xt_lo, x3_lo = [
            (sem(n + "_dve"), sem(n + "_pool"))
            for n in ("x1_lo", "k2_lo", "x2_lo", "l1_lo", "l2_lo", "f1_lo", "xt_lo", "x3_lo")]
        mlp_mm, m_act, m_full, m_hi, m_lo_p, m_lo_v = [
            sem(n) for n in ("mlp_mm", "mlp_act", "mlp_full", "mlp_hi", "mlp_lo_pool", "mlp_lo_dve")]
        o_mm, o_y, o_T, o_st, o_stat, o_mv, o_sd, o_rs, o_ok = [
            sem(n) for n in ("o_mm", "o_y", "o_T", "o_st", "o_stat", "o_mv", "o_sd", "o_rs", "o_ok")]

        def cs(c):
            return slice(c * CH, (c + 1) * CH)

        def full(b):
            return b.bitcast(F32)

        def mm3(dst, w, xs, start=True, stop=True):
            nc.tensor.matmul(dst, w[0], xs[0], start=start, stop=False)
            nc.tensor.matmul(dst, w[0], xs[1], start=False, stop=False)
            return nc.tensor.matmul(dst, w[1], xs[0], start=False, stop=stop)

        def pair(w, *i):
            return w[(slice(None), *i, 0)], w[(slice(None), *i, 1)]

        def parts(b, c, shift=0):
            s = slice(c * CH + shift, (c + 1) * CH + shift)
            return b[:, 0, s], b[:, 1, s]

        def wait_split(eng, lo_sems, c):
            eng.wait_ge(lo_sems[0], c + 1)
            eng.wait_ge(lo_sems[1], c + 1)

        def v_on_pool(e, j):
            return e % 2 == 1 and e > 1 and j == 1

        def group_states(e):
            return [(e % NG) * GN + j for j in range(GN)]

        def pair_tokens(e):
            i = e // NG
            return slice(2 * i * CH, 2 * (i + 1) * CH)

        NE = NG * NCH // 2

        PAIR = 6 * KH
        RING = 6

        def mtile(i, stage, k, o):
            return PAIR * i + (2 * stage + k) * KH + o

        def mbank(i, stage, k, o):
            if stage == 0:
                return (PAIR + 2 * KH) * i + 2 * (k * KH + o)
            return (PAIR + 2 * KH) * i + 4 * KH + (2 * (stage - 1) + k) * KH + o

        def low_on_dve(n):
            return n % PAIR >= 2 * KH and n % 2 == 1

        def wait_low(eng, n):
            on_dve = sum(low_on_dve(j) for j in range(n + 1))
            eng.wait_ge(m_lo_p, n + 1 - on_dve)
            if on_dve:
                eng.wait_ge(m_lo_v, on_dve)

        def wait_bank(pe, b):
            if b >= RING:
                i, r = divmod(b - RING, PAIR + 2 * KH)
                if r >= 4 * KH:
                    pe.wait_ge(m_act, PAIR * i + r - 2 * KH + 1)
                elif r % 2:
                    pe.wait_ge(m_full, 2 * KH * i + r // 2 + 1)
                else:
                    pe.wait_ge(m_act, PAIR * i + r // 2 + 1)

        block = ctx.enter_context(nc.Block())

        @block.sync
        def _(sp):
            sp.dma_start(wa[:, :, :], t["w_attn"]).then_inc(ld_wa, 16)
            sp.dma_start(vec[:, :], t["small"]).then_inc(ld_vec, 16)
            for c in range(NCH):
                sp.dma_start(bx2[:, cs(c)], x_d[:, cs(c)]).then_inc(ld_x[c], 16)
            for j in range(NLOW):
                n = min(FILL, nfill - j * FILL)
                if j == 0:
                    sp.dma_start(h0T[:, :], t["state"]).then_inc(ld_h0, 16)
                if j == 1:
                    sp.dma_start(w0raw[:, :, :], t["w_ffn"]).then_inc(ld_w0, 16)
                    sp.dma_start(w1raw, t["w_ssm"]).then_inc(ld_w1, 16)
                sp.dma_start(staged[j][:, 0:n, :], t["w_mlp"][:, j * FILL:j * FILL + n, :]).then_inc(ld_f[j], 16)
            with sp.Fori(0, NCH) as c:
                sp.wait_ge(o_ok, c * TPC + TPC + 1)
                sp.dma_start(out_d[:, bass.ts(c, TPC), :],
                             bdl[:, bass.ts(c, CH)].rearrange("p (n c) -> p n c", c=P)).then_inc(stored, 16)
            sp.wait_ge(stored, 16 * NCH)

        @block.gpsimd
        def _(pool):
            g = nc.gpsimd
            g.memset(ident[:, :], 0.0).then_inc(pads, 1)
            g.memset(mask[:, :], 0.0).then_inc(pads, 1)
            pool.wait_ge(pads, 2)
            g.affine_select(out=ident[:, :], in_=ident[:, :], compare_op=ALU.not_equal, fill=1.0, base=0,
                            pattern=[[-1, P]], channel_multiplier=1).then_inc(ident_ok, 1)
            m3 = mask[:, :].rearrange("p (h k) -> p h k", k=HD)
            g.affine_select(out=m3, in_=m3, compare_op=ALU.is_ge, fill=-1e30, base=0,
                            pattern=[[-HD, HEADS], [0, HD]], channel_multiplier=1).then_inc(mask_ok, 1)
            pool.wait_ge(mask_ok, 1)
            g.affine_select(out=m3, in_=m3, compare_op=ALU.is_ge, fill=-1e30, base=HD - 1,
                            pattern=[[HD, HEADS], [0, HD]], channel_multiplier=-1).then_inc(mask_ok, 1)
            for c in range(1, NCH, 2):
                pool.wait_ge(x_hi, c + 1)
                g.tensor_tensor(xr[:, 1, cs(c)], bx2[:, cs(c)], full(xr[:, 0, cs(c)]),
                                ALU.subtract).then_inc(x_lo_p, 1)
            pool.wait_ge(ld_f[0], 16)
            g.tensor_copy(wf[:, 0:FILL, 0, :], staged[0]).then_inc(fill_hi0, 1)
            pool.wait_ge(fill_hi0, 1)
            g.tensor_tensor(wf[:, 0:FILL, 1, :], staged[0], full(wf[:, 0:FILL, 0, :]), ALU.subtract).then_inc(fill_lo, 1)
            for j in range(1, NLOW):
                n = min(FILL, nfill - j * FILL)
                pool.wait_ge(fill_hi, j)
                g.tensor_tensor(wf[:, j * FILL:j * FILL + n, 1, :], staged[j][:, 0:n, :],
                                full(wf[:, j * FILL:j * FILL + n, 0, :]), ALU.subtract).then_inc(fill_lo, 1)
            pool.wait_ge(mask_ok, 2)
            pool.wait_ge(h0f_ok, 3)
            for j in range(3):
                r = slice(32 * j, 32 * j + 32)
                if j:
                    pool.wait_ge(h0sel_ok, j)
                src = h0T[r, :].rearrange("p (n c) -> p n c", n=1).broadcast_to([32, NS, P])
                g.affine_select(out=h0sel[r, :, :], in_=src, compare_op=ALU.is_equal, fill=0.0, base=0,
                                pattern=[[-1, NS], [0, P]], channel_multiplier=1).then_inc(h0sel_ok, 1)
            pool.wait_ge(h0sel_ok, 3)
            def lows(hi_sem, lo_sems, full_buf, r):
                for c in range(NCH):
                    pool.wait_ge(hi_sem, c + 1)
                    hi, lo = r(c)
                    g.tensor_tensor(lo[:, LV:], full_buf[:, c * CH + LV:(c + 1) * CH], full(hi[:, LV:]),
                                    ALU.subtract).then_inc(lo_sems[1], 1)

            lows(x1_hi, x1_lo, bx1, lambda c: parts(x1r, c, 2))
            lows(k2_hi, k2_lo, bs3, lambda c: parts(tr, c))
            lows(x2_hi, x2_lo, bx2, lambda c: parts(xr, c))
            lows(l1_hi, l1_lo, bs1, lambda c: parts(tr, c))
            lows(l2_hi, l2_lo, bs3, lambda c: parts(lr, c))
            lows(f1_hi, f1_lo, bs1, lambda c: parts(tr, c))
            lows(xt_hi, xt_lo, bxt, lambda c: parts(x1r, c, 2))
            for pair_ in range(NCH // 2):
                for c in (2 * pair_, 2 * pair_ + 1):
                    pool.wait_ge(d_ln, c + 1)
                    pool.wait_ge(d_max, c + 1)
                    g.tensor_tensor(bdl[:, cs(c)], bs1[:, cs(c)], bs2[:, cs(c)], ALU.add).then_inc(d_ok, 1)
                for c in (2 * pair_, 2 * pair_ + 1):
                    pool.wait_ge(d_ok, c + 1)
                    wait_split(pool, xt_lo, c)
                    g.tensor_tensor(bxt[:, cs(c)], bxt[:, cs(c)], bdl[:, cs(c)], ALU.mult).then_inc(g_ok, 1)
            pool.wait_ge(a_ok, 2)
            pool.wait_ge(e_first, 2)
            on_pool = [(e, j, n) for e in range(NE) for j, n in enumerate(group_states(e)) if v_on_pool(e, j)]

            def z_product(r):
                e, j, n = on_pool[r]
                if r:
                    pool.wait_ge(e_vp, r)
                g.tensor_tensor(zmax, bdl[:, pair_tokens(e)], amax[:, n:n + 1].broadcast_to([P, 2 * CH]),
                                ALU.mult).then_inc(e_zp, 1)

            z_product(0)
            r = 0
            for e in range(1, NE, 2):
                if r < len(on_pool) and on_pool[r][0] == e:
                    _, j, n = on_pool[r]
                    pool.wait_ge(e_zp, r + 1)
                    pool.wait_ge(e_t, GN * e + j + 1)
                    g.tensor_tensor(vbuf[e % NB][:, j, :], vbuf[e % NB][:, j, :], zmax, ALU.add).then_inc(e_vp, 1)
                    r += 1
                    if r < len(on_pool):
                        z_product(r)
                pool.wait_ge(e_p, e)
                b = vbuf[(e - 1) % NB]
                g.tensor_tensor(b[:, 0, :], b[:, 0, :], b[:, 1, :], ALU.add).then_inc(e_add, 1)
            lows(x3_hi, x3_lo, bx2, lambda c: parts(lr, c))
            for i in range(NCH // 2):
                for stage in range(3):
                    for k in range(2):
                        for o in range(KH):
                            n = mtile(i, stage, k, o)
                            if low_on_dve(n):
                                continue
                            pool.wait_ge(m_hi, n + 1)
                            sl = slot[(2 * stage + k) % 3]
                            g.tensor_tensor(sl[:, 1, o, :], hbuf[k][:, o, :], full(sl[:, 0, o, :]),
                                            ALU.subtract).then_inc(m_lo_p, 1)

        @block.scalar
        def _(act):
            a = nc.scalar
            act.preload_act_table(ACT.Sqrt)
            act.wait_ge(ld_wa, 16)
            for i in range(4):
                a.activation(bxt[:, i * P:(i + 1) * P], wa[:, i, :], ACT.Square, accum_out=wss[:, i:i + 1]).then_inc(wnorm_ok, 1)
            act.wait_ge(wnorm_ok, 4)
            a.activation(wnorm[:, :], wss[:, :], ACT.Sqrt).then_inc(wnorm_ok, 1)
            act.wait_ge(wT_mm, 1)
            a.activation(wqk[:, 0, :], ps[:, 7, 0:2 * P], ACT.Copy).then_inc(wqk_hi, 1)
            a.activation(woT[:, :], ps[:, 7, 2 * P:3 * P], ACT.Copy).then_inc(woT_ok, 1)
            for p in range(2 * NCH):
                act.wait_ge(qk_mm, p + 1)
                if p >= 2:
                    act.wait_ge(ss_ok, p - 1)
                a.activation(sq[:, p % 2, :], ps[:, p, :], ACT.Square).then_inc(sq_ok, 1)
                qk = ps[:, p, :].rearrange("p (t w c) -> p t w c", t=2, w=2)
                a.activation(k_sb[:, 2 * p:2 * p + 2, :], qk[:, :, 1, :], ACT.Copy).then_inc(k_ok, 1)
                if p in (NCH, 2 * NCH - 1):
                    h = int(p > NCH)
                    act.wait_ge(ss_ok, NCH * (h + 1))
                    a.activation(ss[:, NCH * h:NCH * (h + 1)], ss[:, NCH * h:NCH * (h + 1)], ACT.Sqrt,
                                 scale=1.0 / HD).then_inc(nrm_ok, 1)
            act.preload_act_table_set(LN_EXP)
            for j in range(1, NLOW):
                n = min(FILL, nfill - j * FILL)
                act.wait_ge(ld_f[j], 16)
                a.activation(wf[:, j * FILL:j * FILL + n, 0, :], staged[j][:, 0:n, :], ACT.Copy).then_inc(fill_hi, 1)
            act.wait_ge(smax_ok, 1)
            a.activation(prob[:, :], sm[:, :], ACT.Exp, bias=smax[:, :], accum_out=ssum[:, :]).then_inc(exp_ok, 1)
            act.wait_ge(u_mm, 1)
            a.activation(u_sb[:, :], ps[:, 1, 0:P], ACT.Copy).then_inc(u_ok, 1)
            act.wait_ge(fill_lo, 1)
            a.activation(bx1[:, :].rearrange("p (f c) -> p f c", c=HID), wf[:, 0:FILL, 1, :], ACT.Abs,
                         accum_out=low_max[:, 0:1]).then_inc(low_ok, 1)

            def rstds(var_sem, ln_sem, rs_sem, buf, bank, chunks=range(NCH)):
                for c in chunks:
                    act.wait_ge(var_sem, c + 1)
                    a.activation(buf[:, cs(c)], ps[:, bank + c, :], ACT.Ln, bias=eps_ln[:, :]).then_inc(ln_sem, 1)
                    act.wait_ge(ln_sem, c + 1)
                    a.activation(buf[:, cs(c)], buf[:, cs(c)], ACT.Exp, scale=-0.5).then_inc(rs_sem, 1)

            def square_and_norm(mm_sem, sq_sem, var_sem, ln_sem, rs_sem):
                def square(c):
                    act.wait_ge(mm_sem, c + 1)
                    a.activation(bs1[:, cs(c)], ps[:, 4 + c, :], ACT.Square).then_inc(sq_sem, 1)

                square(0)
                for c in range(NCH):
                    if c + 1 < NCH:
                        square(c + 1)
                    rstds(var_sem, ln_sem, rs_sem, bs2, 0, [c])

            act.wait_ge(fill_lo, NLOW)
            square_and_norm(y1_mm, y1_sq, y1_var, y1_ln, y1_rs)
            for c in range(NCH):
                act.wait_ge(rk_mm, c + 1)
                act.wait_ge(y1_var, c + 1)
                a.activation(bs1[:, cs(c)], ps[:, c, :], ACT.Tanh, scale=0.5).then_inc(th_ok, 1)
                a.activation(bs2[:, cs(c)], ps[:, 4 + c, :], ACT.Relu).then_inc(relu_ok, 1)
                act.wait_ge(relu_ok, c + 1)
                a.activation(bs3[:, cs(c)], bs2[:, cs(c)], ACT.Square).then_inc(k2_ok, 1)
            act.preload_act_table_set(LN_EXP)
            square_and_norm(y2_mm, y2_sq, y2_var, y2_ln, y2_rs)
            act.preload_act_table(ACT.Tanh)
            for c in range(NCH):
                act.wait_ge(l1_mm, c + 1)
                a.activation(bs1[:, cs(c)], ps[:, 4 + c, :], ACT.Relu, bias=vec[:, BL1:BL1 + 1]).then_inc(l1_ok, 1)
            for c in range(NCH):
                act.wait_ge(l2_mm, c + 1)
                a.activation(bs3[:, cs(c)], ps[:, c, :], ACT.Tanh, bias=vec[:, BL2:BL2 + 1]).then_inc(l2_ok, 1)
            act.preload_act_table_set(LN_EXP)
            for c in range(NCH):
                act.wait_ge(f1_mm, c + 1)
                a.activation(bs1[:, cs(c)], ps[:, 4 + c, :], ACT.Relu, bias=vec[:, BF1:BF1 + 1]).then_inc(f1_ok, 1)
            for c in range(NCH):
                act.wait_ge(xt_mm, c + 1)
                a.activation(bxt[:, cs(c)], ps[:, c, :], ACT.Identity, bias=vec[:, BF2:BF2 + 1]).then_inc(xt_ok, 1)
            def softplus(c):
                act.wait_ge(d_mm, c + 1)
                a.activation(bs1[:, cs(c)], ps[:, 4 + c, :], ACT.Abs, bias=vec[:, B1:B1 + 1]).then_inc(d_abs, 1)
                act.wait_ge(d_abs, c + 1)
                a.activation(bs1[:, cs(c)], bs1[:, cs(c)], ACT.Exp, scale=-1.0).then_inc(d_exp, 1)
                act.wait_ge(d_exp, c + 1)
                a.activation(bs1[:, cs(c)], bs1[:, cs(c)], ACT.Ln, bias=1.0).then_inc(d_ln, 1)

            def c_high(c):
                act.wait_ge(c_mm, c + 1)
                a.activation(tr[0:96, 0, cs(c)], ps[0:96, c, :], ACT.Identity, bias=vec[0:96, B23:B23 + 1]).then_inc(c_hi, 1)

            softplus(0)
            softplus(1)
            c_high(0)
            c_high(1)
            softplus(2)
            c_high(2)
            softplus(3)
            c_high(3)

            def state_t(e):
                if e == 0:
                    act.wait_ge(d_ok, 2)
                if e == 2:
                    act.wait_ge(d_ok, NCH)
                if e == 4:
                    act.wait_ge(bc_mm, NCH)
                if e >= NB:
                    act.wait_ge(e_sum, 2 * (e - NB + 1))
                for j, n in enumerate(group_states(e)):
                    a.activation(vbuf[e % NB][:, j, :], bdl[:, pair_tokens(e)], ACT.Exp,
                                 scale=amin[:, n:n + 1]).then_inc(e_t, 1)

            def state_da(e):
                on_pool = sum(v_on_pool(h, j) for h in range(e + 1) for j in range(GN))
                act.wait_ge(e_v, (e + 1) * GN - on_pool)
                if on_pool:
                    act.wait_ge(e_vp, on_pool)
                a.activation(vbuf[e % NB][:, :, :], vbuf[e % NB][:, :, :], ACT.Exp, scale=-1.0, bias=1.0).then_inc(e_da, 1)

            act.wait_ge(a_ok, 2)
            state_t(0)
            for e in range(NE):
                if e + 1 < NE:
                    state_t(e + 1)
                state_da(e)
                if e == NG + 2:
                    act.wait_ge(e_first, NCH)
                    act.wait_ge(e_sum, 2 * NG)
                    for c in range(2):
                        a.activation(y3sq[c], ps[:, 4 + c, :], ACT.Square).then_inc(y3_sq, 1)
            rstds(y3_var, y3_ln, y3_rs, bx2, 0, range(2))
            for c in range(2, NCH):
                act.wait_ge(e_sum, 2 * NE - NCH + c + 1)
                a.activation(y3sq[c], ps[:, 4 + c, :], ACT.Square).then_inc(y3_sq, 1)
            rstds(y3_var, y3_ln, y3_rs, bx2, 0, range(2, NCH))

            def norm_sd(i, k):
                act.wait_ge(o_mv, 2 * i + k + 1)
                a.activation(rstd[:, k, :], mv[:, k, :, 1], ACT.Sqrt, scale=1.0 / P, bias=eps_ln[:, :]).then_inc(o_sd, 1)

            for i in range(NCH // 2):
                for stage, s in ((0, S1), (1, SH1), (2, SH2)):
                    for k in range(2):
                        for o in range(KH):
                            n = mtile(i, stage, k, o)
                            act.wait_ge(mlp_mm, n + 1)
                            if n >= 2 * KH:
                                wait_low(act, n - 2 * KH)
                            a.activation(hbuf[k][:, o, :], ps[:, mbank(i, stage, k, o) % RING, :],
                                         ACT.Gelu if stage else ACT.Silu,
                                         scale=vec[:, s + o:s + o + 1]).then_inc(m_act, 1)
                    if i > 0 and stage == 0:
                        norm_sd(i - 1, 0)
                        norm_sd(i - 1, 1)
            act.preload_act_table(ACT.Sqrt)
            norm_sd(NCH // 2 - 1, 0)
            norm_sd(NCH // 2 - 1, 1)

        @block.vector
        def _(dve):
            v = nc.vector
            v.memset(ones[:, :], 1.0 / P).then_inc(o_ok, 1)
            dve.wait_ge(o_ok, 1)
            v.memset(ones_n[:, :], 1.0).then_inc(consts, 1)
            v.memset(full(x1r[:, :, 0:2]), 0.0).then_inc(consts, 1)
            v.memset(eps_ln[:, :], EPS_LN).then_inc(consts, 1)
            dve.wait_ge(ident_ok, 1)
            v.tensor_scalar(centre[:, :], ident[:, :], 1.0 / P, None, ALU.subtract).then_inc(consts, 1)
            dve.wait_ge(consts, 4)
            v.tensor_copy(centre_r[:, :], centre[:, :]).then_inc(consts, 1)
            v.tensor_scalar(res_centre[:, :], centre[:, :], float(res_gain), None, ALU.mult).then_inc(consts, 1)
            def x_high(c):
                dve.wait_ge(ld_x[c], 16)
                v.tensor_copy(xr[:, 0, cs(c)], bx2[:, cs(c)]).then_inc(x_hi, 1)

            def x_low(c):
                dve.wait_ge(x_hi, c + 1)
                v.tensor_tensor(xr[:, 1, cs(c)], bx2[:, cs(c)], full(xr[:, 0, cs(c)]), ALU.subtract).then_inc(x_lo_v, 1)

            x_high(0)
            dve.wait_ge(wnorm_ok, 5)
            v.tensor_scalar(wnorm[:, :], wnorm[:, :], float(np.sqrt(P) * EPS_MP), None, ALU.add).then_inc(wnorm_ok, 1)
            dve.wait_ge(wnorm_ok, 6)
            v.reciprocal(wnorm[:, :], wnorm[:, :]).then_inc(wnorm_ok, 1)
            dve.wait_ge(wnorm_ok, 7)
            dve.wait_ge(ld_vec, 16)
            v.tensor_scalar(wnorm[:, :], wnorm[:, :], gain, None, ALU.mult).then_inc(wnorm_ok, 1)
            dve.wait_ge(wnorm_ok, 8)
            for i in range(4):
                v.tensor_scalar(wa[:, i, :], wa[:, i, :], wnorm[:, i:i + 1], None, ALU.mult).then_inc(ws_ok, 1)
            x_high(1)
            x_low(0)
            dve.wait_ge(wqk_hi, 1)
            dve.wait_ge(woT_ok, 1)
            v.tensor_tensor(wqk[:, 1, :], ps[:, 7, 0:2 * P], full(wqk[:, 0, :]), ALU.subtract).then_inc(wqk_lo, 1)
            x_high(2)
            x_high(3)
            x_low(2)
            dve.wait_ge(ld_h0, 16)
            v.tensor_copy(h0hi[:, :], h0T[:, :]).then_inc(h0f_ok, 1)
            dve.wait_ge(h0f_ok, 1)
            v.tensor_copy(h0T[0:64, :], full(h0hi[0:64, :])).then_inc(h0f_ok, 1)
            v.tensor_tensor(h0T[64:96, :], h0T[64:96, :], full(h0hi[64:96, :]), ALU.subtract).then_inc(h0f_ok, 1)
            def head_norms(h):
                s = slice(h * NCH, (h + 1) * NCH)
                dve.wait_ge(nrm_ok, h + 1)
                v.tensor_scalar(ss[:, s], ss[:, s], EPS_MP, None, ALU.add).then_inc(nrm_step, 1)
                dve.wait_ge(nrm_step, 3 * h + 1)
                v.tensor_tensor(qkrec[:, s], ss[:, s, :, 0, :], ss[:, s, :, 1, :], ALU.mult).then_inc(nrm_step, 1)
                dve.wait_ge(nrm_step, 3 * h + 2)
                v.reciprocal(qkrec[:, s], qkrec[:, s]).then_inc(nrm_step, 1)

            def normalise_q(h):
                s = slice(2 * h, 2 * h + 2)
                n = slice(4 * h, 4 * h + 4)
                dve.wait_ge(nrm_step, 3 * (2 * h // NCH + 1))
                dve.wait_ge(k_ok, 2 * h + 2)
                qh = ps[:, s, :].rearrange("p b (t w c) -> p (b t) w c", t=2, w=2)[:, :, 0, :]
                r = qkrec[:, s].rearrange("p a b (h e) -> p (a b) h e", e=1).broadcast_to([P, 4, HEADS, HD])
                v.tensor_tensor(q_sb[:, n, :].rearrange("p n (h e) -> p n h e", e=HD),
                                qh.rearrange("p n (h e) -> p n h e", e=HD), r, ALU.mult).then_inc(qn_ok, 1)

            for p in range(2 * NCH):
                dve.wait_ge(sq_ok, p + 1)
                v.tensor_reduce(ss[:, p].rearrange("p a b h -> p (a b h)"),
                                sq[:, p % 2, :].rearrange("p (g e) -> p g e", e=HD), AX.X, ALU.add).then_inc(ss_ok, 1)
                if p == NCH + 1:
                    head_norms(0)
            normalise_q(0)
            normalise_q(1)
            head_norms(1)
            normalise_q(2)
            normalise_q(3)
            v.tensor_reduce(mrow[:, :], woT[:, :], AX.X, ALU.add).then_inc(wo_step, 1)
            dve.wait_ge(wo_step, 1)
            v.tensor_scalar(mrow[:, :], mrow[:, :], 1.0 / P, None, ALU.mult).then_inc(wo_step, 1)
            dve.wait_ge(wo_step, 2)
            v.tensor_scalar(woT[:, :], woT[:, :], mrow[:, :], None, ALU.subtract).then_inc(wo_step, 1)
            dve.wait_ge(ld_vec, 16)
            v.tensor_scalar(mu1[:, :], vec[:, MU_R:MU_R + 2], -1.0, 1.0, ALU.mult, ALU.add).then_inc(mu1_ok, 1)
            dve.wait_ge(mu1_ok, 1)
            dve.wait_ge(ld_w0, 16)
            for i, (j, sc) in enumerate(((0, vec[:, MU_R:MU_R + 1]), (0, mu1[:, 0:1]), (1, vec[:, MU_K:MU_K + 1]),
                                         (1, mu1[:, 1:2]))):
                v.tensor_scalar(w0f[:, i, :], w0raw[:, j, :], sc, None, ALU.mult).then_inc(w0f_ok, 1)
            v.tensor_copy(w0f[:, 4, :], w0raw[:, 2, :]).then_inc(w0f_ok, 1)
            dve.wait_ge(sc_mm, 1)
            dve.wait_ge(mask_ok, 2)
            v.scalar_tensor_tensor(sm[:, :], ps[:, 0, 0:P], float(1.0 / np.sqrt(T)), mask[:, :], ALU.mult,
                                   ALU.add).then_inc(sm_ok, 1)
            dve.wait_ge(sm_ok, 1)
            v.tensor_reduce(smax[:, :], sm[:, :], AX.X, ALU.max, negate=True).then_inc(smax_ok, 1)
            dve.wait_ge(exp_ok, 1)
            v.reciprocal(srec[:, :], ssum[:, :]).then_inc(srec_ok, 1)
            dve.wait_ge(srec_ok, 1)
            v.tensor_scalar(prob[:, :], prob[:, :], srec[:, :], None, ALU.mult).then_inc(prob_ok, 1)
            dve.wait_ge(m_mm, 1)
            dve.wait_ge(consts, 6)
            v.scalar_tensor_tensor(mix[:, :], ps[:, 2, 0:P], float(out_gain), res_centre[:, :], ALU.mult,
                                   ALU.add).then_inc(mix_ok, 1)
            dve.wait_ge(mix_ok, 1)
            v.tensor_copy(mixr[:, 0, :], mix[:, :]).then_inc(mix_ok, 1)
            dve.wait_ge(mix_ok, 2)
            v.tensor_tensor(mixr[:, 1, :], mix[:, :], full(mixr[:, 0, :]), ALU.subtract).then_inc(mix_ok, 1)
            dve.wait_ge(w0f_ok, 5)
            v.tensor_copy(w0[:, :, 0, :], w0f[:, :, :]).then_inc(w0_hi, 1)
            dve.wait_ge(w0_hi, 1)
            v.tensor_tensor(w0[:, :, 1, :], w0f[:, :, :], full(w0[:, :, 0, :]), ALU.subtract).then_inc(w0_lo, 1)
            dve.wait_ge(ld_w1, 16)
            v.tensor_copy(w1[:, :, 0, :], w1raw[:, :, :]).then_inc(w1_hi, 1)
            dve.wait_ge(w1_hi, 1)
            v.tensor_tensor(w1[:, :, 1, :], w1raw[:, :, :], full(w1[:, :, 0, :]), ALU.subtract).then_inc(w1_lo, 1)
            v.tensor_scalar(amin[:, :], amat[:, :], 0.0, None, ALU.min).then_inc(a_ok, 1)
            v.tensor_scalar(amax[:, :], amat[:, :], 0.0, None, ALU.max).then_inc(a_ok, 1)
            def lows_max(j):
                dve.wait_ge(fill_lo, j + 1)
                v.tensor_reduce(low_max[:, j:j + 1], full(wf[:, j * FILL:min((j + 1) * FILL, nfill), 1, :]), AX.XY,
                                ALU.max, apply_absolute_value=True).then_inc(low_ok_v, 1)

            lows_max(1)

            def split(full_sem, hi_sem, lo_sems, full_buf, dst, c):
                hi, lo = dst(c)
                dve.wait_ge(full_sem, c + 1)
                v.tensor_copy(hi, full_buf[:, cs(c)]).then_inc(hi_sem, 1)
                dve.wait_ge(hi_sem, c + 1)
                v.tensor_tensor(lo[:, :LV], full_buf[:, c * CH:c * CH + LV], full(hi[:, :LV]),
                                ALU.subtract).then_inc(lo_sems[0], 1)

            for c in range(NCH):
                dve.wait_ge(y1_rs, c + 1)
                v.tensor_tensor(bx1[:, cs(c)], ps[:, 4 + c, :], bs2[:, cs(c)], ALU.mult).then_inc(x1_ok, 1)
                split(x1_ok, x1_hi, x1_lo, bx1, lambda c: parts(x1r, c, 2), c)
            lows_max(2)
            def gate(c):
                dve.wait_ge(v_mm, c + 1)
                dve.wait_ge(th_ok, c + 1)
                v.scalar_tensor_tensor(bs1[:, cs(c)], bs1[:, cs(c)], 1.0, ps[:, c, :], ALU.add,
                                       ALU.mult).then_inc(p_ok, 1)
                dve.wait_ge(p_ok, c + 1)
                wait_split(dve, k2_lo, c)
                v.scalar_tensor_tensor(bs3[:, cs(c)], bs1[:, cs(c)], 0.5, bx1[:, cs(c)], ALU.mult,
                                       ALU.add).then_inc(y2_ok, 1)

            def split_k2(c):
                split(k2_ok, k2_hi, k2_lo, bs3, lambda c: parts(tr, c), c)

            split_k2(0)
            for c in range(1, NCH):
                split_k2(c)
                gate(c - 1)
            gate(NCH - 1)
            for c in range(NCH):
                dve.wait_ge(y2_rs, c + 1)
                v.tensor_tensor(bx2[:, cs(c)], ps[:, 4 + c, :], bs2[:, cs(c)], ALU.mult).then_inc(x2_ok, 1)
                split(x2_ok, x2_hi, x2_lo, bx2, lambda c: parts(xr, c), c)
            for c in range(NCH):
                split(l1_ok, l1_hi, l1_lo, bs1, lambda c: parts(tr, c), c)
            for c in range(NCH):
                split(l2_ok, l2_hi, l2_lo, bs3, lambda c: parts(lr, c), c)
            for c in range(NCH):
                split(f1_ok, f1_hi, f1_lo, bs1, lambda c: parts(tr, c), c)
            for c in range(NCH):
                split(xt_ok, xt_hi, xt_lo, bxt, lambda c: parts(x1r, c, 2), c)
            dve.wait_ge(low_mm, 1)
            v.tensor_reduce(low_any[:, :], ps[:, 7, 0:NLOW], AX.X, ALU.add).then_inc(low_flag, 1)
            def positive(c):
                dve.wait_ge(d_abs, c + 1)
                v.tensor_scalar(bs2[:, cs(c)], ps[:, 4 + c, :], vec[:, B1:B1 + 1], 0.0, ALU.add,
                                ALU.max).then_inc(d_max, 1)
            def c_low_and_products(c):
                dve.wait_ge(c_hi, c + 1)
                v.tensor_scalar(bs3[0:32, cs(c)], ps[96:128, c, :], vec[96:128, B23:B23 + 1], None,
                                ALU.add).then_inc(b_ok, 1)
                v.scalar_tensor_tensor(tr[32:64, 0, cs(c)], ps[32:64, c, :], vec[32:64, B23:B23 + 1],
                                       full(tr[32:64, 0, cs(c)]), ALU.add, ALU.subtract).then_inc(c_lo, 1)
                dve.wait_ge(b_ok, c + 1)
                v.scalar_tensor_tensor(bs3[0:32, cs(c)], ps[0:32, c, :], vec[0:32, B23:B23 + 1], bs3[0:32, cs(c)],
                                       ALU.add, ALU.mult).then_inc(bc_ok, 1)

            positive(0)
            positive(1)
            c_low_and_products(0)
            c_low_and_products(1)
            def direct(c):
                dve.wait_ge(g_ok, c + 1)
                dve.wait_ge(bc_mm, c + 1)
                v.tensor_tensor(bxt[:, cs(c)], bxt[:, cs(c)], ps[:, 4 + c, :], ALU.mult).then_inc(o2_ok, 1)

            def state_v(e):
                for j, n in enumerate(group_states(e)):
                    if not v_on_pool(e, j):
                        dve.wait_ge(e_t, GN * e + j + 1)
                        v.scalar_tensor_tensor(vbuf[e % NB][:, j, :], bdl[:, pair_tokens(e)], amax[:, n:n + 1],
                                               vbuf[e % NB][:, j, :], ALU.mult, ALU.add).then_inc(e_v, 1)

            def state_p(e):
                dve.wait_ge(e_da, e + 1)
                dve.wait_ge(e_ch, e + 1)
                v.tensor_tensor(vbuf[e % NB].rearrange("p j (k n) -> p (j k) n", n=CH),
                                vbuf[e % NB].rearrange("p j (k n) -> p (j k) n", n=CH), ps[:, 0:4, :],
                                ALU.mult).then_inc(e_p, 1)

            positive(2)
            c_low_and_products(2)
            state_v(0)
            positive(3)
            c_low_and_products(3)
            direct(0)
            direct(1)
            for e in range(NE):
                if e + 1 < NE:
                    state_v(e + 1)
                state_p(e)
                if e in (0, 1):
                    direct(2 + e)
            b = vbuf[(NE - 1) % NB]
            dve.wait_ge(e_p, NE)
            v.tensor_tensor(b[:, 0, :], b[:, 0, :], b[:, 1, :], ALU.add).then_inc(e_add_last, 1)

            for c in range(NCH):
                dve.wait_ge(y3_rs, c + 1)
                v.tensor_tensor(bx2[:, cs(c)], ps[:, 4 + c, :], bx2[:, cs(c)], ALU.mult).then_inc(x3_ok, 1)
                split(x3_ok, x3_hi, x3_lo, bx2, lambda c: parts(lr, c), c)

            def mlp_tiles(i, stage, k):
                def gate_tile(o):
                    dve.wait_ge(m_act, mtile(i, stage, k, o) + 1)
                    v.scalar_tensor_tensor(hbuf[k][:, o, :], ps[:, (mbank(i, stage, k, o) + 1) % RING, :],
                                           vec[:, S2 + o:S2 + o + 1], hbuf[k][:, o, :], ALU.mult,
                                           ALU.mult).then_inc(m_full, 1)

                if stage == 0:
                    gate_tile(0)
                for o in range(KH):
                    n = mtile(i, stage, k, o)
                    sl = slot[(2 * stage + k) % 3]
                    if stage == 0:
                        if o + 1 < KH:
                            gate_tile(o + 1)
                        dve.wait_ge(m_full, 2 * KH * i + k * KH + o + 1)
                    else:
                        dve.wait_ge(m_act, n + 1)
                    v.tensor_copy(sl[:, 0, o, :], hbuf[k][:, o, :]).then_inc(m_hi, 1)
                    if low_on_dve(n):
                        dve.wait_ge(m_hi, n + 1)
                        v.tensor_tensor(sl[:, 1, o, :], hbuf[k][:, o, :], full(sl[:, 0, o, :]),
                                        ALU.subtract).then_inc(m_lo_v, 1)

            def residual(i, k):
                dve.wait_ge(o_mm, 2 * i + k + 1)
                v.scalar_tensor_tensor(bs3[:, k * CH:(k + 1) * CH], ps[:, RING + k, :], vec[:, S3:S3 + 1],
                                       bx2[:, cs(2 * i + k)], ALU.mult, ALU.add).then_inc(o_y, 1)

            def norm_stats(i, k):
                dve.wait_ge(o_T, 2 * i + k + 1)
                yt = ps[:, RING + k, :].rearrange("p (n c) -> p n c", c=P)
                for n in range(TPC):
                    v.bn_stats(stats[:, k, n, :], yt[:, n, :]).then_inc(o_st, 1)
                dve.wait_ge(o_st, (2 * i + k + 1) * TPC)
                me, mo, m2e, m2o = [stats[:, k, :, j] for j in (1, 4, 2, 5)]
                v.tensor_tensor(mv[:, k, :, 0], me, mo, ALU.add).then_inc(o_stat, 1)
                v.tensor_tensor(mdif[:, k, :], me, mo, ALU.subtract).then_inc(o_stat, 1)
                v.tensor_tensor(mv[:, k, :, 1], m2e, m2o, ALU.add).then_inc(o_stat, 1)
                dve.wait_ge(o_stat, (2 * i + k) * 5 + 2)
                v.tensor_tensor(mdif[:, k, :], mdif[:, k, :], mdif[:, k, :], ALU.mult).then_inc(o_stat, 1)
                dve.wait_ge(o_stat, (2 * i + k) * 5 + 1)
                v.tensor_scalar(mv[:, k, :, 0], mv[:, k, :, 0], 0.5, None, ALU.mult).then_inc(o_stat, 1)
                dve.wait_ge(o_stat, (2 * i + k) * 5 + 4)
                v.scalar_tensor_tensor(mv[:, k, :, 1], mdif[:, k, :], P / 4.0, mv[:, k, :, 1], ALU.mult,
                                       ALU.add).then_inc(o_mv, 1)

            def normalise(i, k):
                dve.wait_ge(o_sd, 2 * i + k + 1)
                v.reciprocal(rstd[:, k, :], rstd[:, k, :]).then_inc(o_rs, 1)
                dve.wait_ge(o_rs, 2 * i + k + 1)
                dve.wait_ge(o_stat, (2 * i + k) * 5 + 5)
                yt = ps[:, RING + k, :].rearrange("p (n c) -> p n c", c=P)
                for n in range(TPC):
                    v.tensor_scalar(bdl[:, bass.ds((2 * i + k) * CH + n * P, P)], yt[:, n, :],
                                    mv[:, k, n, 0:1], rstd[:, k, n:n + 1], ALU.subtract,
                                    ALU.mult).then_inc(o_ok, 1)

            for i in range(NCH // 2):
                for stage in range(3):
                    for k in range(2):
                        mlp_tiles(i, stage, k)
                        if i > 0 and stage == 0:
                            residual(i - 1, k)
                    if i > 0 and stage == 0:
                        for k in range(2):
                            norm_stats(i - 1, k)
                        for k in range(2):
                            normalise(i - 1, k)
            last = NCH // 2 - 1
            residual(last, 0)
            residual(last, 1)
            norm_stats(last, 0)
            norm_stats(last, 1)
            normalise(last, 0)
            normalise(last, 1)

        @block.tensor
        def _(pe):
            m = nc.tensor
            pe.wait_ge(ident_ok, 1)
            pe.wait_ge(ws_ok, 3)
            for i in range(3):
                last = m.transpose(ps[:, 7, i * P:(i + 1) * P], wa[:, i, :], ident[:, :])
            last.then_inc(wT_mm, 1)
            pe.wait_ge(wqk_lo, 1)
            for p in range(2 * NCH):
                c = p // 2
                if c % 2:
                    pe.wait_ge(x_lo_p, c // 2 + 1)
                else:
                    pe.wait_ge(x_lo_v, c // 2 + 1)
                if p == 2 * NCH - 1:
                    pe.wait_ge(woT_ok, 1)
                for h in range(2):
                    tok = slice((2 * p + h) * P, (2 * p + h + 1) * P)
                    last = mm3(ps[:, p, h * 2 * P:(h + 1) * 2 * P], (xr[:, 0, tok], xr[:, 1, tok]),
                               (wqk[:, 0, :], wqk[:, 1, :]))
                last.then_inc(qk_mm, 1)
            for n in range(NT):
                if n % 4 == 0:
                    pe.wait_ge(qn_ok, n // 4 + 1)
                pe.wait_ge(k_ok, n // 2 + 1)
                last = m.matmul(ps[:, 0, 0:P], q_sb[:, n, :], k_sb[:, n, :], start=(n == 0), stop=(n == NT - 1))
            last.then_inc(sc_mm, 1)
            pe.wait_ge(prob_ok, 1)
            pe.wait_ge(wo_step, 3)
            m.matmul(ps[:, 1, 0:P], prob[:, :], woT[:, :], start=True, stop=True).then_inc(u_mm, 1)
            pe.wait_ge(u_ok, 1)
            pe.wait_ge(ws_ok, 4)
            m.matmul(ps[:, 2, 0:P], wa[:, 3, :], u_sb[:, :], start=True, stop=True).then_inc(m_mm, 1)

            def over_channels(src_sem, dst_sem, w, buf, bank, c):
                pe.wait_ge(src_sem, c + 1)
                m.matmul(ps[:, bank + c, :], w[:, :], buf[:, cs(c)], start=True, stop=True).then_inc(dst_sem, 1)

            def y1(c):
                mm3(ps[:, 4 + c, :], (mixr[:, 0, :], mixr[:, 1, :]), parts(xr, c)).then_inc(y1_mm, 1)

            def y1_variance(c):
                over_channels(y1_sq, y1_var, ones, bs1, 0, c)

            pe.wait_ge(mix_ok, 3)
            pe.wait_ge(consts, 6)
            pe.wait_ge(o_ok, 1)
            y1(0)
            for c in range(1, NCH):
                y1(c)
                y1_variance(c - 1)
            y1_variance(NCH - 1)

            def rk(c):
                wait_split(pe, x1_lo, c)
                for bank, w in ((c, 0), (4 + c, 2)):
                    mm3(ps[:, bank, :], pair(w0, w), parts(x1r, c, 2), stop=False)
                    last = mm3(ps[:, bank, :], pair(w0, w + 1), parts(x1r, c, 1), start=False)
                last.then_inc(rk_mm, 1)

            def value(c):
                wait_split(pe, k2_lo, c)
                mm3(ps[:, c, :], pair(w0, 4), parts(tr, c)).then_inc(v_mm, 1)

            def y2(c):
                over_channels(y2_ok, y2_mm, centre, bs3, 4, c)

            def y2_variance(c):
                over_channels(y2_sq, y2_var, ones, bs1, 0, c)

            pe.wait_ge(w0_lo, 1)
            rk(0)
            rk(1)
            rk(2)
            value(0)
            rk(3)
            value(1)
            y2(0)
            value(2)
            y2(1)
            y2_variance(0)
            value(3)
            y2(2)
            y2_variance(1)
            y2(3)
            y2_variance(2)
            y2_variance(3)
            pe.wait_ge(w1_lo, 1)
            for c in range(NCH):
                wait_split(pe, x2_lo, c)
                mm3(ps[:, 4 + c, :], pair(w1, 0), parts(xr, c)).then_inc(l1_mm, 1)
            for c in range(NCH):
                wait_split(pe, l1_lo, c)
                mm3(ps[:, c, :], pair(w1, 1), parts(tr, c)).then_inc(l2_mm, 1)
            for c in range(NCH):
                mm3(ps[:, 4 + c, :], pair(w1, 2), parts(xr, c), stop=False)
                wait_split(pe, l2_lo, c)
                mm3(ps[:, 4 + c, :], pair(w1, 3), parts(lr, c), start=False).then_inc(f1_mm, 1)
            for c in range(NCH):
                wait_split(pe, f1_lo, c)
                mm3(ps[:, c, :], pair(w1, 4), parts(tr, c)).then_inc(xt_mm, 1)
            pe.wait_ge(low_ok, 1)
            pe.wait_ge(low_ok_v, NLOW - 1)
            pe.wait_ge(f1_ok, NCH)
            m.matmul(ps[:, 7, 0:NLOW], ones[:, :], low_max[:, :], start=True, stop=True).then_inc(low_mm, 1)
            for c in range(NCH):
                wait_split(pe, xt_lo, c)
                if c == 3:
                    pe.wait_ge(low_flag, 1)
                mm3(ps[:, 4 + c, :], pair(w1, 5), parts(x1r, c, 2)).then_inc(d_mm, 1)
            for c in range(NCH):
                mm3(ps[:, c, :], pair(w1, 6), parts(x1r, c, 2)).then_inc(c_mm, 1)
            for c in range(NCH):
                pe.wait_ge(bc_ok, c + 1)
                pe.wait_ge(d_abs, c + 1)
                pe.wait_ge(d_max, c + 1)
                m.matmul(ps[:, 4 + c, :], ones_n[:, :], bs3[0:32, cs(c)], start=True, stop=True).then_inc(bc_mm, 1)

            def state_ch(e):
                for j, n in enumerate(group_states(e)):
                    for k in range(2):
                        last = m.matmul(ps[:, 2 * j + k, :], h0sel[:, n, :], tr[0:96, 0, cs(2 * (e // NG) + k)],
                                        start=True, stop=True)
                last.then_inc(e_ch, 1)

            def state_first(c):
                pe.wait_ge(o2_ok, c + 1)
                for h in range(2):
                    m.matmul(ps[:, 4 + c, :], centre_r[:, :], xr[:, h, cs(c)], start=(h == 0), stop=False)
                m.matmul(ps[:, 4 + c, :], centre[:, :], bxt[:, cs(c)], start=False, stop=False).then_inc(e_first, 1)

            def state_sum(e):
                if e % 2 == 0:
                    pe.wait_ge(e_add, e // 2 + 1)
                if e == NE - 1:
                    pe.wait_ge(e_add_last, 1)
                added = e % 2 == 0 or e == NE - 1
                for k in range(2):
                    for j in range(1 if added else GN):
                        last = m.matmul(ps[:, 4 + 2 * (e // NG) + k, :], centre[:, :],
                                        vbuf[e % NB][:, j, k * CH:(k + 1) * CH], start=False,
                                        stop=(e % NG == NG - 1 and (added or j == GN - 1)))
                    last.then_inc(e_sum, 1)

            pe.wait_ge(h0sel_ok, 3)
            pe.wait_ge(c_lo, NCH)
            pe.wait_ge(bc_ok, NCH)
            state_ch(0)
            state_first(0)
            state_first(1)
            for e in range(NE - 1):
                pe.wait_ge(e_p, e + 1)
                state_ch(e + 1)
                if e:
                    state_sum(e - 1)
                if e in (5, 7):
                    state_first((e - 1) // 2)
            pe.wait_ge(e_p, NE)
            for c in range(NCH):
                if c == 2:
                    state_sum(NE - 2)
                    state_sum(NE - 1)
                pe.wait_ge(y3_sq, c + 1)
                m.matmul(ps[:, c, :], ones[:, :], y3sq[c], start=True, stop=True).then_inc(y3_var, 1)

            def product(low_weights, dst, f, wo, x, start=True, stop=True):
                m.matmul(dst, wf[:, f, 0, wo], x[0], start=start, stop=False)
                last = m.matmul(dst, wf[:, f, 0, wo], x[1], start=False, stop=stop and not low_weights)
                if low_weights:
                    last = m.matmul(dst, wf[:, f, 1, wo], x[0], start=False, stop=stop)
                return last

            def gated(low_weights, i, k):
                wait_split(pe, x3_lo, 2 * i + k)
                for o in range(KH):
                    wo = slice(o * P, (o + 1) * P)
                    for f in range(2):
                        b = mbank(i, 0, k, o) + f
                        wait_bank(pe, b)
                        if b < 4:
                            pe.wait_ge(y3_ln, b + 1)
                        elif b < RING:
                            pe.wait_ge(x3_ok, b - 3)
                        last = product(low_weights, ps[:, b % RING, :], f, wo, parts(lr, 2 * i + k))
                    last.then_inc(mlp_mm, 1)

            def hidden(low_weights, i, stage, k, tiles):
                src = slot[(2 * stage - 2 + k) % 3]
                for o in tiles:
                    b = mbank(i, stage, k, o)
                    wait_bank(pe, b)
                    for kk in range(KH):
                        if o == 0:
                            wait_low(pe, mtile(i, stage - 1, k, kk))
                        last = product(low_weights, ps[:, b % RING, :], 3 + (stage - 1) * KH + kk,
                                       slice(o * P, (o + 1) * P), (src[:, 0, kk, :], src[:, 1, kk, :]),
                                       start=(kk == 0), stop=(kk == KH - 1))
                    last.then_inc(mlp_mm, 1)

            def output(low_weights, i, k):
                src = slot[(4 + k) % 3]
                if i > 0:
                    pe.wait_ge(o_ok, (2 * i - 1 + k) * TPC + 1)
                for kk in range(KH):
                    wait_low(pe, mtile(i, 2, k, kk))
                    last = product(low_weights, ps[:, RING + k, :], 2, slice(kk * P, (kk + 1) * P),
                                   (src[:, 0, kk, :], src[:, 1, kk, :]), start=(kk == 0), stop=(kk == KH - 1))
                last.then_inc(o_mm, 1)

            def token_major(i, k):
                pe.wait_ge(o_y, 2 * i + k + 1)
                for n in range(TPC):
                    last = m.transpose(ps[:, RING + k, n * P:(n + 1) * P],
                                       bs3[:, k * CH + n * P:k * CH + (n + 1) * P], ident[:, :])
                last.then_inc(o_T, 1)

            def mlp(low_weights):
                for i in range(NCH // 2):
                    for k in range(2):
                        gated(low_weights, i, k)
                        if i > 0:
                            output(low_weights, i - 1, k)
                    if i > 0:
                        hidden(low_weights, i, 1, 0, range(2))
                        token_major(i - 1, 0)
                        token_major(i - 1, 1)
                        hidden(low_weights, i, 1, 0, range(2, KH))
                    else:
                        hidden(low_weights, i, 1, 0, range(KH))
                    hidden(low_weights, i, 1, 1, range(KH))
                    for k in range(2):
                        hidden(low_weights, i, 2, k, range(KH))
                for k in range(2):
                    output(low_weights, NCH // 2 - 1, k)
                for k in range(2):
                    token_major(NCH // 2 - 1, k)

            pe.wait_ge(low_flag, 1)
            has_low = pe.value_load(low_any[0:1, 0:1].bitcast(mybir.dt.int32))
            with pe.If(has_low):
                mlp(True)
            with pe.Else():
                mlp(False)


def layout(d):
    import numpy as _np

    def columns(name):
        a = d[name]
        return a.reshape(-1, P).T

    small = _np.zeros((P, NSMALL), _np.float32)
    for name, col in (("L0_ffn_mu_r", MU_R), ("L0_ffn_mu_k", MU_K), ("L1_attn_bl1", BL1), ("L1_attn_bl2", BL2),
                      ("L1_attn_bf1", BF1), ("L1_attn_bf2", BF2), ("L1_attn_b1", B1), ("L1_ffn_w3_s", S3),
                      ("L1_ffn_w1_s", S1), ("L1_ffn_w2_s", S2), ("L1_ffn_h1_s", SH1), ("L1_ffn_h2_s", SH2)):
        c = columns(name)
        small[:, col:col + c.shape[1]] = c
    for r in (0, 32, 64):
        small[r:r + NS, B23] = d["L1_attn_b3"]
    small[96:96 + NS, B23] = d["L1_attn_b2"]
    small[:, A_COL:A_COL + NS] = d["L1_attn_A"]
    small[:, GAIN_COL] = d["L0_attn_gain"]
    w_ssm = _np.zeros((P, 7, P), _np.float32)
    for i, w in enumerate((d["L1_attn_Wl1"], d["L1_attn_Wl2"], d["L1_attn_Wf1"][:P], d["L1_attn_Wf1"][P:],
                           d["L1_attn_Wf2"], d["L1_attn_W1"])):
        w_ssm[:, i] = w
    for r in (0, 32, 64):
        w_ssm[:, 6, r:r + NS] = d["L1_attn_W3"]
    w_ssm[:, 6, 96:96 + NS] = d["L1_attn_W2"]
    state = _np.zeros((96, P), _np.float32)
    for r in (0, 32, 64):
        state[r:r + NS] = d["L1_attn_state_init"][0].T
    hid = d["L1_ffn_w1_w"].shape[0]

    def blocks(w):
        return w.T.reshape(-1, P, w.shape[0]).transpose(1, 0, 2)

    w_mlp = _np.concatenate([blocks(d["L1_ffn_w1_w"]), blocks(d["L1_ffn_w2_w"]),
                             blocks(d["L1_ffn_w3_w"]).reshape(P, 1, hid), blocks(d["L1_ffn_h1_w"]),
                             blocks(d["L1_ffn_h2_w"])], axis=1)
    return {
        "x": d["L0_attn_query"].reshape(-1, P).T,
        "w_attn": _np.stack([d["L0_attn_" + n] for n in ("w_q", "w_k", "w_o", "w_v")], axis=1),
        "small": small,
        "w_ffn": _np.stack([d["L0_ffn_" + n].T for n in ("W_r", "W_k", "W_v")], axis=1),
        "w_ssm": w_ssm,
        "state": state,
        "w_mlp": w_mlp,
    }


def kernel(**inputs):
    import numpy as _np
    import concourse.bacc as _bacc
    from concourse import mybir as _mybir
    from concourse.bass_utils import run_bass_kernel_spmd as _run

    nc = _bacc.Bacc("TRN2", target_bir_lowering=False, num_devices=1)
    arrays, tensors = {}, {}
    for name, a in layout({k: _np.asarray(a) for k, a in inputs.items()}).items():
        a = _np.ascontiguousarray(a)
        arrays[f"in_{name}_dram"] = a
        tensors[name] = nc.dram_tensor(f"in_{name}_dram", a.shape, _mybir.dt.from_np(a.dtype),
                                       kind="ExternalInput").ap()
    shape = inputs["L0_attn_query"].shape
    out = nc.dram_tensor("out_0_dram", tuple(shape), _mybir.dt.float32, kind="ExternalOutput").ap()
    build(nc, tensors, out)
    r = _run(nc, [arrays], core_ids=[0])
    return r.results[0]["out_0_dram"]
```
